# Optimizing a Trainium2 kernel written in Bass

```python
import numpy as np
import jax
import jax.numpy as jnp

def _softmax(x, axis=-1):
    return jax.nn.softmax(x, axis=axis)

def _gelu(x):
    return jax.nn.gelu(x, approximate=True)

def _silu(x):
    return jax.nn.silu(x)

def _sigmoid(x):
    return jax.nn.sigmoid(x)

def _layernorm(x, axis=-1, eps=1e-05):
    m = jnp.mean(x, axis=axis, keepdims=True)
    v = jnp.var(x, axis=axis, keepdims=True)
    return (x - m) / jnp.sqrt(v + eps)

def _scatter_add(tgt, idx, src, axis=0):
    return tgt.at[idx].add(src)

def _segment_sum(src, seg, n):
    return jax.ops.segment_sum(src, seg, n)
kernel_name = 'mk_decoder_preln_d1_seqx_r8_49e170'

def setup_inputs(seed: int=0):
    np.random.seed(seed)
    _w = jnp.asarray

    def _rec_inputs():
        import jax
        import jax.numpy as jnp
        _rk = jax.random.key(seed)
        x = 7.22e-05 + 1 * jax.random.normal(jax.random.fold_in(_rk, 1), (32, 64, 256), jnp.float32)
        _lenS = 64 - jax.random.randint(jax.random.fold_in(_rk, 7), (32,), 0, max(1, 64 // 4) + 1, jnp.int32)
        _lenS2 = 64 - jax.random.randint(jax.random.fold_in(_rk, 8), (32,), 0, max(1, 64 // 4) + 1, jnp.int32)
        _ctx_2048P = jax.random.normal(jax.random.fold_in(_rk, 11), (32, 16, 256), jnp.float32)
        _ctx_2048c = jax.random.dirichlet(jax.random.fold_in(_rk, 511), 0.3 * jnp.ones((16,), jnp.float32), (32, 64))
        _ctx_2048t = jnp.einsum('bsk,bkd->bsd', _ctx_2048c, _ctx_2048P)
        _ctx_2048t = _ctx_2048t * jax.lax.rsqrt(jnp.mean(jnp.square(_ctx_2048t)) + 1e-12) * 0.953939
        ctx_2048 = 4.13588e-05 + 0.999923 * (_ctx_2048t + 0.3 * jax.random.normal(jax.random.fold_in(_rk, 611), (32, 64, 256), jnp.float32))
        return (x, ctx_2048)
    x, ctx_2048 = _rec_inputs()

    def _L0_attn_setup():
        import jax, jax.numpy as jnp
        import numpy as np
        EMBED_DIM = 256
        NUM_HEADS = 16
        HEAD_DIM = EMBED_DIM // NUM_HEADS
        BASE = 10000.0

        def rotate_half(x):
            half = x.shape[-1] // 2
            x1, x2 = (x[..., :half], x[..., half:])
            return jnp.concatenate([-x2, x1], axis=-1)

        def apply_rope(x, base=BASE):
            S, Dh = (x.shape[-2], x.shape[-1])
            inv_freq = 1.0 / base ** (jnp.arange(0, Dh, 2, dtype=jnp.float32) / Dh)
            t = jnp.arange(S, dtype=jnp.float32)
            freqs = jnp.einsum('i,j->ij', t, inv_freq)
            emb = jnp.concatenate([freqs, freqs], axis=-1)
            return x * jnp.cos(emb) + rotate_half(x) * jnp.sin(emb)
        key = jax.random.key(seed)
        ks = jax.random.split(key, 9)
        B, S, D = (2, 256, EMBED_DIM)
        xavier = lambda k, shape: jax.random.uniform(k, shape, jnp.float32, -1.0, 1.0) * float(np.sqrt(6.0 / (shape[0] + shape[1])))
        return {'x': jax.random.normal(ks[0], (B, S, D), jnp.float32), 'q_w': xavier(ks[1], (D, D)), 'k_w': xavier(ks[2], (D, D)), 'v_w': xavier(ks[3], (D, D)), 'q_b': jnp.zeros((D,), jnp.float32), 'k_b': jnp.zeros((D,), jnp.float32), 'v_b': jnp.zeros((D,), jnp.float32), 'out_w': xavier(ks[4], (D, D)), 'out_b': jnp.zeros((D,), jnp.float32)}
    _L0_attn_all = _L0_attn_setup()
    _L0_attn_in = {k: v for k, v in _L0_attn_all.items() if k in ('q_w', 'k_w', 'v_w', 'q_b', 'k_b', 'v_b', 'out_w', 'out_b')}
    del _L0_attn_all

    def _L0_xattn_setup():
        import jax, jax.numpy as jnp
        import numpy as np
        N, E, T, H = (8, 64, 256, 8)
        key = jax.random.key(seed)
        ks = jax.random.split(key, 6)
        s = 1.0 / np.sqrt(E)
        return {'mask': jax.random.normal(ks[0], (N, E, T), jnp.float32), 'encodings': jax.random.normal(ks[1], (N, E, T), jnp.float32), 'w_in': jax.random.normal(ks[2], (3 * E, E), jnp.float32) * s, 'b_in': jnp.zeros((3 * E,), jnp.float32), 'w_out': jax.random.normal(ks[3], (E, E), jnp.float32) * s, 'b_out': jnp.zeros((E,), jnp.float32), 'w_ct': jax.random.normal(ks[4], (E, E), jnp.float32) * s, 'b_ct': jnp.zeros((E,), jnp.float32), 'local_size': 64}
    _L0_xattn_all = _L0_xattn_setup()
    _L0_xattn_in = {k: v for k, v in _L0_xattn_all.items() if k in ('w_in', 'b_in', 'w_out', 'b_out', 'w_ct', 'b_ct')}
    del _L0_xattn_all

    def _L0_ffn_setup():
        import jax, jax.numpy as jnp
        import numpy as np
        import math
        NUM_EXPERTS = 12
        TOP_K = 2
        CAP_FACTOR = 1.25
        key = jax.random.key(seed)
        k0, k1, k2, k3, k4 = jax.random.split(key, 5)
        B, S, H, F = (4, 512, 256, 32)
        hidden_states = jax.random.normal(k0, (B, S, H), jnp.float32)
        gate_w = jax.random.normal(k1, (NUM_EXPERTS, H), jnp.float32) * 0.02
        w1 = jax.random.normal(k2, (NUM_EXPERTS, F, H), jnp.float32) * 0.02
        w2 = jax.random.normal(k3, (NUM_EXPERTS, H, F), jnp.float32) * 0.02
        w3 = jax.random.normal(k4, (NUM_EXPERTS, F, H), jnp.float32) * 0.02
        return dict(hidden_states=hidden_states, gate_w=gate_w, w1=w1, w2=w2, w3=w3)
    _L0_ffn_all = _L0_ffn_setup()
    _L0_ffn_in = {k: v for k, v in _L0_ffn_all.items() if k in ('gate_w', 'w1', 'w2', 'w3')}
    del _L0_ffn_all
    return {'x': x, 'ctx_2048': ctx_2048, 'L0_attn_q_w': _L0_attn_in['q_w'], 'L0_attn_k_w': _L0_attn_in['k_w'], 'L0_attn_v_w': _L0_attn_in['v_w'], 'L0_attn_q_b': _L0_attn_in['q_b'], 'L0_attn_k_b': _L0_attn_in['k_b'], 'L0_attn_v_b': _L0_attn_in['v_b'], 'L0_attn_out_w': _L0_attn_in['out_w'], 'L0_attn_out_b': _L0_attn_in['out_b'], 'L0_xattn_w_in': _L0_xattn_in['w_in'], 'L0_xattn_b_in': _L0_xattn_in['b_in'], 'L0_xattn_w_out': _L0_xattn_in['w_out'], 'L0_xattn_b_out': _L0_xattn_in['b_out'], 'L0_xattn_w_ct': _L0_xattn_in['w_ct'], 'L0_xattn_b_ct': _L0_xattn_in['b_ct'], 'L0_ffn_gate_w': _L0_ffn_in['gate_w'], 'L0_ffn_w1': _L0_ffn_in['w1'], 'L0_ffn_w2': _L0_ffn_in['w2'], 'L0_ffn_w3': _L0_ffn_in['w3']}

def reference(x, ctx_2048, L0_attn_q_w, L0_attn_k_w, L0_attn_v_w, L0_attn_q_b, L0_attn_k_b, L0_attn_v_b, L0_attn_out_w, L0_attn_out_b, L0_xattn_w_in, L0_xattn_b_in, L0_xattn_w_out, L0_xattn_b_out, L0_xattn_w_ct, L0_xattn_b_ct, L0_ffn_gate_w, L0_ffn_w1, L0_ffn_w2, L0_ffn_w3):
    import jax
    import jax.numpy as jnp

    def _L0_attn_ref(x, q_w, k_w, v_w, q_b, k_b, v_b, out_w, out_b):
        import jax, jax.numpy as jnp
        import numpy as np
        EMBED_DIM = 256
        NUM_HEADS = 16
        HEAD_DIM = EMBED_DIM // NUM_HEADS
        BASE = 10000.0

        def rotate_half(x):
            half = x.shape[-1] // 2
            x1, x2 = (x[..., :half], x[..., half:])
            return jnp.concatenate([-x2, x1], axis=-1)

        def apply_rope(x, base=BASE):
            S, Dh = (x.shape[-2], x.shape[-1])
            inv_freq = 1.0 / base ** (jnp.arange(0, Dh, 2, dtype=jnp.float32) / Dh)
            t = jnp.arange(S, dtype=jnp.float32)
            freqs = jnp.einsum('i,j->ij', t, inv_freq)
            emb = jnp.concatenate([freqs, freqs], axis=-1)
            return x * jnp.cos(emb) + rotate_half(x) * jnp.sin(emb)
        B, S, D = x.shape
        H, Dh = (NUM_HEADS, HEAD_DIM)
        scaling = Dh ** (-0.5)
        q = (x @ q_w.T + q_b).reshape(B, S, H, Dh).transpose(0, 2, 1, 3)
        k = (x @ k_w.T + k_b).reshape(B, S, H, Dh).transpose(0, 2, 1, 3)
        v = (x @ v_w.T + v_b).reshape(B, S, H, Dh).transpose(0, 2, 1, 3)
        q = apply_rope(q)
        k = apply_rope(k)
        attn = jnp.einsum('bhqd,bhkd->bhqk', q, k) * scaling
        probs = jax.nn.softmax(attn, axis=-1)
        out = jnp.einsum('bhqk,bhkd->bhqd', probs, v)
        out = out.transpose(0, 2, 1, 3).reshape(B, S, D)
        return out @ out_w.T + out_b

    def _L0_xattn_ref(mask, encodings, w_in, b_in, w_out, b_out, w_ct, b_ct, local_size):
        import jax, jax.numpy as jnp
        import numpy as np
        N, E, T, H = (8, 64, 256, 8)
        n, e, t = mask.shape
        d = e // H
        x = jnp.transpose(mask, (0, 2, 1))
        qkv = x @ w_in.T + b_in
        q, k, v = jnp.split(qkv, 3, axis=-1)
        q = q.reshape(n, t, H, d)
        k = k.reshape(n, t, H, d)
        v = v.reshape(n, t, H, d)
        scores = jnp.einsum('bqhd,bkhd->bhqk', q, k) / jnp.sqrt(jnp.asarray(d, q.dtype))
        idx = jnp.arange(t)
        band = jnp.abs(idx[:, None] - idx[None, :]) <= local_size
        neg = jnp.asarray(jnp.finfo(scores.dtype).min, scores.dtype)
        scores = jnp.where(band[None, None], scores, neg)
        attn = jax.nn.softmax(scores, axis=-1)
        o = jnp.einsum('bhqk,bkhd->bqhd', attn, v).reshape(n, t, e)
        o = o @ w_out.T + b_out
        o = jnp.transpose(o, (0, 2, 1))
        y = jax.nn.relu(o) * encodings
        out = jnp.einsum('nit,io->not', y, w_ct) + b_ct[None, :, None]
        return out

    def _L0_ffn_ref(hidden_states, gate_w, w1, w2, w3):
        import jax, jax.numpy as jnp
        import numpy as np
        import math
        NUM_EXPERTS = 12
        TOP_K = 2
        CAP_FACTOR = 1.25
        B, S, H = hidden_states.shape
        T = B * S
        E = gate_w.shape[0]
        cap = math.ceil(T / E * CAP_FACTOR)
        x = hidden_states.reshape(T, H)
        logits = x @ gate_w.T
        probs = jax.nn.softmax(logits, axis=-1)
        rw, sel = jax.lax.top_k(probs, TOP_K)
        rw = rw / rw.sum(axis=-1, keepdims=True)
        ar_cap = jnp.arange(cap)
        ar_flat = jnp.arange(TOP_K * T, dtype=jnp.int32)

        def per_expert(e, we1, we2, we3):
            mask = sel.T == e
            fm = mask.ravel()
            pos = jnp.cumsum(fm) - 1
            slot_idx = jnp.where(fm & (pos < cap), pos, cap)
            buf = jnp.zeros(cap + 1, jnp.int32).at[slot_idx].set(ar_flat)
            flat = buf[:cap]
            valid = ar_cap < fm.sum()
            tok = flat % T
            slot = flat // T
            xs = x[tok]
            h = jax.nn.silu(xs @ we1.T * (xs @ we3.T)) @ we2.T
            w = jnp.where(valid, rw[tok, slot], 0.0)
            return (tok, h * w[:, None])
        toks, contribs = jax.vmap(per_expert)(jnp.arange(E), w1, w2, w3)
        out = jnp.zeros((T, H), x.dtype).at[toks.ravel()].add(contribs.reshape(-1, H))
        return out.reshape(B, S, H)
    x = x + _L0_attn_ref(_layernorm(x, axis=-1), L0_attn_q_w, L0_attn_k_w, L0_attn_v_w, L0_attn_q_b, L0_attn_k_b, L0_attn_v_b, L0_attn_out_w, L0_attn_out_b)
    x = x + _L0_xattn_ref(_layernorm(x, axis=-1), ctx_2048, L0_xattn_w_in, L0_xattn_b_in, L0_xattn_w_out, L0_xattn_b_out, L0_xattn_w_ct, L0_xattn_b_ct, 64)
    x = x + _L0_ffn_ref(_layernorm(x, axis=-1), L0_ffn_gate_w, L0_ffn_w1, L0_ffn_w2, L0_ffn_w3)
    return x

_drawn_inputs = setup_inputs


def setup_inputs(seed=0):
    import zlib

    import numpy as np

    out = dict(_drawn_inputs(seed))
    spreads = {'L0_attn_q_b': (0.0, 0.401),
     'L0_attn_k_b': (0.0, 0.589),
     'L0_attn_v_b': (0.0, 0.1),
     'L0_attn_out_b': (0.0, 0.1),
     'L0_xattn_b_in': (0.0, 0.1),
     'L0_xattn_b_out': (0.0, 0.1),
     'L0_xattn_b_ct': (0.0, 0.1)}
    factors = {'L0_ffn_gate_w': 8.0, 'L0_ffn_w1': 8.0, 'L0_ffn_w2': 8.0, 'L0_ffn_w3': 8.0}
    for name, (base, spread) in spreads.items():
        noise = np.random.default_rng([zlib.crc32(name.encode()), seed]).standard_normal(out[name].shape)
        drawn = base * np.exp(spread * noise) if base else spread * noise
        out[name] = jnp.asarray(drawn.astype(out[name].dtype))
    for name, factor in factors.items():
        out[name] = (out[name] * factor).astype(out[name].dtype)
    return out
```

```python
from contextlib import ExitStack

import numpy as np

import concourse.bass as bass
from concourse import mybir

ALU = mybir.AluOpType
ACT = mybir.ActivationFunctionType
F32 = mybir.dt.float32
BF16 = mybir.dt.bfloat16
AX = mybir.AxisListType

P = 128
D = 256
SEQ = 64
NB = 32
TILES = NB * SEQ // P
EPS = 1e-5

H1 = 16
D1 = D // H1
HC = H1 // 2

SLOTS = 3


def want(eng, sem, n):
    if isinstance(n, int) and n <= 0:
        return
    eng.wait_ge(sem, n)


def want_alone(eng, sem, n, passed):
    if isinstance(n, int) and n <= 0:
        return
    eng.wait_ge(sem, n)
    eng.sem_inc(passed, 1)


def run_steps(eng, body, lags):
    head, last = 2, TILES // SLOTS
    for t in range(SLOTS * head):
        body(t, t // SLOTS, t % SLOTS)
    with eng.Fori(head, last) as turn:
        for slot in range(SLOTS):
            body(turn * SLOTS + slot, turn, slot)
    for t in range(last * SLOTS, TILES + lags):
        body(t, t // SLOTS, t % SLOTS)


def live(t, lag):
    return not isinstance(t, int) or 0 <= t - lag < TILES


def self_attention(nc, ctx, io, xres, consts_sem, c):

    def sb(name, shape, dt=F32):
        return ctx.enter_context(nc.sbuf_tensor(name, shape, dt))

    def sem(name):
        return ctx.enter_context(nc.semaphore(name))

    x_in = sb("x_in", [P, SLOTS, D])
    xb = sb("xb", [P, SLOTS, D])
    stats = sb("stats", [P, SLOTS, 6])
    mv = sb("mv", [P, SLOTS, 2])
    vare = sb("vare", [P, SLOTS, 1])
    rstd = sb("rstd", [P, SLOTS, 1])
    z = sb("z", [P, SLOTS, D])
    zT = sb("zT", [P, SLOTS, 2, P])
    qk = sb("qk", [P, SLOTS, 2 * D])
    qk_cos = sb("qk_cos", [P, SLOTS, 2 * D])
    qk_rot = sb("qk_rot", [P, SLOTS, 2 * D])
    qk_rope = sb("qk_rope", [P, SLOTS, 2 * D])
    qkT = sb("qkT", [P, SLOTS, 4, P])
    kTm = sb("kTm", [P, SLOTS, 2, HC, P])
    v_bd = sb("v_bd", [P, SLOTS, 2, HC, 2, D1 + 1])
    top = sb("top", [P, SLOTS, H1])
    prob = sb("prob", [P, SLOTS, H1, SEQ])
    probT = sb("probT", [P, SLOTS, HC, P])
    rden = sb("rden", [P, SLOTS, H1])
    att = sb("att", [P, SLOTS, H1, D1])
    attT = sb("attT", [P, SLOTS, 2, P])

    ps_z = ctx.enter_context(nc.psum_tensor("ps_z", [P, 2, P], F32))
    ps_qk = ctx.enter_context(nc.psum_tensor("ps_qk", [P, 512], F32))
    ps_v = ctx.enter_context(nc.psum_tensor("ps_v", [P, 512], F32))
    ps_s = ctx.enter_context(nc.psum_tensor("ps_s", [P, 2, 512], F32))
    ps_pT = ctx.enter_context(nc.psum_tensor("ps_pT", [P, 2, 512], F32))
    ps_o = ctx.enter_context(nc.psum_tensor("ps_o", [P, 512], F32))

    x_loaded = [sem(f"a_x_loaded{i}") for i in range(SLOTS)]
    cleared = sem("a_cleared")
    stats_done = sem("a_stats")
    mv_done = sem("a_mean_var")
    vare_done = sem("a_vare")
    rstd_done = sem("a_rstd")
    norm_done = sem("a_norm")
    xb_done = sem("a_xb")
    zT_done = sem("a_zT")
    zT_copied = sem("a_zT_copied")
    qk_done = sem("a_qk")
    v_done = sem("a_v")
    qk_biased = sem("a_qk_biased")
    v_copied = sem("a_v_copied")
    cos_done = sem("a_cos")
    rot_done = sem("a_rot")
    rope_done = sem("a_rope")
    qkT_done = sem("a_qkT")
    qkT_copied = sem("a_qkT_copied")
    masked = sem("a_masked")
    s_done = sem("a_s")
    top_done = sem("a_top")
    sub_done = sem("a_sub")
    exp_done = sem("a_exp")
    pT_done = sem("a_pT")
    pT_copied = sem("a_pT_copied")
    o_done = sem("a_o")
    rden_done = sem("a_rden")
    att_done = sem("a_att")
    attT_done = sem("a_attT")
    attT_copied = sem("a_attT_copied")
    y_done = sem("a_y")
    x1_done = sem("a_x1")

    x_tiles = io["x"].rearrange("(n b) s d -> n (b s) d", b=2)
    block = nc.Block()
    ctx.enter_context(block)

    @block.sync
    def _(sp):
        def body(t, turn, s0):
            s1, s2 = (s0 - 1) % SLOTS, (s0 - 2) % SLOTS
            if live(t, 0):
                want(sp, norm_done, t - 1)
                want(sp, xb_done, t - 1)
                sp.dma_start(x_in[:, s0, :], x_tiles[t]).then_inc(x_loaded[s0], 16)
        run_steps(sp, body, 2)

    @block.gpsimd
    def _(pool):
        pool.wait_ge(consts_sem, c["loaded"])
        pool.memset(v_bd[:], 0.0).then_inc(cleared, 1)
        pool.wait_ge(cleared, 1)
        pool.memset(v_bd[0:64, :, :, :, 0, D1], 1.0).then_inc(cleared, 1)
        pool.memset(v_bd[64:128, :, :, :, 1, D1], 1.0).then_inc(cleared, 1)
        pool.wait_ge(cleared, 3)

        def body(t, turn, s0):
            s1, s2 = (s0 - 1) % SLOTS, (s0 - 2) % SLOTS
            if live(t, 0):
                pool.wait_ge(mv_done, t + 1)
                want(pool, norm_done, t - 2)
                pool.tensor_tensor(vare[:, s0, :], mv[:, s0, 1:2], c["eps"][:], ALU.add).then_inc(vare_done, 1)
                pool.wait_ge(vare_done, t + 1)
                pool.tensor_tensor(rstd[:, s0, :], vare[:, s0, :], c["minus_half"][:], ALU.pow).then_inc(rstd_done, 1)
                pool.wait_ge(qk_biased, t + 1)
                want(pool, rope_done, t - 1)
                pool.tensor_tensor(
                    qk_cos[:, s0, :].rearrange("p (h d) -> p h d", d=D1), qk[:, s0, :].rearrange("p (h d) -> p h d", d=D1),
                    c["cos"][:].rearrange("p (o d) -> p o d", o=1).broadcast_to([P, 2 * H1, D1]), ALU.mult).then_inc(cos_done, 1)
                pool.wait_ge(qkT_copied, t + 1)
                want(pool, s_done, t - 1)
                for ch in range(2):
                    i = pool.tensor_tensor(
                        kTm[:, s0, ch, :, :],
                        qkT[:, s0, 2 + ch:3 + ch, :].broadcast_to([P, HC, P]),
                        c["hmask"][:].rearrange("p (h o) -> p h o", o=1).broadcast_to([P, HC, P]), ALU.mult)
                i.then_inc(masked, 1)
        run_steps(pool, body, 2)

    @block.tensor
    def _(pe):
        pe.wait_ge(consts_sem, c["loaded"])

        def body(t, turn, s0):
            s1, s2 = (s0 - 1) % SLOTS, (s0 - 2) % SLOTS
            if live(t, 2):
                i = t - 2
                pe.wait_ge(exp_done, i + 1)
                want(pe, pT_copied, 2 * i)
                for hh in range(HC):
                    m = pe.transpose(ps_pT[:, hh // 4, (hh % 4) * P:(hh % 4 + 1) * P],
                                     prob[:, s2, 2 * hh:2 * hh + 2, :].rearrange("p h k -> p (h k)"), c["ident"][:])
                m.then_inc(pT_done, 1)
            if live(t, 0):
                pe.wait_ge(norm_done, t + 1)
                want(pe, attT_copied, t - 2)
                for ch in range(2):
                    m = pe.transpose(ps_z[:, ch, :], z[:, s0, ch * P:(ch + 1) * P], c["ident"][:])
                m.then_inc(zT_done, 1)
            if live(t, 1):
                i = t - 1
                pe.wait_ge(masked, i + 1)
                want(pe, sub_done, i)
                for ch in range(2):
                    for b in range(2):
                        m = pe.matmul(ps_s[64 * b:64 * b + 64, ch, :].rearrange("p (h k) -> p h k", k=SEQ),
                                      qkT[:, s1, ch, 64 * b:64 * b + 64], kTm[:, s1, ch, :, 64 * b:64 * b + 64],
                                      start=True, stop=True)
                m.then_inc(s_done, 1)
            if live(t, 2):
                i = t - 2
                pe.wait_ge(pT_copied, 2 * (i + 1))
                want(pe, att_done, i)
                pe.wait_ge(v_copied, i + 1)
                for hh in range(HC):
                    for b in range(2):
                        m = pe.matmul(ps_o[64 * b:64 * b + 64, hh * 34:hh * 34 + 34],
                                      probT[:, s2, hh, 64 * b:64 * b + 64],
                                      v_bd[:, s2, b, hh, :, :].rearrange("p g d -> p (g d)"),
                                      start=True, stop=True)
                m.then_inc(o_done, 1)
            if live(t, 0):
                pe.wait_ge(zT_copied, t + 1)
                want(pe, qkT_copied, t)
                for ch in range(2):
                    m = pe.matmul(ps_qk[:], zT[:, s0, ch, :], c["wqk"][:, ch, :], start=(ch == 0), stop=(ch == 1))
                m.then_inc(qk_done, 1)
                want(pe, x1_done, t - 2)
                for b in range(2):
                    for g in range(2):
                        for ch in range(2):
                            m = pe.matmul(ps_v[64 * g:64 * g + 64, b * D:(b + 1) * D], zT[:, s0, ch, 64 * b:64 * b + 64],
                                          c["wv"][:, ch, :], start=(ch == 0), stop=(ch == 1))
                m.then_inc(v_done, 1)
            if live(t, 2):
                i = t - 2
                pe.wait_ge(att_done, i + 1)
                if live(t, 0):
                    pe.wait_ge(zT_copied, t + 1)
                for ch in range(2):
                    m = pe.transpose(ps_z[:, ch, :], att[:, s2, ch * 8:ch * 8 + 8, :].rearrange("p h d -> p (h d)"), c["ident"][:])
                m.then_inc(attT_done, 1)
            if live(t, 0):
                pe.wait_ge(rope_done, t + 1)
                for j in range(4):
                    m = pe.transpose(ps_qk[:, j * P:(j + 1) * P], qk_rope[:, s0, j * P:(j + 1) * P], c["ident"][:])
                m.then_inc(qkT_done, 1)
            if live(t, 2):
                i = t - 2
                pe.wait_ge(attT_copied, i + 1)
                if live(t, 0):
                    pe.wait_ge(v_copied, t + 1)
                else:
                    want(pe, x1_done, i)
                for ch in range(2):
                    m = pe.matmul(ps_v[:, 0:D], attT[:, s2, ch, :], c["wo"][:, ch, :], start=(ch == 0), stop=(ch == 1))
                m.then_inc(y_done, 1)
        run_steps(pe, body, 2)

    @block.scalar
    def _(act):
        def body(t, turn, s0):
            s1, s2 = (s0 - 1) % SLOTS, (s0 - 2) % SLOTS
            if live(t, 2):
                i = t - 2
                act.wait_ge(pT_done, i + 1)
                want(act, o_done, i - 1)
                nc.scalar.copy(probT[:, s2, 0:4, :].rearrange("p h t -> p (h t)"), ps_pT[:, 0, :]).then_inc(pT_copied, 1)
            if live(t, 0):
                act.wait_ge(zT_done, t + 1)
                want(act, v_done, t - 1)
                nc.scalar.copy(zT[:, s0, :, :].rearrange("p c t -> p (c t)"), ps_z[:].rearrange("p c t -> p (c t)")).then_inc(zT_copied, 1)
            if live(t, 2):
                i = t - 2
                act.wait_ge(attT_done, i + 1)
                want(act, y_done, i - 1)
                nc.scalar.copy(attT[:, s2, :, :].rearrange("p c t -> p (c t)"), ps_z[:].rearrange("p c t -> p (c t)")).then_inc(attT_copied, 1)
            if live(t, 1):
                i = t - 1
                act.wait_ge(sub_done, i + 1)
                pr = prob[:, s1, :, :].rearrange("p h k -> p (h k)")
                nc.scalar.activation(pr, pr, ACT.Exp, scale=float(D1) ** -0.5).then_inc(exp_done, 1)
            if live(t, 0):
                act.wait_ge(qkT_done, t + 1)
                want(act, s_done, t - 1)
                nc.scalar.copy(qkT[:, s0, :, :].rearrange("p c t -> p (c t)"), ps_qk[:]).then_inc(qkT_copied, 1)
        run_steps(act, body, 2)

    @block.vector
    def _(dve):
        dve.wait_ge(consts_sem, c["loaded"])
        dve.wait_ge(cleared, 3)

        def body(t, turn, s0):
            s1, s2 = (s0 - 1) % SLOTS, (s0 - 2) % SLOTS
            if live(t, 0):
                dve.wait_ge(x_loaded[s0], 16 * (turn + 1))
                want(dve, zT_done, t - 1)
                nc.vector.bn_stats(stats[:, s0, :], x_in[:, s0, :]).then_inc(stats_done, 1)
                dve.wait_ge(stats_done, t + 1)
                nc.vector.tensor_tensor(xb[:, s0, :], x_in[:, s0, :], c["ob"][:], ALU.add).then_inc(xb_done, 1)
                nc.vector.bn_aggr(mv[:, s0, :], stats[:, s0, :]).then_inc(mv_done, 1)
                dve.wait_ge(rstd_done, t + 1)
                nc.vector.tensor_scalar(z[:, s0, :], x_in[:, s0, :], mv[:, s0, 0:1], rstd[:, s0, :], ALU.subtract, ALU.mult).then_inc(norm_done, 1)
            if live(t, 2):
                i = t - 2
                dve.wait_ge(pT_done, i + 1)
                want(dve, o_done, i - 1)
                nc.vector.tensor_copy(probT[:, s2, 4:8, :].rearrange("p h t -> p (h t)"), ps_pT[:, 1, :]).then_inc(pT_copied, 1)
            if live(t, 1):
                i = t - 1
                dve.wait_ge(s_done, i + 1)
                s = ps_s[:].rearrange("p c (h k) -> p (c h) k", k=SEQ)
                nc.vector.tensor_reduce(top[:, s1, :], s, AX.X, ALU.max).then_inc(top_done, 1)
                dve.wait_ge(top_done, i + 1)
                want(dve, pT_done, i - 1)
                nc.vector.tensor_tensor(prob[:, s1, :, :], s, top[:, s1, :].rearrange("p (h o) -> p h o", o=1).broadcast_to([P, H1, SEQ]),
                                        ALU.subtract).then_inc(sub_done, 1)
            if live(t, 0):
                dve.wait_ge(qk_done, t + 1)
                want(dve, cos_done, t - 1)
                want(dve, rot_done, 2 * (t - 1))
                nc.vector.tensor_tensor(qk[:, s0, :], ps_qk[:], c["qkb"][:], ALU.add).then_inc(qk_biased, 1)
                dve.wait_ge(v_done, t + 1)
                want(dve, o_done, t - 2)
                for g in range(2):
                    rows = slice(64 * g, 64 * g + 64)
                    m = nc.vector.tensor_tensor(
                        v_bd[rows, s0, :, :, g, 0:D1].rearrange("p b h d -> p (b h) d"),
                        ps_v[rows, :].rearrange("p (b h g d) -> p (b h) g d", b=2, g=2, d=D1)[:, :, g, :],
                        c["vb"][rows, :].rearrange("p (b h g d) -> p (b h) g d", b=2, g=2, d=D1)[:, :, g, :], ALU.add)
                m.then_inc(v_copied, 1)
                dve.wait_ge(qk_biased, t + 1)
                q4 = qk[:, s0, :].rearrange("p (h two d) -> p h two d", two=2, d=D1 // 2)
                r4 = qk_rot[:, s0, :].rearrange("p (h two d) -> p h two d", two=2, d=D1 // 2)
                for half in range(2):
                    nc.vector.tensor_tensor(
                        r4[:, :, half, :], q4[:, :, 1 - half, :],
                        c["sin"][:, half * 8:half * 8 + 8].rearrange("p (o d) -> p o d", o=1).broadcast_to([P, 2 * H1, D1 // 2]),
                        ALU.mult).then_inc(rot_done, 1)
                dve.wait_ge(rot_done, 2 * (t + 1))
                dve.wait_ge(cos_done, t + 1)
                want(dve, qkT_done, t - 1)
                nc.vector.tensor_tensor(qk_rope[:, s0, :], qk_cos[:, s0, :], qk_rot[:, s0, :], ALU.add).then_inc(rope_done, 1)
            if live(t, 2):
                i = t - 2
                dve.wait_ge(o_done, i + 1)
                o = ps_o[:, 0:H1 * (D1 + 1)].rearrange("p (h d) -> p h d", d=D1 + 1)
                nc.vector.reciprocal(rden[:, s2, :], o[:, :, D1]).then_inc(rden_done, 1)
                dve.wait_ge(rden_done, i + 1)
                want(dve, attT_done, i - 1)
                nc.vector.tensor_tensor(att[:, s2, :, :], o[:, :, 0:D1],
                                        rden[:, s2, :].rearrange("p (h o) -> p h o", o=1).broadcast_to([P, H1, D1]), ALU.mult).then_inc(att_done, 1)
                dve.wait_ge(y_done, i + 1)
                nc.vector.tensor_tensor(xres[:, i, :], ps_v[:, 0:D], xb[:, s2, :], ALU.add).then_inc(x1_done, 1)
        run_steps(dve, body, 2)
    return x1_done




H2 = 8
D2 = SEQ // H2
HP = H2 // 2
TERMS = 6
ROWS = TERMS * D2
NEG = -1e30
ORDER = ((0, 0, 0, 1, 1, 2), (0, 1, 2, 0, 1, 0))
KB = D // 64
W_IN = 192


def ctx_attention(nc, ctx, io, xres, consts_sem, c):

    def sb(name, shape, dt=F32):
        return ctx.enter_context(nc.sbuf_tensor(name, shape, dt))

    def sem(name):
        return ctx.enter_context(nc.semaphore(name))

    def bank(name):
        return ctx.enter_context(nc.psum_tensor(name, [P, 512], F32))

    stats = sb("b_stats", [P, SLOTS, 6])
    mv = sb("b_mv", [P, SLOTS, 2])
    vare = sb("b_vare", [P, SLOTS, 1])
    rstd = sb("b_rstd", [P, SLOTS, 1])
    z = sb("b_z", [P, SLOTS, D])
    split = sb("split", [P, SLOTS, 2, 3, D], BF16)
    rest = sb("rest", [P, SLOTS, 2, D])
    stack = [sb(f"stack{i}", [P, SLOTS, 2, HP, D], BF16) for i in range(2)]
    v_bd = sb("b_v_bd", [P, SLOTS, 2, HP, KB, 32])
    top = sb("b_top", [P, SLOTS, KB, 2, HP])
    top_bd = sb("top_bd", [P, SLOTS, KB, 32])
    shift = sb("shift", [96, SLOTS, D], BF16)
    shift_rest = sb("shift_rest", [96, SLOTS, D])
    prob = sb("b_prob", [P, 2, 5 * 512])
    oT = sb("oT", [P, 2, D])
    rden = sb("b_rden", [P, 2, D])
    on = sb("on", [P, 2, D])
    stats_ready = sb("stats_ready", [1, 1])
    enc = sb("enc", [P, SLOTS, D])
    yr = sb("yr", [P, D])
    gated = sb("gated", [P, D])
    scratch = nc.dram_tensor("qk_terms", [SLOTS, 2, 16, TERMS, D2, D], BF16, kind="Internal").ap()

    ps_s = [bank(f"b_ps_s{i}") for i in range(2)]
    ps_t = [bank(f"b_ps_t{i}") for i in range(2)]
    ps_a = bank("b_ps_a")
    ps_b = bank("b_ps_b")
    ps_c = bank("b_ps_c")
    ps_o = bank("b_ps_o")

    cleared = sem("b_cleared")
    stats_done = sem("b_stats_done")
    stats_seen = sem("b_stats_seen")
    mv_done = sem("b_mv_done")
    vare_done = sem("b_vare_done")
    rstd_done = sem("b_rstd_done")
    norm_done = sem("b_norm_done")
    qk_done = sem("b_qk_done")
    v_done = sem("b_v_done")
    part0_done = sem("part0_done")
    rest_done = sem("rest_done")
    part1_done = sem("part1_done")
    part2_done = sem("part2_done")
    v_copied = sem("b_v_copied")
    written = [sem(f"written{i}") for i in range(SLOTS)]
    stacked = [sem(f"stacked{i}") for i in range(SLOTS)]
    enc_loaded = [sem(f"enc_loaded{i}") for i in range(SLOTS)]
    s_done = sem("b_s_done")
    max_done = sem("b_max_done")
    top_bd_done = sem("top_bd_done")
    shift_ps = sem("shift_ps")
    shift0 = sem("shift0")
    shift_r = sem("shift_r")
    shift1 = sem("shift1")
    shift2 = sem("shift2")
    t_done = sem("b_t_done")
    exp_done = sem("b_exp_done")
    o_done = sem("b_o_done")
    oT_copied = sem("oT_copied")
    den_done = sem("den_done")
    rden_done = sem("b_rden_done")
    on_done = sem("on_done")
    y_done = sem("b_y_done")
    yr_done = sem("yr_done")
    gated_done = sem("gated_done")
    passed = sem("sp_passed")
    f_done = sem("f_done")
    x2_done = sem("x2_done")

    def units(b):
        if b < HP:
            return [(b, kb, (kb - 1) * W_IN, (kb - 1) * 64, W_IN) for kb in (1, 2)]
        kb = 0 if b == HP else 3
        return [(hp, kb, hp * 128, 0 if kb == 0 else 128, 128) for hp in range(HP)]

    BANKS = HP + 2
    cols = [2 * W_IN] * HP + [512, 512]
    start = [sum(cols[:b]) for b in range(BANKS)]

    def masked_out(ps, b):
        if b < HP:
            return ps[:, 0:2 * W_IN].rearrange("p (u s c) -> p u s c", u=2, s=3)[:, :, 0:3:2, :]
        half = 1 if b == HP else 0
        return ps[:, :].rearrange("p (u s c) -> p u s c", u=4, s=2)[:, :, half, :]

    def mask_of(b):
        if b < HP:
            return c["band_in"][:].rearrange("p (u s c) -> p u s c", u=2, s=2)
        return (c["band_0"] if b == HP else c["band_3"])[:].rearrange("p (u c) -> p u c", u=4)

    n_tiles = io["ctx"].rearrange("(n b) s d -> n (b s) d", b=2)

    def tile_turn(turn, s0, lag):
        return turn + (s0 - lag) // SLOTS

    LAGS = 5
    LATE = 4
    BOTH = 2 * BANKS

    def by_key(t, u):
        lag, e = (3, u - LATE) if u >= LATE else (4, u - LATE + BOTH)
        return lag, e // BANKS, e % BANKS

    with nc.Block() as block:
        @block.sync
        def _(sp):
            def body(t, turn, s0):
                if live(t, 3):
                    i, s = t - 3, (s0 - 3) % SLOTS
                    want_alone(sp, gated_done, i - 2, passed)
                    sp.dma_start(enc[:, s, :], n_tiles[i]).then_inc(enc_loaded[s], 16)
                if live(t, 1):
                    i, s = t - 1, (s0 - 1) % SLOTS
                    own = tile_turn(turn, s0, 1)
                    want_alone(sp, stacked[s], 64 * own, passed)
                    for j, done, n in ((0, part0_done, 2 * (i + 1)), (1, part1_done, i + 1), (2, part2_done, i + 1)):
                        want_alone(sp, done, n, passed)
                        for qk, order in enumerate(ORDER):
                            for term in range(TERMS):
                                if order[term] == j:
                                    sp.dma_start(scratch[s, qk, :, term, :, :], split[:, s, qk, j, :]).then_inc(written[s], 16)
                    want_alone(sp, written[s], 2 * TERMS * 16 * (own + 1), passed)
                    want_alone(sp, t_done, BOTH * (i - 2), passed)
                    for qk in range(2):
                        for g in range(2):
                            sp.dma_start(stack[qk][64 * g:64 * g + ROWS, s, :, :, :].rearrange("r n h t -> r (n h) t"),
                                         scratch[s, qk].rearrange("(x g) m d t -> g (m d) x t", g=2)[g]).then_inc(stacked[s], 16)
            run_steps(sp, body, LAGS)

        @block.gpsimd
        def _(pool):
            pool.memset(v_bd[:], 0.0).then_inc(cleared, 1)
            pool.memset(top_bd[:], 0.0).then_inc(cleared, 1)
            pool.wait_ge(cleared, 2)
            pool.memset(v_bd[0:64, :, :, :, :, D2], 1.0).then_inc(cleared, 1)
            pool.memset(v_bd[64:128, :, :, :, :, 16 + D2], 1.0).then_inc(cleared, 1)
            pool.wait_ge(cleared, 4)

            def body(t, turn, s0):
                if live(t, 1):
                    i, s = t - 1, (s0 - 1) % SLOTS
                    pool.wait_ge(part1_done, i + 1)
                    want(pool, written[s], 2 * TERMS * 16 * tile_turn(turn, s0, 1))
                    pool.tensor_tensor(split[:, s, :, 2, :], rest[:, s, :, :], split[:, s, :, 1, :], ALU.subtract).then_inc(part2_done, 1)
                if live(t, 5):
                    i, s = t - 5, (s0 - 5) % SLOTS
                    pool.wait_ge(yr_done, i + 1)
                    pool.wait_ge(enc_loaded[s], 16 * (tile_turn(turn, s0, 5) + 1))
                    want(pool, f_done, i)
                    pool.tensor_tensor(gated[:], yr[:], enc[:, s, :], ALU.mult).then_inc(gated_done, 1)
                if live(t, 0):
                    pool.wait_ge(mv_done, t + 1)
                    want(pool, norm_done, t - 2)
                    pool.tensor_tensor(vare[:, s0, :], mv[:, s0, 1:2], c["eps"][:], ALU.add).then_inc(vare_done, 1)
                    pool.wait_ge(vare_done, t + 1)
                    pool.tensor_tensor(rstd[:, s0, :], vare[:, s0, :], c["minus_half"][:], ALU.pow).then_inc(rstd_done, 1)
                if live(t, 4):
                    i = t - 4
                    for n in range(2):
                        pool.wait_ge(rden_done, 4 * i + 2 * n + 2)
                        want(pool, y_done, 2 * i + n - 1)
                        pool.tensor_tensor(on[:, n, :], oT[:, n, :], rden[:, n, :], ALU.mult).then_inc(on_done, 1)
            run_steps(pool, body, LAGS)

        @block.tensor
        def _(pe):
            pe.wait_ge(consts_sem, c["loaded"])

            def scores(n, b, s, ps, left, right):
                pe.matmul(masked_out(ps, b), c["identb"][:], mask_of(b), start=True, stop=False, skip_group_check=True)
                for hp, kb, col, tok, w in units(b):
                    for g in range(2):
                        r = slice(64 * g, 64 * g + ROWS)
                        m = pe.matmul(ps[64 * g:64 * g + 64, col:col + w], left[r, s, n, hp, 64 * kb:64 * kb + 64],
                                      right[r, s, n, hp, tok:tok + w], start=False, stop=False, skip_group_check=True)
                return m

            def weighted(i, s, n):
                if n == 0:
                    pe.wait_ge(v_copied, i + 1)
                pe.wait_ge(exp_done, BOTH * i + BANKS * (n + 1))
                want(pe, oT_copied, 2 * i + n)
                for kb in (1, 3, 0, 2):
                    for hp in range(HP):
                        b = hp if kb in (1, 2) else HP + (kb == 3)
                        _, _, col, tok, w = [u for u in units(b) if u[0] == hp and u[1] == kb][0]
                        m = pe.matmul(ps_o[32 * hp:32 * hp + 32, tok:tok + w], v_bd[:, s, n, hp, kb, :],
                                      prob[:, n, start[b] + col:start[b] + col + w],
                                      start=(kb == 1), stop=(kb == 2), skip_group_check=True)
                m.then_inc(o_done, 1)

            def between(t, s0, u):
                if u == 0 and live(t, 3):
                    i, s = t - 3, (s0 - 3) % SLOTS
                    pe.wait_ge(top_bd_done, i + 1)
                    want(pe, rden_done, 4 * (i - 1))
                    for qb in range(KB):
                        for j in range(3):
                            m = pe.matmul(ps_c[32 * j:32 * j + 32, 64 * qb:64 * qb + 64], top_bd[:, s, qb, :], c["ident2"][:],
                                          start=True, stop=True)
                    m.then_inc(shift_ps, 1)
                if u == 6 and live(t, 5):
                    i = t - 5
                    pe.wait_ge(gated_done, i + 1)
                    pe.matmul(ps_b[:, 0:D], c["w_ct"][:], gated[:], start=True, stop=True).then_inc(f_done, 1)
                if u == 5 and live(t, 4):
                    weighted(t - 4, (s0 - 4) % SLOTS, 1)
                if u == 8 and live(t, 1):
                    i, s = t - 1, (s0 - 1) % SLOTS
                    want(pe, x2_done, t - 4)
                    for kb in range(KB):
                        for g in range(2):
                            m = pe.matmul(ps_b[64 * g:64 * g + 64, kb * P:(kb + 1) * P], z[:, s, kb * 64:kb * 64 + 64],
                                          c["w_v"][:], start=True, stop=True)
                    m.then_inc(v_done, 1)
                if u == 7 and live(t, 4):
                    i = t - 4
                    pe.wait_ge(oT_copied, 2 * i + 2)
                    if live(t, 3):
                        pe.wait_ge(shift_r, i + 2)
                    pe.matmul(ps_c[:], c["den_rows"][:], oT[:].rearrange("p n t -> p (n t)"), start=True, stop=True).then_inc(den_done, 1)
                if u == 2 and live(t, 5):
                    i = t - 5
                    if live(t, 2):
                        pe.wait_ge(v_copied, t - 1)
                    else:
                        want(pe, x2_done, i)
                    for n in range(2):
                        pe.wait_ge(on_done, 2 * i + n + 1)
                        pe.matmul(ps_b[64 * n:64 * n + 64, 0:D], c["w_out"][:], on[:, n, :], start=True, stop=True).then_inc(y_done, 1)
                if u == 11 and live(t, 3):
                    weighted(t - 3, (s0 - 3) % SLOTS, 0)

            def body(t, turn, s0):
                if live(t, 1):
                    i, s = t - 1, (s0 - 1) % SLOTS
                    pe.wait_ge(norm_done, i + 1)
                    want(pe, rest_done, 2 * i)
                    for qk in range(2):
                        m = pe.matmul(ps_a[:, qk * D:(qk + 1) * D], c["w_qk"][:, qk, :], z[:, s, :], start=True, stop=True)
                    m.then_inc(qk_done, 1)
                for u in range(BOTH):
                    if live(t, 2):
                        i, s = t - 2, (s0 - 2) % SLOTS
                        if u == 0:
                            pe.wait_ge(stacked[s], 64 * (tile_turn(turn, s0, 2) + 1))
                        e = BOTH * i + u
                        want(pe, max_done, e - 1)
                        scores(u // BANKS, u % BANKS, s, ps_s[u % 2], stack[0], stack[1]).then_inc(s_done, 1)
                    lag, n, b = by_key(t, u)
                    if live(t, lag):
                        i, s = t - lag, (s0 - lag) % SLOTS
                        e = BOTH * i + BANKS * n + b
                        if n == 0 and b == 0:
                            pe.wait_ge(shift2, i + 1)
                        want(pe, exp_done, e - 1)
                        ps = ps_t[b % 2]
                        scores(n, b, s, ps, stack[1], stack[0])
                        for hp, kb, col, tok, w in units(b):
                            m = pe.matmul(ps[:, col:col + w], c["pick"][:, n * HP + hp, :], shift[:, s, tok:tok + w],
                                          start=False, stop=True, skip_group_check=True)
                        m.then_inc(t_done, 1)
                    between(t, s0, u)
            run_steps(pe, body, LAGS)

        @block.scalar
        def _(act):
            act.wait_ge(consts_sem, c["loaded"])

            def copy_o(i, n):
                act.wait_ge(o_done, 2 * i + n + 1)
                want(act, on_done, 2 * i + n - 1)
                nc.scalar.copy(oT[:, n, :], ps_o[:, 0:D]).then_inc(oT_copied, 1)

            def body(t, turn, s0):
                if live(t, 4):
                    copy_o(t - 4, 0)
                if live(t, 1):
                    i, s = t - 1, (s0 - 1) % SLOTS
                    act.wait_ge(qk_done, i + 1)
                    want(act, written[s], 2 * TERMS * 16 * tile_turn(turn, s0, 1))
                    for qk in range(2):
                        nc.scalar.activation(split[:, s, qk, 0, :], ps_a[:, qk * D:(qk + 1) * D], ACT.Identity,
                                             bias=c["b_qk"][:, qk:qk + 1]).then_inc(part0_done, 1)
                for u in range(BOTH):
                    if u == 1 and live(t, 3):
                        i, s = t - 3, (s0 - 3) % SLOTS
                        act.wait_ge(shift_ps, i + 1)
                        want(act, t_done, BOTH * (i - 2))
                        nc.scalar.copy(shift[:, s, :], ps_c[0:96, 0:D]).then_inc(shift0, 1)
                    lag, n, b = by_key(t, u)
                    if live(t, lag):
                        i = t - lag
                        if b == 0:
                            want(act, o_done, 2 * i + n - 1)
                        act.wait_ge(t_done, BOTH * i + BANKS * n + b + 1)
                        nc.scalar.activation(prob[:, n, start[b]:start[b] + cols[b]], ps_t[b % 2][:, 0:cols[b]],
                                             ACT.Exp, scale=float(D2) ** -0.5).then_inc(exp_done, 1)
                    if u == 1 and live(t, 3):
                        i, s = t - 3, (s0 - 3) % SLOTS
                        act.wait_ge(shift_r, i + 1)
                        for j in (1, 2):
                            r = slice(32 * j, 32 * j + 32)
                            nc.scalar.copy(shift[r, s, :], shift_rest[r, s, :]).then_inc(shift1, 1)
                    if u == 1 and live(t, 1):
                        i, s = t - 1, (s0 - 1) % SLOTS
                        act.wait_ge(rest_done, 2 * (i + 1))
                        nc.scalar.copy(split[:, s, :, 1, :], rest[:, s, :, :]).then_inc(part1_done, 1)
                    if u == 3 and live(t, 5):
                        i = t - 5
                        act.wait_ge(y_done, 2 * (i + 1))
                        want(act, gated_done, i)
                        nc.scalar.activation(yr[:], ps_b[:, 0:D], ACT.Relu, bias=c["b_out"][:]).then_inc(yr_done, 1)
                    if u == 6 and live(t, 4):
                        copy_o(t - 4, 1)
            run_steps(act, body, LAGS)

        @block.vector
        def _(dve):
            dve.wait_ge(consts_sem, c["loaded"])
            dve.wait_ge(cleared, 4)

            def between(t, s0, u):
                if u == 0 and live(t, 1):
                    i, s = t - 1, (s0 - 1) % SLOTS
                    dve.wait_ge(part0_done, 2 * (i + 1))
                    want(dve, part2_done, i - 2)
                    for qk in range(2):
                        nc.vector.scalar_tensor_tensor(out=rest[:, s, qk, :], in0=ps_a[:, qk * D:(qk + 1) * D], scalar=c["b_qk"][:, qk:qk + 1],
                                                       in1=split[:, s, qk, 0, :], op0=ALU.add, op1=ALU.subtract).then_inc(rest_done, 1)
                if u == 1 and live(t, 3):
                    i, s = t - 3, (s0 - 3) % SLOTS
                    dve.wait_ge(shift0, i + 1)
                    nc.vector.tensor_tensor(shift_rest[:, s, :], ps_c[0:96, 0:D], shift[:, s, :], ALU.subtract).then_inc(shift_r, 1)
                if u == 7 and live(t, 5):
                    i = t - 5
                    dve.wait_ge(f_done, i + 1)
                    nc.vector.scalar_tensor_tensor(out=xres[:, i, :], in0=ps_b[:, 0:D], scalar=c["b_ct"][:], in1=xres[:, i, :],
                                                   op0=ALU.add, op1=ALU.add).then_inc(x2_done, 1)
                if u == 2 and live(t, 3):
                    i, s = t - 3, (s0 - 3) % SLOTS
                    dve.wait_ge(shift1, 2 * (i + 1))
                    nc.vector.tensor_tensor(shift[64:96, s, :], shift_rest[64:96, s, :], shift[64:96, s, :], ALU.subtract).then_inc(shift2, 1)
                if u == 3 and live(t, 0):
                    nc.vector.bn_stats(stats[:, s0, :], xres[:, t, :]).then_inc(stats_done, 1)
                if u == 4 and live(t, 0):
                    dve.wait_ge(stats_done, t + 1)
                    nc.vector.tensor_copy(stats_ready[:], stats[0:1, s0, 0:1]).then_inc(stats_seen, 1)
                    nc.vector.bn_aggr(mv[:, s0, :], stats[:, s0, :]).then_inc(mv_done, 1)
                if u == 6 and live(t, 0):
                    dve.wait_ge(rstd_done, t + 1)
                    want(dve, v_done, t - 2)
                    nc.vector.tensor_scalar(z[:, s0, :], xres[:, t, :], mv[:, s0, 0:1], rstd[:, s0, :], ALU.subtract, ALU.mult).then_inc(norm_done, 1)
                if u == 9 and live(t, 1):
                    i, s = t - 1, (s0 - 1) % SLOTS
                    dve.wait_ge(v_done, i + 1)
                    want(dve, o_done, 2 * (i - 2))
                    for g in range(2):
                        r = slice(64 * g, 64 * g + 64)
                        m = nc.vector.tensor_tensor(
                            v_bd[r, s, :, :, :, 16 * g:16 * g + D2].rearrange("p n h k d -> p (n h) k d"),
                            ps_b[r, :].rearrange("p (k x g d) -> p g x k d", k=KB, g=2, d=D2)[:, g],
                            c["b_v"][r, g, :].rearrange("p (x o d) -> p x o d", o=1, d=D2).broadcast_to([64, 8, KB, D2]), ALU.add)
                    m.then_inc(v_copied, 1)
                if u >= 8 and live(t, 4):
                    i, n, half = t - 4, (u - 8) // 2, (u - 8) % 2
                    dve.wait_ge(den_done, i + 1)
                    want(dve, on_done, 2 * i + n - 1)
                    q = slice(half * P, (half + 1) * P)
                    nc.vector.reciprocal(rden[:, n, q], ps_c[:, n * D + half * P:n * D + (half + 1) * P]).then_inc(rden_done, 1)

            def body(t, turn, s0):
                for u in range(BOTH):
                    if live(t, 2):
                        i, s, n, b = t - 2, (s0 - 2) % SLOTS, u // BANKS, u % BANKS
                        dve.wait_ge(s_done, BOTH * i + u + 1)
                        if b < HP:
                            dst, src = top[:, s, 1:3, n, b], ps_s[b % 2][:, 0:2 * W_IN].rearrange("p (u w) -> p u w", u=2)
                        else:
                            dst, src = top[:, s, 0 if b == HP else 3, n, :], ps_s[b % 2][:].rearrange("p (u w) -> p u w", u=4)
                        nc.vector.tensor_reduce(dst, src, AX.X, ALU.max).then_inc(max_done, 1)
                    between(t, s0, u)
                if live(t, 2):
                    i, s = t - 2, (s0 - 2) % SLOTS
                    dve.wait_ge(max_done, BOTH * (i + 1))
                    nc.vector.tensor_tensor(
                        top_bd[:, s, :, 0:16].rearrange("p k (x g) -> p k x g", g=2),
                        top[:, s, :, :, :].rearrange("p k n (h o) -> p k (n h) o", o=1).broadcast_to([P, KB, 8, 2]),
                        c["minus_half_rows"][:].rearrange("p (a b g) -> p a b g", a=1, b=1).broadcast_to([P, KB, 8, 2]), ALU.mult).then_inc(top_bd_done, 1)
            run_steps(dve, body, LAGS)
    return x2_done


E = 12
F = 32
CAP = -(-NB * SEQ * 5 // (E * 4))
HID = E * F // P
GROUP = 512
GROUPS = NB * SEQ // GROUP
GT = GROUP // P
PICKS = 2


def gate_logits(nc, ctx, xres, zT, ps_l, consts_sem, c):

    def sb(name, shape, dt=F32):
        return ctx.enter_context(nc.sbuf_tensor(name, shape, dt))

    def sem(name):
        return ctx.enter_context(nc.semaphore(name))

    stats = sb("g_stats", [P, SLOTS, 6])
    stats_ready = sb("g_stats_ready", [1, 1])
    mv = sb("g_mv", [P, SLOTS, 2])
    vare = sb("g_vare", [P, SLOTS, 1])
    rstd = sb("g_rstd", [P, SLOTS, 1])
    z = sb("g_z", [P, SLOTS, D])
    zt = sb("g_zt", [P, SLOTS, 2, P])
    stats_done, stats_seen, mv_done, vare_done, rstd_done, norm_done, t_done, t_copied, l_done = (
        sem("g_" + n) for n in ("stats_done", "stats_seen", "mv_done", "vare_done", "rstd_done", "norm_done", "t_done", "t_copied", "l_done"))

    with nc.psum_tensor("g_ps0", [P, 512], F32) as ps0, nc.psum_tensor("g_ps1", [P, 512], F32) as ps1, \
            nc.psum_tensor("g_ps2", [P, 512], F32) as ps2, nc.Block() as block:
        ps = [ps0, ps1, ps2]

        @block.gpsimd
        def _(pool):
            pool.wait_ge(consts_sem, c["loaded"])

            def body(t, turn, s0):
                if live(t, 0):
                    pool.wait_ge(mv_done, t + 1)
                    want(pool, norm_done, t - 2)
                    pool.tensor_tensor(vare[:, s0, :], mv[:, s0, 1:2], c["eps"][:], ALU.add).then_inc(vare_done, 1)
                    pool.wait_ge(vare_done, t + 1)
                    pool.tensor_tensor(rstd[:, s0, :], vare[:, s0, :], c["minus_half"][:], ALU.pow).then_inc(rstd_done, 1)
            run_steps(pool, body, 1)

        @block.vector
        def _(dve):
            def body(t, turn, s0):
                if live(t, 0):
                    nc.vector.bn_stats(stats[:, s0, :], xres[:, t, :]).then_inc(stats_done, 1)
                    dve.wait_ge(stats_done, t + 1)
                    nc.vector.tensor_copy(stats_ready[:], stats[0:1, s0, 0:1]).then_inc(stats_seen, 1)
                    nc.vector.bn_aggr(mv[:, s0, :], stats[:, s0, :]).then_inc(mv_done, 1)
                if live(t, 1):
                    i, s = t - 1, (s0 - 1) % SLOTS
                    dve.wait_ge(rstd_done, i + 1)
                    want(dve, t_done, i - 2)
                    nc.vector.tensor_scalar(z[:, s, :], xres[:, i, :], mv[:, s, 0:1], rstd[:, s, :], ALU.subtract, ALU.mult).then_inc(norm_done, 1)
            run_steps(dve, body, 1)

        @block.tensor
        def _(pe):
            pe.wait_ge(consts_sem, c["loaded"])

            def body(t, turn, s0):
                if live(t, 0):
                    pe.wait_ge(norm_done, t + 1)
                    want(pe, t_copied, 2 * (t - 2))
                    for ch in range(2):
                        m = pe.transpose(ps[s0][:, ch * P:(ch + 1) * P], z[:, s0, ch * P:(ch + 1) * P], c["ident"][:])
                    m.then_inc(t_done, 1)
                if live(t, 1):
                    i, s = t - 1, (s0 - 1) % SLOTS
                    pe.wait_ge(t_copied, 2 * (i + 1))
                    for ch in range(2):
                        m = pe.matmul(ps_l[:, i, :], zt[:, s, ch, :], c["gate"][:, ch, :], start=(ch == 0), stop=(ch == 1))
                    m.then_inc(l_done, 1)
            run_steps(pe, body, 1)

        @block.scalar
        def _(act):
            def body(t, turn, s0):
                if live(t, 0):
                    act.wait_ge(t_done, t + 1)
                    want(act, l_done, t - 2)
                    src = ps[s0][:, 0:2 * P].rearrange("p (c t) -> p c t", c=2)
                    nc.scalar.copy(zt[:, s0, :, :], src).then_inc(t_copied, 1)
                    nc.scalar.copy(zT[:, :, t, :], src).then_inc(t_copied, 1)
            run_steps(act, body, 1)


def route(nc, ctx, wT, ps_l, consts_sem, c):

    def sb(name, shape, dt=F32):
        return ctx.enter_context(nc.sbuf_tensor(name, shape, dt))

    def wide(x, n=E):
        return x.rearrange("p (a o) -> p a o", o=1).broadcast_to([P, x.shape[1], n])

    less = sb("r_less", [P, TILES, E])
    prob = sb("r_prob", [P, TILES, E])
    key = sb("r_key", [P, TILES, E])
    eq = sb("r_eq", [P, TILES, E])
    sel = sb("r_sel", [P, PICKS, TILES, E])
    best = sb("r_best", [P, PICKS, TILES])
    low = sb("r_low", [P, 4, TILES])
    eqt = sb("r_total_by_expert", [P, E, PICKS * TILES])
    run = sb("r_run", [P, E, PICKS * TILES])
    pos = sb("r_pos", [P, PICKS * TILES, E])
    w = sb("r_w", [P, TILES, E])
    step_done = ctx.enter_context(nc.semaphore("route_step"))
    less_done = ctx.enter_context(nc.semaphore("less_done"))
    exp_done = ctx.enter_context(nc.semaphore("route_exp"))
    sel_done = ctx.enter_context(nc.semaphore("sel_done"))
    counted = ctx.enter_context(nc.semaphore("counted"))
    w_done = ctx.enter_context(nc.semaphore("w_done"))
    w_turned = ctx.enter_context(nc.semaphore("w_turned"))
    wT_done = ctx.enter_context(nc.semaphore("wT_done"))

    with nc.psum_tensor("r_rank", [P, 512], F32) as ps_rank, nc.psum_tensor("r_total", [P, 512], F32) as ps_total, \
            nc.psum_tensor("r_wT", [P, GROUPS, GROUP], F32) as ps_w, nc.Block() as block:

        @block.vector
        def _(dve):
            steps = [0]

            def then(ins):
                steps[0] += 1
                ins.then_inc(step_done, 1)
                dve.wait_ge(step_done, steps[0])

            v = nc.vector
            dve.wait_ge(consts_sem, c["loaded"])
            lg = ps_l[:]
            then(v.tensor_reduce(low[:, 0, :], lg, AX.X, ALU.max))
            v.tensor_tensor(less[:], lg, wide(low[:, 0, :]), ALU.subtract).then_inc(less_done, 1)
            dve.wait_ge(exp_done, 1)
            then(v.tensor_reduce(low[:, 1, :], prob[:], AX.X, ALU.add))
            then(v.reciprocal(low[:, 2, :], low[:, 1, :]))
            then(v.tensor_tensor(prob[:], prob[:], wide(low[:, 2, :]), ALU.mult))
            for k in range(PICKS):
                then(v.tensor_reduce(best[:, k, :], prob[:], AX.X, ALU.max))
                then(v.tensor_tensor(eq[:], prob[:], wide(best[:, k, :]), ALU.is_equal))
                then(v.tensor_tensor(key[:], eq[:], c["order"][:].rearrange("p (o e) -> p o e", o=1).broadcast_to([P, TILES, E]), ALU.mult))
                then(v.tensor_reduce(low[:, 3, :], key[:], AX.X, ALU.max))
                then(v.tensor_tensor(sel[:, k, :, :], key[:], wide(low[:, 3, :]), ALU.is_equal))
                if k == 0:
                    then(v.scalar_tensor_tensor(out=prob[:], in0=sel[:, 0, :, :], scalar=-2.0, in1=prob[:], op0=ALU.mult, op1=ALU.add))
            then(v.tensor_tensor(low[:, 0, :], best[:, 0, :], best[:, 1, :], ALU.add))
            then(v.reciprocal(low[:, 1, :], low[:, 0, :]))
            last = v.scalar_tensor_tensor(out=best[:], in0=best[:], scalar=0.5,
                                          in1=low[:, 1:2, :].broadcast_to([P, PICKS, TILES]), op0=ALU.mult, op1=ALU.mult)
            then(last)
            v.memset(low[:, 2, :], 0.0).then_inc(sel_done, 1)
            dve.wait_ge(counted, 2)
            total = ps_total[:, 0:PICKS * TILES * E].rearrange("p (j e) -> p e j", e=E)
            then(v.tensor_tensor(eqt[:], total, c["zero"][:].rearrange("p (a b) -> p a b", a=E), ALU.add))
            then(v.tensor_tensor_scan(run[:].rearrange("p e j -> p (e j)"), c["carry"][:], eqt[:].rearrange("p e j -> p (e j)"), 0.0, ALU.mult, ALU.add))
            then(v.tensor_tensor(run[:], run[:], eqt[:], ALU.subtract))
            then(v.tensor_tensor(pos[:], ps_rank[:, 0:PICKS * TILES * E].rearrange("p (j e) -> p j e", e=E), run[:].rearrange("p e j -> p j e"), ALU.add))
            selj = sel[:].rearrange("p k t e -> p (k t) e")
            then(v.scalar_tensor_tensor(out=pos[:], in0=pos[:], scalar=float(CAP), in1=selj, op0=ALU.is_le, op1=ALU.mult))
            then(v.tensor_tensor(pos[:], pos[:], wide(best[:].rearrange("p k t -> p (k t)")), ALU.mult))
            v.tensor_tensor(w[:], pos[:, 0:TILES, :], pos[:, TILES:, :], ALU.add).then_inc(w_done, 1)
            dve.wait_ge(w_turned, 1)
            for g in range(GROUPS):
                m = v.tensor_copy(wT[:, g * GROUP:(g + 1) * GROUP], ps_w[0:E, g, :])
            m.then_inc(wT_done, 1)

        @block.scalar
        def _(act):
            act.wait_ge(less_done, 1)
            nc.scalar.activation(prob[:], less[:], ACT.Exp).then_inc(exp_done, 1)

        @block.tensor
        def _(pe):
            pe.wait_ge(sel_done, 1)
            s = sel[:].rearrange("p k t e -> p (k t e)")
            n = PICKS * TILES * E
            pe.matmul(ps_rank[:, 0:n], c["upto"][:], s, start=True, stop=True).then_inc(counted, 1)
            pe.matmul(ps_total[:, 0:n], c["ones"][:], s, start=True, stop=True).then_inc(counted, 1)
            pe.wait_ge(w_done, 1)
            for t in range(TILES):
                m = pe.transpose(ps_w[0:E, t // GT, (t % GT) * P:(t % GT + 1) * P], w[:, t, :], c["ident"][:])
            m.then_inc(w_turned, 1)


def experts(nc, ctx, io, xres, zT, wT, consts_sem, c):

    def sb(name, shape, dt=F32):
        return ctx.enter_context(nc.sbuf_tensor(name, shape, dt))

    def sem(name):
        return ctx.enter_context(nc.semaphore(name))

    up3 = sb("up3", [P, 2, GROUP])
    prod = sb("prod", [P, 2, GROUP])
    act_h = sb("act_h", [P, 2, GROUP])
    hid = sb("hid", [P, HID, GROUP])
    out = sb("x_out", [P, 2, 2, D])
    up_done, up3_copied, prod_done, silu_done, hid_done, down_done, out_done = (
        sem("e_" + n) for n in ("up_done", "up3_copied", "prod_done", "silu_done", "hid_done", "down_done", "out_done"))
    twice = sem("e_twice")
    stored = [sem(f"stored{i}") for i in range(2)]
    ps_1, ps_3, ps_w, ps_d = ([ctx.enter_context(nc.psum_tensor(f"e_ps{n}{i}", [P, 512], F32)) for i in range(2)] for n in "13wd")
    out_tiles = io["out"].rearrange("(n b) s d -> (b s) n d", b=2)

    with nc.Block() as block:
        @block.sync
        def _(sp):
            def body(g):
                for half in range(2):
                    sp.wait_ge(out_done, GT * g + 2 * half + 2)
                    sp.dma_start(out_tiles[:, bass.ds(GT * g + 2 * half, 2), :], out[:, half, :, :]).then_inc(stored[half], 16)
            body(0)
            with sp.Fori(1, GROUPS) as g:
                body(g)
            for half in range(2):
                sp.wait_ge(stored[half], 16 * GROUPS)

        @block.tensor
        def _(pe):
            pe.wait_ge(consts_sem, c["loaded"])
            def body(g):
                z = [zT[:, ch, bass.ds(GT * g, GT), :].rearrange("p t c -> p (t c)") for ch in range(2)]
                for h in range(HID):
                    cols = slice(h * P, (h + 1) * P)
                    want(pe, hid_done, HID * g + max(h - 1, 0))
                    for ch in range(2):
                        pe.matmul(ps_1[h % 2][:], c["w1"][:, ch, cols], z[ch], start=(ch == 0), stop=(ch == 1))
                    for ch in range(2):
                        pe.matmul(ps_3[h % 2][:], c["w3"][:, ch, cols], z[ch], start=(ch == 0), stop=(ch == 1))
                    pe.matmul(ps_w[h % 2][:], c["expand"][:, cols], wT[:, bass.ds(GROUP * g, GROUP)], start=True, stop=True).then_inc(up_done, 1)
                pe.wait_ge(hid_done, HID * g + HID)
                for t in range(GT):
                    want(pe, out_done, GT * g + max(t - 1, 0))
                    for h in range(HID):
                        m = pe.matmul(ps_d[t % 2][:, 0:D], hid[:, h, t * P:(t + 1) * P], c["w2"][:, h, :], start=(h == 0), stop=(h == HID - 1))
                    m.then_inc(down_done, 1)
            body(0)
            with pe.Fori(1, GROUPS) as g:
                body(g)

        @block.scalar
        def _(act):
            def body(g):
                for h in range(HID):
                    act.wait_ge(up_done, HID * g + h + 1)
                    if h == 2:
                        act.wait_ge(prod_done, HID * g + 1)
                    else:
                        want(act, prod_done, HID * g)
                    nc.scalar.copy(up3[:, h % 2, :], ps_3[h % 2][:]).then_inc(up3_copied, 1)
                    act.wait_ge(prod_done, HID * g + h + 1)
                    nc.scalar.activation(act_h[:, h % 2, :], prod[:, h % 2, :], ACT.Tanh, scale=0.5).then_inc(silu_done, 1)
            body(0)
            with act.Fori(1, GROUPS) as g:
                body(g)

        @block.vector
        def _(dve):
            def body(g):
                for h in range(HID):
                    dve.wait_ge(up3_copied, HID * g + h + 1)
                    nc.vector.tensor_tensor(prod[:, h % 2, :], ps_1[h % 2][:], up3[:, h % 2, :], ALU.mult).then_inc(prod_done, 1)
                    dve.wait_ge(silu_done, HID * g + h + 1)
                    nc.vector.scalar_tensor_tensor(out=act_h[:, h % 2, :], in0=act_h[:, h % 2, :], scalar=1.0, in1=prod[:, h % 2, :],
                                                   op0=ALU.add, op1=ALU.mult).then_inc(twice, 1)
                    dve.wait_ge(twice, HID * g + h + 1)
                    want(dve, down_done, GT * g)
                    nc.vector.tensor_tensor(hid[:, h, :], act_h[:, h % 2, :], ps_w[h % 2][:], ALU.mult).then_inc(hid_done, 1)
                for t in range(GT):
                    dve.wait_ge(down_done, GT * g + t + 1)
                    want(dve, stored[t // 2], 16 * g)
                    nc.vector.tensor_tensor(out[:, t // 2, t % 2, :], ps_d[t % 2][:, 0:D], xres[:, GT * g + t, :], ALU.add).then_inc(out_done, 1)
            body(0)
            with dve.Fori(1, GROUPS) as g:
                body(g)


def program(nc, io, DEBUG=False):
    ctx = ExitStack()
    with ctx:
        def sb(name, shape, dt=F32):
            return ctx.enter_context(nc.sbuf_tensor(name, shape, dt))

        xres = sb("xres", [P, TILES, D])

        def load(names, stage, narrow=()):
            loaded = stage.enter_context(nc.semaphore("consts_" + names[0]))
            c = {n: stage.enter_context(nc.sbuf_tensor(f"{names[0]}_{n}", list(io[n].shape), io[n].dtype)) for n in names}
            c16 = {n: stage.enter_context(nc.sbuf_tensor(f"{n}_16", list(io[n].shape), BF16)) for n in narrow}
            with nc.Block() as block:
                @block.sync
                def _(sp):
                    for n in names:
                        sp.dma_start(c[n][:], io[n]).then_inc(loaded, 16)
                    sp.wait_ge(loaded, 16 * len(names))

                @block.vector
                def _(dve):
                    if narrow:
                        dve.wait_ge(loaded, 16 * len(names))
                    for n in narrow:
                        i = nc.vector.tensor_copy(c16[n][:], c[n][:])
                    if narrow:
                        i.then_inc(loaded, 1)
            c.update(c16)
            c["loaded"] = 16 * len(names) + (1 if narrow else 0)
            return loaded, c

        with ExitStack() as stage:
            loaded, c = load(["ident", "wqk", "wv", "wo", "qkb", "vb", "ob", "cos", "sin", "hmask", "minus_half", "eps"], stage)
            self_attention(nc, stage, io, xres, loaded, c)
        with ExitStack() as stage:
            loaded, c = load(["identb", "w_qk", "w_v", "b_qk", "b_v", "w_out", "b_out", "w_ct", "b_ct", "band_in", "band_0", "band_3",
                              "pick", "den_rows", "ident2", "minus_half_rows", "minus_half", "eps"], stage, ["identb", "band_in", "band_0", "band_3", "pick"])
            ctx_attention(nc, stage, io, xres, loaded, c)
        if DEBUG:
            with nc.Block() as block, nc.semaphore("out_done") as od:
                @block.sync
                def _(sp):
                    sp.dma_start(io["out"].rearrange("(n b) s d -> (b s) n d", b=2), xres[:]).then_inc(od, 16)
                    sp.wait_ge(od, 16)
            return
        with ExitStack() as stage:
            loaded, c = load(["gate", "order", "carry", "zero", "upto", "ones", "expand", "w1", "w3", "w2", "ident", "minus_half", "eps"], stage)
            zT = stage.enter_context(nc.sbuf_tensor("zT_all", [P, 2, TILES, P], F32))
            wT = stage.enter_context(nc.sbuf_tensor("wT", [E, NB * SEQ], F32))
            with nc.psum_tensor("logits", [P, TILES, E], F32) as ps_l:
                gate_logits(nc, stage, xres, zT, ps_l, loaded, c)
                route(nc, stage, wT, ps_l, loaded, c)
            experts(nc, stage, io, xres, zT, wT, loaded, c)


def layout(x):
    f = np.float32

    def cut(w):
        return np.ascontiguousarray(w.reshape(2, P, -1).transpose(1, 0, 2))

    pos = np.arange(SEQ, dtype=f)
    inv = (1.0 / 10000.0 ** (np.arange(0, D1, 2, dtype=f) / f(D1))).astype(f)
    ang = np.tile(pos[:, None] * inv[None, :], (2, 2)).astype(f)
    sin = np.sin(ang)
    sin[:, :D1 // 2] *= -1
    def pair(w):
        out = np.zeros((P, P), f)
        out[:64, :64] = out[64:, 64:] = w
        return out

    w_in, b_in = x["L0_xattn_w_in"], x["L0_xattn_b_in"]
    pq, ph = np.arange(P) % 64, np.arange(P) // 64
    col = np.arange(64)
    prev = np.where(col[None] >= pq[:, None], 0, NEG).astype(f)
    nxt = np.where(col[None] <= pq[:, None], 0, NEG).astype(f)
    w_out = np.zeros((P, 64), f)
    den = np.zeros((P, P), f)
    for h in range(H2):
        w_out[16 * h:16 * h + D2] = x["L0_xattn_w_out"].T[D2 * h:D2 * h + D2]
        den[16 * h + D2, 16 * h:16 * h + 16] = 1
    pick = np.zeros((96, 2 * HP, P), f)
    for j in range(3):
        for r in range(16):
            pick[32 * j + r, r // 2] = ph == r % 2
    b_v = np.tile(b_in[128:].reshape(HP, 2, D2), (2, 1, 1)).transpose(1, 0, 2).reshape(2, 64)
    rows = lambda v: np.ascontiguousarray(np.broadcast_to(v, (P, v.shape[-1])))
    return {
        "x": x["x"],
        "minus_half": np.full((P, 1), -0.5, f),
        "eps": np.full((P, 1), EPS, f),
        "ident": np.eye(P, dtype=f),
        "wqk": cut(np.concatenate([x["L0_attn_q_w"].T, x["L0_attn_k_w"].T], 1)),
        "wv": cut(x["L0_attn_v_w"].T),
        "wo": cut(x["L0_attn_out_w"].T),
        "qkb": rows(np.concatenate([x["L0_attn_q_b"], x["L0_attn_k_b"]])),
        "vb": rows(np.concatenate([x["L0_attn_v_b"]] * 2)),
        "ob": rows(x["L0_attn_out_b"]),
        "cos": np.cos(ang).astype(f),
        "sin": sin.astype(f),
        "ctx": x["ctx_2048"],
        "identb": np.eye(P, dtype=f),
        "w_qk": np.stack([pair(w_in[0:64].T), pair(w_in[64:128].T)], 1),
        "w_v": pair(w_in[128:].T),
        "b_qk": np.stack([np.tile(b_in[0:64], 2), np.tile(b_in[64:128], 2)], 1),
        "b_v": np.ascontiguousarray(np.broadcast_to(b_v, (P, 2, 64))),
        "w_out": w_out,
        "b_out": np.tile(x["L0_xattn_b_out"], 2)[:, None],
        "w_ct": pair(x["L0_xattn_w_ct"]),
        "b_ct": np.tile(x["L0_xattn_b_ct"], 2)[:, None],
        "band_in": np.concatenate([prev, nxt, prev, nxt], 1),
        "band_0": np.tile(nxt, (1, 4)),
        "band_3": np.tile(prev, (1, 4)),
        "pick": pick,
        "den_rows": den,
        "ident2": (pq[:, None] == col[None]).astype(f),
        "minus_half_rows": -(ph[:, None] == np.arange(2)[None]).astype(f),
        "gate": cut(x["L0_ffn_gate_w"].T),
        "order": rows(np.arange(E, 0, -1).astype(f)),
        "carry": rows((np.arange(E * PICKS * TILES) % (PICKS * TILES) > 0).astype(f)),
        "zero": np.zeros((P, E * PICKS * TILES), f),
        "upto": np.triu(np.ones((P, P), f)),
        "ones": np.ones((P, P), f),
        "expand": (np.arange(E)[:, None] == np.arange(E * F)[None] // F).astype(f),
        "w1": cut(x["L0_ffn_w1"].reshape(E * F, D).T),
        "w3": cut(x["L0_ffn_w3"].reshape(E * F, D).T),
        "w2": np.ascontiguousarray(x["L0_ffn_w2"].transpose(0, 2, 1).reshape(HID, P, D).transpose(1, 0, 2)),
        "hmask": (np.arange(P)[:, None] // D1 == np.arange(HC)[None]).astype(f),
    }


def kernel(**inputs):
    import concourse.bacc as bacc
    from concourse.bass_utils import run_bass_kernel_spmd

    nc = bacc.Bacc("TRN2", target_bir_lowering=False, num_devices=1)
    arrays = layout({k: np.asarray(v) for k, v in inputs.items()})
    io = {k: nc.dram_tensor("in_" + k, a.shape, mybir.dt.from_np(a.dtype), kind="ExternalInput").ap() for k, a in arrays.items()}
    io["out"] = nc.dram_tensor("out", (NB, SEQ, D), F32, kind="ExternalOutput").ap()
    program(nc, io)
    got = run_bass_kernel_spmd(nc, [{"in_" + k: a for k, a in arrays.items()}], core_ids=[0])
    return got.results[0]["out"]
```

```python
from contextlib import ExitStack

import numpy as np

import concourse.bass as bass
from concourse import mybir

ALU = mybir.AluOpType
ACT = mybir.ActivationFunctionType
F32 = mybir.dt.float32
BF16 = mybir.dt.bfloat16
AX = mybir.AxisListType

P = 128
D = 256
SEQ = 64
NB = 32
TILES = NB * SEQ // P
EPS = 1e-5

H1 = 16
D1 = D // H1
HC = H1 // 2

SLOTS = 3


def want(eng, sem, n):
    if isinstance(n, int) and n <= 0:
        return
    eng.wait_ge(sem, n)


def want_alone(eng, sem, n, passed):
    if isinstance(n, int) and n <= 0:
        return
    eng.wait_ge(sem, n)
    eng.sem_inc(passed, 1)


def run_steps(eng, body, lags):
    head, last = 2, TILES // SLOTS
    for t in range(SLOTS * head):
        body(t, t // SLOTS, t % SLOTS)
    with eng.Fori(head, last) as turn:
        for slot in range(SLOTS):
            body(turn * SLOTS + slot, turn, slot)
    for t in range(last * SLOTS, TILES + lags):
        body(t, t // SLOTS, t % SLOTS)


def live(t, lag):
    return not isinstance(t, int) or 0 <= t - lag < TILES


def self_attention(nc, ctx, io, xres, consts_sem, c):

    def sb(name, shape, dt=F32):
        return ctx.enter_context(nc.sbuf_tensor(name, shape, dt))

    def sem(name):
        return ctx.enter_context(nc.semaphore(name))

    stats = sb("stats", [P, SLOTS, 6])
    stats_ready = sb("a_stats_ready", [1, 1])
    mv = sb("mv", [P, SLOTS, 2])
    vare = sb("vare", [P, SLOTS, 1])
    rstd = sb("rstd", [P, SLOTS, 1])
    z = sb("z", [P, SLOTS, D])
    zT = sb("zT", [P, SLOTS, 2, P])
    qk = sb("qk", [P, SLOTS, 2 * D])
    qk_cos = sb("qk_cos", [P, SLOTS, 2 * D])
    qk_rot = sb("qk_rot", [P, SLOTS, 2 * D])
    qk_rope = sb("qk_rope", [P, SLOTS, 2 * D])
    qkT = sb("qkT", [P, SLOTS, 4, P])
    kTm = sb("kTm", [P, SLOTS, 2, HC, P])
    v_bd = sb("v_bd", [P, SLOTS, 2, HC, 2, D1 + 1])
    top = sb("top", [P, SLOTS, H1])
    prob = sb("prob", [P, SLOTS, H1, SEQ])
    probT = sb("probT", [P, SLOTS, HC, P])
    rden = sb("rden", [P, SLOTS, H1])
    att = sb("att", [P, SLOTS, H1, D1])
    attT = sb("attT", [P, SLOTS, 2, P])

    ps_z = ctx.enter_context(nc.psum_tensor("ps_z", [P, 2, P], F32))
    ps_qk = ctx.enter_context(nc.psum_tensor("ps_qk", [P, 512], F32))
    ps_v = ctx.enter_context(nc.psum_tensor("ps_v", [P, 512], F32))
    ps_s = ctx.enter_context(nc.psum_tensor("ps_s", [P, 2, 512], F32))
    ps_pT = ctx.enter_context(nc.psum_tensor("ps_pT", [P, 2, 512], F32))
    ps_o = ctx.enter_context(nc.psum_tensor("ps_o", [P, 512], F32))

    x_loaded = [sem(f"a_x_loaded{i}") for i in range(SLOTS)]
    cleared = sem("a_cleared")
    stats_done = sem("a_stats")
    stats_seen = sem("a_stats_seen")
    mv_done = sem("a_mean_var")
    vare_done = sem("a_vare")
    rstd_done = sem("a_rstd")
    norm_done = sem("a_norm")
    xb_done = sem("a_xb")
    zT_done = sem("a_zT")
    zT_copied = sem("a_zT_copied")
    qk_done = sem("a_qk")
    v_done = sem("a_v")
    qk_biased = sem("a_qk_biased")
    v_copied = sem("a_v_copied")
    cos_done = sem("a_cos")
    rot_done = sem("a_rot")
    rope_done = sem("a_rope")
    qkT_done = sem("a_qkT")
    qkT_copied = sem("a_qkT_copied")
    masked = sem("a_masked")
    s_done = sem("a_s")
    top_done = sem("a_top")
    sub_done = sem("a_sub")
    exp_done = sem("a_exp")
    pT_done = sem("a_pT")
    pT_copied = sem("a_pT_copied")
    o_done = sem("a_o")
    rden_done = sem("a_rden")
    att_done = sem("a_att")
    attT_done = sem("a_attT")
    attT_copied = sem("a_attT_copied")
    y_done = sem("a_y")
    x1_done = sem("a_x1")

    x_tiles = io["x"].rearrange("(n b) s d -> n (b s) d", b=2)
    block = nc.Block()
    ctx.enter_context(block)

    LAGS = 5

    @block.sync
    def _(sp):
        def body(t, turn, s0):
            if live(t, 0):
                want(sp, norm_done, t - 2)
                sp.dma_start(xres[:, t, :], x_tiles[t]).then_inc(x_loaded[s0], 16)
        run_steps(sp, body, LAGS)

    @block.gpsimd
    def _(pool):
        pool.wait_ge(consts_sem, c["loaded"])
        pool.memset(v_bd[:], 0.0).then_inc(cleared, 1)
        pool.wait_ge(cleared, 1)
        pool.memset(v_bd[0:64, :, :, :, 0, D1], 1.0).then_inc(cleared, 1)
        pool.memset(v_bd[64:128, :, :, :, 1, D1], 1.0).then_inc(cleared, 1)
        pool.wait_ge(cleared, 3)

        def body(t, turn, s0):
            if live(t, 2):
                i, s = t - 2, (s0 - 2) % SLOTS
                pool.wait_ge(qkT_copied, i + 1)
                want(pool, s_done, i - 2)
                for ch in range(2):
                    m = pool.tensor_tensor(
                        kTm[:, s, ch, :, :],
                        qkT[:, s, 2 + ch:3 + ch, :].broadcast_to([P, HC, P]),
                        c["hmask"][:].rearrange("p (h o) -> p h o", o=1).broadcast_to([P, HC, P]), ALU.mult)
                m.then_inc(masked, 1)
            if live(t, 0):
                pool.wait_ge(mv_done, t + 1)
                want(pool, norm_done, t - 2)
                pool.tensor_tensor(vare[:, s0, :], mv[:, s0, 1:2], c["eps"][:], ALU.add).then_inc(vare_done, 1)
                pool.wait_ge(vare_done, t + 1)
                pool.tensor_tensor(rstd[:, s0, :], vare[:, s0, :], c["minus_half"][:], ALU.pow).then_inc(rstd_done, 1)
            if live(t, 1):
                i, s = t - 1, (s0 - 1) % SLOTS
                pool.wait_ge(qk_biased, i + 1)
                want(pool, rope_done, i - 2)
                pool.tensor_tensor(
                    qk_cos[:, s, :].rearrange("p (h d) -> p h d", d=D1), qk[:, s, :].rearrange("p (h d) -> p h d", d=D1),
                    c["cos"][:].rearrange("p (o d) -> p o d", o=1).broadcast_to([P, 2 * H1, D1]), ALU.mult).then_inc(cos_done, 1)
            if live(t, 0):
                pool.wait_ge(norm_done, t + 1)
                pool.tensor_tensor(xres[:, t, :], xres[:, t, :], c["ob"][:], ALU.add).then_inc(xb_done, 1)
        run_steps(pool, body, LAGS)

    @block.tensor
    def _(pe):
        pe.wait_ge(consts_sem, c["loaded"])

        def body(t, turn, s0):
            if live(t, 4):
                i, s = t - 4, (s0 - 4) % SLOTS
                pe.wait_ge(exp_done, i + 1)
                want(pe, pT_copied, 2 * i)
                for hh in range(HC):
                    m = pe.transpose(ps_pT[:, hh // 4, (hh % 4) * P:(hh % 4 + 1) * P],
                                     prob[:, s, 2 * hh:2 * hh + 2, :].rearrange("p h k -> p (h k)"), c["ident"][:])
                    if hh % 4 == 3:
                        m.then_inc(pT_done, 1)
            if live(t, 1):
                i, s = t - 1, (s0 - 1) % SLOTS
                pe.wait_ge(norm_done, i + 1)
                want(pe, zT_copied, i)
                for ch in range(2):
                    m = pe.transpose(ps_z[:, ch, :], z[:, s, ch * P:(ch + 1) * P], c["ident"][:])
                m.then_inc(zT_done, 1)
            if live(t, 5):
                i, s = t - 5, (s0 - 5) % SLOTS
                pe.wait_ge(att_done, i + 1)
                for ch in range(2):
                    m = pe.transpose(ps_o[:, ch * P:(ch + 1) * P], att[:, s, ch * 8:ch * 8 + 8, :].rearrange("p h d -> p (h d)"), c["ident"][:])
                m.then_inc(attT_done, 1)
            if live(t, 2):
                i, s = t - 2, (s0 - 2) % SLOTS
                pe.wait_ge(rope_done, i + 1)
                for j in range(4):
                    m = pe.transpose(ps_qk[:, j * P:(j + 1) * P], qk_rope[:, s, j * P:(j + 1) * P], c["ident"][:])
                m.then_inc(qkT_done, 1)
            if live(t, 3):
                i, s = t - 3, (s0 - 3) % SLOTS
                pe.wait_ge(masked, i + 1)
                want(pe, sub_done, i)
                for ch in range(2):
                    for b in range(2):
                        m = pe.matmul(ps_s[64 * b:64 * b + 64, ch, :].rearrange("p (h k) -> p h k", k=SEQ),
                                      qkT[:, s, ch, 64 * b:64 * b + 64], kTm[:, s, ch, :, 64 * b:64 * b + 64],
                                      start=True, stop=True)
                m.then_inc(s_done, 1)
            if live(t, 5):
                i, s = t - 5, (s0 - 5) % SLOTS
                pe.wait_ge(attT_copied, i + 1)
                if live(t, 2):
                    pe.wait_ge(v_copied, t - 1)
                else:
                    want(pe, x1_done, i)
                for ch in range(2):
                    m = pe.matmul(ps_v[:, 0:D], attT[:, s, ch, :], c["wo"][:, ch, :], start=(ch == 0), stop=(ch == 1))
                m.then_inc(y_done, 1)
            if live(t, 1):
                i, s = t - 1, (s0 - 1) % SLOTS
                pe.wait_ge(zT_copied, i + 1)
                want(pe, qkT_copied, i)
                for ch in range(2):
                    m = pe.matmul(ps_qk[:], zT[:, s, ch, :], c["wqk"][:, ch, :], start=(ch == 0), stop=(ch == 1))
                m.then_inc(qk_done, 1)
            if live(t, 4):
                i, s = t - 4, (s0 - 4) % SLOTS
                pe.wait_ge(pT_copied, 2 * (i + 1))
                pe.wait_ge(v_copied, i + 1)
                want(pe, attT_copied, i)
                for hh in range(HC):
                    for b in range(2):
                        m = pe.matmul(ps_o[64 * b:64 * b + 64, hh * 34:hh * 34 + 34],
                                      probT[:, s, hh, 64 * b:64 * b + 64],
                                      v_bd[:, s, b, hh, :, :].rearrange("p g d -> p (g d)"),
                                      start=True, stop=True)
                m.then_inc(o_done, 1)
            if live(t, 1):
                i, s = t - 1, (s0 - 1) % SLOTS
                want(pe, v_copied, i)
                want(pe, x1_done, t - 4)
                for b in range(2):
                    for ch in range(2):
                        for g in range(2):
                            m = pe.matmul(ps_v[64 * g:64 * g + 64, b * D:(b + 1) * D], zT[:, s, ch, 64 * b:64 * b + 64],
                                          c["wv"][:, ch, :], start=(ch == 0), stop=(ch == 1))
                m.then_inc(v_done, 1)
        run_steps(pe, body, LAGS)

    @block.scalar
    def _(act):
        def body(t, turn, s0):
            if live(t, 1):
                i, s = t - 1, (s0 - 1) % SLOTS
                act.wait_ge(zT_done, i + 1)
                want(act, v_done, i - 2)
                nc.scalar.copy(zT[:, s, :, :].rearrange("p c t -> p (c t)"), ps_z[:].rearrange("p c t -> p (c t)")).then_inc(zT_copied, 1)
            if live(t, 5):
                i, s = t - 5, (s0 - 5) % SLOTS
                act.wait_ge(attT_done, i + 1)
                want(act, y_done, i)
                nc.scalar.copy(attT[:, s, :, :].rearrange("p c t -> p (c t)"), ps_o[:, 0:2 * P]).then_inc(attT_copied, 1)
            if live(t, 2):
                i, s = t - 2, (s0 - 2) % SLOTS
                act.wait_ge(qkT_done, i + 1)
                want(act, s_done, i - 2)
                nc.scalar.copy(qkT[:, s, :, :].rearrange("p c t -> p (c t)"), ps_qk[:]).then_inc(qkT_copied, 1)
            if live(t, 4):
                i, s = t - 4, (s0 - 4) % SLOTS
                want(act, o_done, i - 1)
                for half in range(2):
                    act.wait_ge(pT_done, 2 * i + half + 1)
                    nc.scalar.copy(probT[:, s, 4 * half:4 * half + 4, :].rearrange("p h t -> p (h t)"), ps_pT[:, half, :]).then_inc(pT_copied, 1)
            if live(t, 3):
                i, s = t - 3, (s0 - 3) % SLOTS
                act.wait_ge(sub_done, i + 1)
                pr = prob[:, s, :, :].rearrange("p h k -> p (h k)")
                nc.scalar.activation(pr, pr, ACT.Exp, scale=float(D1) ** -0.5).then_inc(exp_done, 1)
        run_steps(act, body, LAGS)

    @block.vector
    def _(dve):
        dve.wait_ge(consts_sem, c["loaded"])
        dve.wait_ge(cleared, 3)

        def body(t, turn, s0):
            if live(t, 5):
                i, s = t - 5, (s0 - 5) % SLOTS
                dve.wait_ge(o_done, i + 1)
                o = ps_o[:, 0:H1 * (D1 + 1)].rearrange("p (h d) -> p h d", d=D1 + 1)
                nc.vector.reciprocal(rden[:, s, :], o[:, :, D1]).then_inc(rden_done, 1)
                dve.wait_ge(rden_done, i + 1)
                want(dve, attT_done, i)
                nc.vector.tensor_tensor(att[:, s, :, :], o[:, :, 0:D1],
                                        rden[:, s, :].rearrange("p (h o) -> p h o", o=1).broadcast_to([P, H1, D1]), ALU.mult).then_inc(att_done, 1)
            if live(t, 2):
                i, s = t - 2, (s0 - 2) % SLOTS
                dve.wait_ge(v_done, i + 1)
                want(dve, o_done, i - 2)
                for g in range(2):
                    rows = slice(64 * g, 64 * g + 64)
                    m = nc.vector.tensor_tensor(
                        v_bd[rows, s, :, :, g, 0:D1].rearrange("p b h d -> p (b h) d"),
                        ps_v[rows, :].rearrange("p (b h g d) -> p (b h) g d", b=2, g=2, d=D1)[:, :, g, :],
                        c["vb"][rows, :].rearrange("p (b h g d) -> p (b h) g d", b=2, g=2, d=D1)[:, :, g, :], ALU.add)
                m.then_inc(v_copied, 1)
            if live(t, 0):
                dve.wait_ge(x_loaded[s0], 16 * (turn + 1))
                nc.vector.bn_stats(stats[:, s0, :], xres[:, t, :]).then_inc(stats_done, 1)
                dve.wait_ge(stats_done, t + 1)
                nc.vector.tensor_copy(stats_ready[:], stats[0:1, s0, 0:1]).then_inc(stats_seen, 1)
                nc.vector.bn_aggr(mv[:, s0, :], stats[:, s0, :]).then_inc(mv_done, 1)
            if live(t, 3):
                i, s = t - 3, (s0 - 3) % SLOTS
                dve.wait_ge(s_done, i + 1)
                sc = ps_s[:].rearrange("p c (h k) -> p (c h) k", k=SEQ)
                nc.vector.tensor_reduce(top[:, s, :], sc, AX.X, ALU.max).then_inc(top_done, 1)
                dve.wait_ge(top_done, i + 1)
                want(dve, pT_done, 2 * (i - 2))
                nc.vector.tensor_tensor(prob[:, s, :, :], sc, top[:, s, :].rearrange("p (h o) -> p h o", o=1).broadcast_to([P, H1, SEQ]),
                                        ALU.subtract).then_inc(sub_done, 1)
            if live(t, 5):
                i = t - 5
                dve.wait_ge(y_done, i + 1)
                dve.wait_ge(xb_done, i + 1)
                nc.vector.tensor_tensor(xres[:, i, :], ps_v[:, 0:D], xres[:, i, :], ALU.add).then_inc(x1_done, 1)
            if live(t, 0):
                dve.wait_ge(rstd_done, t + 1)
                want(dve, zT_done, t - 2)
                nc.vector.tensor_scalar(z[:, s0, :], xres[:, t, :], mv[:, s0, 0:1], rstd[:, s0, :], ALU.subtract, ALU.mult).then_inc(norm_done, 1)
            if live(t, 1):
                i, s = t - 1, (s0 - 1) % SLOTS
                dve.wait_ge(qk_done, i + 1)
                want(dve, cos_done, i - 2)
                want(dve, rot_done, 2 * (i - 2))
                nc.vector.tensor_tensor(qk[:, s, :], ps_qk[:], c["qkb"][:], ALU.add).then_inc(qk_biased, 1)
                dve.wait_ge(qk_biased, i + 1)
                q4 = qk[:, s, :].rearrange("p (h two d) -> p h two d", two=2, d=D1 // 2)
                r4 = qk_rot[:, s, :].rearrange("p (h two d) -> p h two d", two=2, d=D1 // 2)
                for half in range(2):
                    nc.vector.tensor_tensor(
                        r4[:, :, half, :], q4[:, :, 1 - half, :],
                        c["sin"][:, half * 8:half * 8 + 8].rearrange("p (o d) -> p o d", o=1).broadcast_to([P, 2 * H1, D1 // 2]),
                        ALU.mult).then_inc(rot_done, 1)
                dve.wait_ge(rot_done, 2 * (i + 1))
                dve.wait_ge(cos_done, i + 1)
                want(dve, qkT_done, i - 2)
                nc.vector.tensor_tensor(qk_rope[:, s, :], qk_cos[:, s, :], qk_rot[:, s, :], ALU.add).then_inc(rope_done, 1)
        run_steps(dve, body, LAGS)
    return x1_done




H2 = 8
D2 = SEQ // H2
HP = H2 // 2
TERMS = 6
ROWS = TERMS * D2
NEG = -1e30
ORDER = ((0, 0, 0, 1, 1, 2), (0, 1, 2, 0, 1, 0))
KB = D // 64
W_IN = 192


def ctx_attention(nc, ctx, io, xres, consts_sem, c):

    def sb(name, shape, dt=F32):
        return ctx.enter_context(nc.sbuf_tensor(name, shape, dt))

    def sem(name):
        return ctx.enter_context(nc.semaphore(name))

    def bank(name):
        return ctx.enter_context(nc.psum_tensor(name, [P, 512], F32))

    stats = sb("b_stats", [P, SLOTS, 6])
    mv = sb("b_mv", [P, SLOTS, 2])
    vare = sb("b_vare", [P, SLOTS, 1])
    rstd = sb("b_rstd", [P, SLOTS, 1])
    z = sb("b_z", [P, SLOTS, D])
    split = sb("split", [P, SLOTS, 2, 3, D], BF16)
    rest = sb("rest", [P, SLOTS, 2, D])
    stack = [sb(f"stack{i}", [P, SLOTS, 2, HP, D], BF16) for i in range(2)]
    v_bd = sb("b_v_bd", [P, SLOTS, 2, HP, KB, 32])
    top = sb("b_top", [P, SLOTS, KB, 2, HP])
    top_bd = sb("top_bd", [P, SLOTS, KB, 32])
    shift = sb("shift", [96, SLOTS, D], BF16)
    shift_rest = sb("shift_rest", [96, SLOTS, D])
    prob = sb("b_prob", [P, 2, 5 * 512])
    oT = sb("oT", [P, 2, D])
    rden = sb("b_rden", [P, 2, D])
    on = sb("on", [P, 2, D])
    stats_ready = sb("stats_ready", [1, 1])
    enc = sb("enc", [P, SLOTS, D])
    yr = sb("yr", [P, D])
    gated = sb("gated", [P, D])
    scratch = nc.dram_tensor("qk_terms", [SLOTS, 2, 16, TERMS, D2, D], BF16, kind="Internal").ap()

    ps_s = [bank(f"b_ps_s{i}") for i in range(2)]
    ps_t = [bank(f"b_ps_t{i}") for i in range(2)]
    ps_a = bank("b_ps_a")
    ps_b = bank("b_ps_b")
    ps_c = bank("b_ps_c")
    ps_o = bank("b_ps_o")

    cleared = sem("b_cleared")
    stats_done = sem("b_stats_done")
    stats_seen = sem("b_stats_seen")
    mv_done = sem("b_mv_done")
    vare_done = sem("b_vare_done")
    rstd_done = sem("b_rstd_done")
    norm_done = sem("b_norm_done")
    qk_done = sem("b_qk_done")
    v_done = sem("b_v_done")
    part0_done = sem("part0_done")
    rest_done = sem("rest_done")
    part1_done = sem("part1_done")
    part2_done = sem("part2_done")
    v_copied = sem("b_v_copied")
    written = [sem(f"written{i}") for i in range(SLOTS)]
    stacked = [sem(f"stacked{i}") for i in range(SLOTS)]
    enc_loaded = [sem(f"enc_loaded{i}") for i in range(SLOTS)]
    s_done = sem("b_s_done")
    max_done = sem("b_max_done")
    top_bd_done = sem("top_bd_done")
    shift_ps = sem("shift_ps")
    shift0 = sem("shift0")
    shift_r = sem("shift_r")
    shift1 = sem("shift1")
    shift2 = sem("shift2")
    t_done = sem("b_t_done")
    exp_done = sem("b_exp_done")
    o_done = sem("b_o_done")
    oT_copied = sem("oT_copied")
    den_done = sem("den_done")
    rden_done = sem("b_rden_done")
    on_done = sem("on_done")
    y_done = sem("b_y_done")
    yr_done = sem("yr_done")
    gated_done = sem("gated_done")
    passed = sem("sp_passed")
    f_done = sem("f_done")
    x2_done = sem("x2_done")

    def units(b):
        if b < HP:
            return [(b, kb, (kb - 1) * W_IN, (kb - 1) * 64, W_IN) for kb in (1, 2)]
        kb = 0 if b == HP else 3
        return [(hp, kb, hp * 128, 0 if kb == 0 else 128, 128) for hp in range(HP)]

    BANKS = HP + 2
    cols = [2 * W_IN] * HP + [512, 512]
    start = [sum(cols[:b]) for b in range(BANKS)]

    def masked_out(ps, b):
        if b < HP:
            return ps[:, 0:2 * W_IN].rearrange("p (u s c) -> p u s c", u=2, s=3)[:, :, 0:3:2, :]
        half = 1 if b == HP else 0
        return ps[:, :].rearrange("p (u s c) -> p u s c", u=4, s=2)[:, :, half, :]

    def mask_of(b):
        if b < HP:
            return c["band_in"][:].rearrange("p (u s c) -> p u s c", u=2, s=2)
        return (c["band_0"] if b == HP else c["band_3"])[:].rearrange("p (u c) -> p u c", u=4)

    n_tiles = io["ctx"].rearrange("(n b) s d -> n (b s) d", b=2)

    def tile_turn(turn, s0, lag):
        return turn + (s0 - lag) // SLOTS

    LAGS = 5
    LATE = 4
    BOTH = 2 * BANKS

    def by_key(t, u):
        lag, e = (3, u - LATE) if u >= LATE else (4, u - LATE + BOTH)
        return lag, e // BANKS, e % BANKS

    with nc.Block() as block:
        @block.sync
        def _(sp):
            def body(t, turn, s0):
                if live(t, 3):
                    i, s = t - 3, (s0 - 3) % SLOTS
                    want_alone(sp, gated_done, i - 2, passed)
                    sp.dma_start(enc[:, s, :], n_tiles[i]).then_inc(enc_loaded[s], 16)
                if live(t, 1):
                    i, s = t - 1, (s0 - 1) % SLOTS
                    own = tile_turn(turn, s0, 1)
                    want_alone(sp, stacked[s], 64 * own, passed)
                    for j, done, n in ((0, part0_done, 2 * (i + 1)), (1, part1_done, i + 1), (2, part2_done, i + 1)):
                        want_alone(sp, done, n, passed)
                        for qk, order in enumerate(ORDER):
                            for term in range(TERMS):
                                if order[term] == j:
                                    sp.dma_start(scratch[s, qk, :, term, :, :], split[:, s, qk, j, :]).then_inc(written[s], 16)
                    want_alone(sp, written[s], 2 * TERMS * 16 * (own + 1), passed)
                    want_alone(sp, t_done, BOTH * (i - 2), passed)
                    for qk in range(2):
                        for g in range(2):
                            sp.dma_start(stack[qk][64 * g:64 * g + ROWS, s, :, :, :].rearrange("r n h t -> r (n h) t"),
                                         scratch[s, qk].rearrange("(x g) m d t -> g (m d) x t", g=2)[g]).then_inc(stacked[s], 16)
            run_steps(sp, body, LAGS)

        @block.gpsimd
        def _(pool):
            pool.memset(v_bd[:], 0.0).then_inc(cleared, 1)
            pool.memset(top_bd[:], 0.0).then_inc(cleared, 1)
            pool.wait_ge(cleared, 2)
            pool.memset(v_bd[0:64, :, :, :, :, D2], 1.0).then_inc(cleared, 1)
            pool.memset(v_bd[64:128, :, :, :, :, 16 + D2], 1.0).then_inc(cleared, 1)
            pool.wait_ge(cleared, 4)

            def body(t, turn, s0):
                if live(t, 1):
                    i, s = t - 1, (s0 - 1) % SLOTS
                    pool.wait_ge(part1_done, i + 1)
                    want(pool, written[s], 2 * TERMS * 16 * tile_turn(turn, s0, 1))
                    pool.tensor_tensor(split[:, s, :, 2, :], rest[:, s, :, :], split[:, s, :, 1, :], ALU.subtract).then_inc(part2_done, 1)
                if live(t, 5):
                    i, s = t - 5, (s0 - 5) % SLOTS
                    pool.wait_ge(yr_done, i + 1)
                    pool.wait_ge(enc_loaded[s], 16 * (tile_turn(turn, s0, 5) + 1))
                    want(pool, f_done, i)
                    pool.tensor_tensor(gated[:], yr[:], enc[:, s, :], ALU.mult).then_inc(gated_done, 1)
                if live(t, 0):
                    pool.wait_ge(mv_done, t + 1)
                    want(pool, norm_done, t - 2)
                    pool.tensor_tensor(vare[:, s0, :], mv[:, s0, 1:2], c["eps"][:], ALU.add).then_inc(vare_done, 1)
                    pool.wait_ge(vare_done, t + 1)
                    pool.tensor_tensor(rstd[:, s0, :], vare[:, s0, :], c["minus_half"][:], ALU.pow).then_inc(rstd_done, 1)
                if live(t, 4):
                    i = t - 4
                    for n in range(2):
                        pool.wait_ge(rden_done, 4 * i + 2 * n + 2)
                        want(pool, y_done, 2 * i + n - 1)
                        pool.tensor_tensor(on[:, n, :], oT[:, n, :], rden[:, n, :], ALU.mult).then_inc(on_done, 1)
            run_steps(pool, body, LAGS)

        @block.tensor
        def _(pe):
            pe.wait_ge(consts_sem, c["loaded"])

            def scores(n, b, s, ps, left, right):
                pe.matmul(masked_out(ps, b), c["identb"][:], mask_of(b), start=True, stop=False, skip_group_check=True)
                for hp, kb, col, tok, w in units(b):
                    for g in range(2):
                        r = slice(64 * g, 64 * g + ROWS)
                        m = pe.matmul(ps[64 * g:64 * g + 64, col:col + w], left[r, s, n, hp, 64 * kb:64 * kb + 64],
                                      right[r, s, n, hp, tok:tok + w], start=False, stop=False, skip_group_check=True)
                return m

            def weighted(i, s, n):
                if n == 0:
                    pe.wait_ge(v_copied, i + 1)
                pe.wait_ge(exp_done, BOTH * i + BANKS * (n + 1))
                want(pe, oT_copied, 2 * i + n)
                for kb in (1, 3, 0, 2):
                    for hp in range(HP):
                        b = hp if kb in (1, 2) else HP + (kb == 3)
                        _, _, col, tok, w = [u for u in units(b) if u[0] == hp and u[1] == kb][0]
                        m = pe.matmul(ps_o[32 * hp:32 * hp + 32, tok:tok + w], v_bd[:, s, n, hp, kb, :],
                                      prob[:, n, start[b] + col:start[b] + col + w],
                                      start=(kb == 1), stop=(kb == 2), skip_group_check=True)
                m.then_inc(o_done, 1)

            def between(t, s0, u):
                if u == 0 and live(t, 3):
                    i, s = t - 3, (s0 - 3) % SLOTS
                    pe.wait_ge(top_bd_done, i + 1)
                    want(pe, rden_done, 4 * (i - 1))
                    for qb in range(KB):
                        for j in range(3):
                            m = pe.matmul(ps_c[32 * j:32 * j + 32, 64 * qb:64 * qb + 64], top_bd[:, s, qb, :], c["ident2"][:],
                                          start=True, stop=True)
                    m.then_inc(shift_ps, 1)
                if u == 6 and live(t, 5):
                    i = t - 5
                    pe.wait_ge(gated_done, i + 1)
                    pe.matmul(ps_b[:, 0:D], c["w_ct"][:], gated[:], start=True, stop=True).then_inc(f_done, 1)
                if u == 5 and live(t, 4):
                    weighted(t - 4, (s0 - 4) % SLOTS, 1)
                if u == 8 and live(t, 1):
                    i, s = t - 1, (s0 - 1) % SLOTS
                    want(pe, x2_done, t - 4)
                    for kb in range(KB):
                        for g in range(2):
                            m = pe.matmul(ps_b[64 * g:64 * g + 64, kb * P:(kb + 1) * P], z[:, s, kb * 64:kb * 64 + 64],
                                          c["w_v"][:], start=True, stop=True)
                    m.then_inc(v_done, 1)
                if u == 7 and live(t, 4):
                    i = t - 4
                    pe.wait_ge(oT_copied, 2 * i + 2)
                    if live(t, 3):
                        pe.wait_ge(shift_r, i + 2)
                    pe.matmul(ps_c[:], c["den_rows"][:], oT[:].rearrange("p n t -> p (n t)"), start=True, stop=True).then_inc(den_done, 1)
                if u == 2 and live(t, 5):
                    i = t - 5
                    if live(t, 2):
                        pe.wait_ge(v_copied, t - 1)
                    else:
                        want(pe, x2_done, i)
                    for n in range(2):
                        pe.wait_ge(on_done, 2 * i + n + 1)
                        pe.matmul(ps_b[64 * n:64 * n + 64, 0:D], c["w_out"][:], on[:, n, :], start=True, stop=True).then_inc(y_done, 1)
                if u == 11 and live(t, 3):
                    weighted(t - 3, (s0 - 3) % SLOTS, 0)

            def body(t, turn, s0):
                if live(t, 1):
                    i, s = t - 1, (s0 - 1) % SLOTS
                    pe.wait_ge(norm_done, i + 1)
                    want(pe, rest_done, 2 * i)
                    for qk in range(2):
                        m = pe.matmul(ps_a[:, qk * D:(qk + 1) * D], c["w_qk"][:, qk, :], z[:, s, :], start=True, stop=True)
                    m.then_inc(qk_done, 1)
                for u in range(BOTH):
                    if live(t, 2):
                        i, s = t - 2, (s0 - 2) % SLOTS
                        if u == 0:
                            pe.wait_ge(stacked[s], 64 * (tile_turn(turn, s0, 2) + 1))
                        e = BOTH * i + u
                        want(pe, max_done, e - 1)
                        scores(u // BANKS, u % BANKS, s, ps_s[u % 2], stack[0], stack[1]).then_inc(s_done, 1)
                    lag, n, b = by_key(t, u)
                    if live(t, lag):
                        i, s = t - lag, (s0 - lag) % SLOTS
                        e = BOTH * i + BANKS * n + b
                        if n == 0 and b == 0:
                            pe.wait_ge(shift2, i + 1)
                        want(pe, exp_done, e - 1)
                        ps = ps_t[b % 2]
                        scores(n, b, s, ps, stack[1], stack[0])
                        for hp, kb, col, tok, w in units(b):
                            m = pe.matmul(ps[:, col:col + w], c["pick"][:, n * HP + hp, :], shift[:, s, tok:tok + w],
                                          start=False, stop=True, skip_group_check=True)
                        m.then_inc(t_done, 1)
                    between(t, s0, u)
            run_steps(pe, body, LAGS)

        @block.scalar
        def _(act):
            act.wait_ge(consts_sem, c["loaded"])

            def copy_o(i, n):
                act.wait_ge(o_done, 2 * i + n + 1)
                want(act, on_done, 2 * i + n - 1)
                nc.scalar.copy(oT[:, n, :], ps_o[:, 0:D]).then_inc(oT_copied, 1)

            def body(t, turn, s0):
                if live(t, 4):
                    copy_o(t - 4, 0)
                if live(t, 1):
                    i, s = t - 1, (s0 - 1) % SLOTS
                    act.wait_ge(qk_done, i + 1)
                    want(act, written[s], 2 * TERMS * 16 * tile_turn(turn, s0, 1))
                    for qk in range(2):
                        nc.scalar.activation(split[:, s, qk, 0, :], ps_a[:, qk * D:(qk + 1) * D], ACT.Identity,
                                             bias=c["b_qk"][:, qk:qk + 1]).then_inc(part0_done, 1)
                for u in range(BOTH):
                    if u == 1 and live(t, 3):
                        i, s = t - 3, (s0 - 3) % SLOTS
                        act.wait_ge(shift_ps, i + 1)
                        want(act, t_done, BOTH * (i - 2))
                        nc.scalar.copy(shift[:, s, :], ps_c[0:96, 0:D]).then_inc(shift0, 1)
                    lag, n, b = by_key(t, u)
                    if live(t, lag):
                        i = t - lag
                        if b == 0:
                            want(act, o_done, 2 * i + n - 1)
                        act.wait_ge(t_done, BOTH * i + BANKS * n + b + 1)
                        nc.scalar.activation(prob[:, n, start[b]:start[b] + cols[b]], ps_t[b % 2][:, 0:cols[b]],
                                             ACT.Exp, scale=float(D2) ** -0.5).then_inc(exp_done, 1)
                    if u == 1 and live(t, 3):
                        i, s = t - 3, (s0 - 3) % SLOTS
                        act.wait_ge(shift_r, i + 1)
                        for j in (1, 2):
                            r = slice(32 * j, 32 * j + 32)
                            nc.scalar.copy(shift[r, s, :], shift_rest[r, s, :]).then_inc(shift1, 1)
                    if u == 1 and live(t, 1):
                        i, s = t - 1, (s0 - 1) % SLOTS
                        act.wait_ge(rest_done, 2 * (i + 1))
                        nc.scalar.copy(split[:, s, :, 1, :], rest[:, s, :, :]).then_inc(part1_done, 1)
                    if u == 3 and live(t, 5):
                        i = t - 5
                        act.wait_ge(y_done, 2 * (i + 1))
                        want(act, gated_done, i)
                        nc.scalar.activation(yr[:], ps_b[:, 0:D], ACT.Relu, bias=c["b_out"][:]).then_inc(yr_done, 1)
                    if u == 6 and live(t, 4):
                        copy_o(t - 4, 1)
            run_steps(act, body, LAGS)

        @block.vector
        def _(dve):
            dve.wait_ge(consts_sem, c["loaded"])
            dve.wait_ge(cleared, 4)

            def between(t, s0, u):
                if u == 0 and live(t, 1):
                    i, s = t - 1, (s0 - 1) % SLOTS
                    dve.wait_ge(part0_done, 2 * (i + 1))
                    want(dve, part2_done, i - 2)
                    for qk in range(2):
                        nc.vector.scalar_tensor_tensor(out=rest[:, s, qk, :], in0=ps_a[:, qk * D:(qk + 1) * D], scalar=c["b_qk"][:, qk:qk + 1],
                                                       in1=split[:, s, qk, 0, :], op0=ALU.add, op1=ALU.subtract).then_inc(rest_done, 1)
                if u == 1 and live(t, 3):
                    i, s = t - 3, (s0 - 3) % SLOTS
                    dve.wait_ge(shift0, i + 1)
                    nc.vector.tensor_tensor(shift_rest[:, s, :], ps_c[0:96, 0:D], shift[:, s, :], ALU.subtract).then_inc(shift_r, 1)
                if u == 7 and live(t, 5):
                    i = t - 5
                    dve.wait_ge(f_done, i + 1)
                    nc.vector.scalar_tensor_tensor(out=xres[:, i, :], in0=ps_b[:, 0:D], scalar=c["b_ct"][:], in1=xres[:, i, :],
                                                   op0=ALU.add, op1=ALU.add).then_inc(x2_done, 1)
                if u == 2 and live(t, 3):
                    i, s = t - 3, (s0 - 3) % SLOTS
                    dve.wait_ge(shift1, 2 * (i + 1))
                    nc.vector.tensor_tensor(shift[64:96, s, :], shift_rest[64:96, s, :], shift[64:96, s, :], ALU.subtract).then_inc(shift2, 1)
                if u == 3 and live(t, 0):
                    nc.vector.bn_stats(stats[:, s0, :], xres[:, t, :]).then_inc(stats_done, 1)
                if u == 4 and live(t, 0):
                    dve.wait_ge(stats_done, t + 1)
                    nc.vector.tensor_copy(stats_ready[:], stats[0:1, s0, 0:1]).then_inc(stats_seen, 1)
                    nc.vector.bn_aggr(mv[:, s0, :], stats[:, s0, :]).then_inc(mv_done, 1)
                if u == 6 and live(t, 0):
                    dve.wait_ge(rstd_done, t + 1)
                    want(dve, v_done, t - 2)
                    nc.vector.tensor_scalar(z[:, s0, :], xres[:, t, :], mv[:, s0, 0:1], rstd[:, s0, :], ALU.subtract, ALU.mult).then_inc(norm_done, 1)
                if u == 9 and live(t, 1):
                    i, s = t - 1, (s0 - 1) % SLOTS
                    dve.wait_ge(v_done, i + 1)
                    want(dve, o_done, 2 * (i - 2))
                    for g in range(2):
                        r = slice(64 * g, 64 * g + 64)
                        m = nc.vector.tensor_tensor(
                            v_bd[r, s, :, :, :, 16 * g:16 * g + D2].rearrange("p n h k d -> p (n h) k d"),
                            ps_b[r, :].rearrange("p (k x g d) -> p g x k d", k=KB, g=2, d=D2)[:, g],
                            c["b_v"][r, g, :].rearrange("p (x o d) -> p x o d", o=1, d=D2).broadcast_to([64, 8, KB, D2]), ALU.add)
                    m.then_inc(v_copied, 1)
                if u >= 8 and live(t, 4):
                    i, n, half = t - 4, (u - 8) // 2, (u - 8) % 2
                    dve.wait_ge(den_done, i + 1)
                    want(dve, on_done, 2 * i + n - 1)
                    q = slice(half * P, (half + 1) * P)
                    nc.vector.reciprocal(rden[:, n, q], ps_c[:, n * D + half * P:n * D + (half + 1) * P]).then_inc(rden_done, 1)

            def body(t, turn, s0):
                for u in range(BOTH):
                    if live(t, 2):
                        i, s, n, b = t - 2, (s0 - 2) % SLOTS, u // BANKS, u % BANKS
                        dve.wait_ge(s_done, BOTH * i + u + 1)
                        if b < HP:
                            dst, src = top[:, s, 1:3, n, b], ps_s[b % 2][:, 0:2 * W_IN].rearrange("p (u w) -> p u w", u=2)
                        else:
                            dst, src = top[:, s, 0 if b == HP else 3, n, :], ps_s[b % 2][:].rearrange("p (u w) -> p u w", u=4)
                        nc.vector.tensor_reduce(dst, src, AX.X, ALU.max).then_inc(max_done, 1)
                    between(t, s0, u)
                if live(t, 2):
                    i, s = t - 2, (s0 - 2) % SLOTS
                    dve.wait_ge(max_done, BOTH * (i + 1))
                    nc.vector.tensor_tensor(
                        top_bd[:, s, :, 0:16].rearrange("p k (x g) -> p k x g", g=2),
                        top[:, s, :, :, :].rearrange("p k n (h o) -> p k (n h) o", o=1).broadcast_to([P, KB, 8, 2]),
                        c["minus_half_rows"][:].rearrange("p (a b g) -> p a b g", a=1, b=1).broadcast_to([P, KB, 8, 2]), ALU.mult).then_inc(top_bd_done, 1)
            run_steps(dve, body, LAGS)
    return x2_done


E = 12
F = 32
CAP = -(-NB * SEQ * 5 // (E * 4))
HID = E * F // P
GROUP = 512
GROUPS = NB * SEQ // GROUP
GT = GROUP // P
PICKS = 2


def gate_logits(nc, ctx, xres, zT, ps_l, consts_sem, c):

    def sb(name, shape, dt=F32):
        return ctx.enter_context(nc.sbuf_tensor(name, shape, dt))

    def sem(name):
        return ctx.enter_context(nc.semaphore(name))

    stats = sb("g_stats", [P, SLOTS, 6])
    stats_ready = sb("g_stats_ready", [1, 1])
    mv = sb("g_mv", [P, SLOTS, 2])
    vare = sb("g_vare", [P, SLOTS, 1])
    rstd = sb("g_rstd", [P, SLOTS, 1])
    z = sb("g_z", [P, SLOTS, D])
    zt = sb("g_zt", [P, SLOTS, 2, P])
    stats_done, stats_seen, mv_done, vare_done, rstd_done, norm_done, t_done, t_copied, l_done = (
        sem("g_" + n) for n in ("stats_done", "stats_seen", "mv_done", "vare_done", "rstd_done", "norm_done", "t_done", "t_copied", "l_done"))

    with nc.psum_tensor("g_ps0", [P, 512], F32) as ps0, nc.psum_tensor("g_ps1", [P, 512], F32) as ps1, \
            nc.psum_tensor("g_ps2", [P, 512], F32) as ps2, nc.Block() as block:
        ps = [ps0, ps1, ps2]

        @block.gpsimd
        def _(pool):
            pool.wait_ge(consts_sem, c["loaded"])

            def body(t, turn, s0):
                if live(t, 0):
                    pool.wait_ge(mv_done, t + 1)
                    want(pool, norm_done, t - 2)
                    pool.tensor_tensor(vare[:, s0, :], mv[:, s0, 1:2], c["eps"][:], ALU.add).then_inc(vare_done, 1)
                    pool.wait_ge(vare_done, t + 1)
                    pool.tensor_tensor(rstd[:, s0, :], vare[:, s0, :], c["minus_half"][:], ALU.pow).then_inc(rstd_done, 1)
            run_steps(pool, body, 1)

        @block.vector
        def _(dve):
            def body(t, turn, s0):
                if live(t, 0):
                    nc.vector.bn_stats(stats[:, s0, :], xres[:, t, :]).then_inc(stats_done, 1)
                    dve.wait_ge(stats_done, t + 1)
                    nc.vector.tensor_copy(stats_ready[:], stats[0:1, s0, 0:1]).then_inc(stats_seen, 1)
                    nc.vector.bn_aggr(mv[:, s0, :], stats[:, s0, :]).then_inc(mv_done, 1)
                if live(t, 1):
                    i, s = t - 1, (s0 - 1) % SLOTS
                    dve.wait_ge(rstd_done, i + 1)
                    want(dve, t_done, i - 2)
                    nc.vector.tensor_scalar(z[:, s, :], xres[:, i, :], mv[:, s, 0:1], rstd[:, s, :], ALU.subtract, ALU.mult).then_inc(norm_done, 1)
            run_steps(dve, body, 1)

        @block.tensor
        def _(pe):
            pe.wait_ge(consts_sem, c["loaded"])

            def body(t, turn, s0):
                if live(t, 0):
                    pe.wait_ge(norm_done, t + 1)
                    want(pe, t_copied, 2 * (t - 2))
                    for ch in range(2):
                        m = pe.transpose(ps[s0][:, ch * P:(ch + 1) * P], z[:, s0, ch * P:(ch + 1) * P], c["ident"][:])
                    m.then_inc(t_done, 1)
                if live(t, 1):
                    i, s = t - 1, (s0 - 1) % SLOTS
                    pe.wait_ge(t_copied, 2 * (i + 1))
                    for ch in range(2):
                        m = pe.matmul(ps_l[:, i, :], zt[:, s, ch, :], c["gate"][:, ch, :], start=(ch == 0), stop=(ch == 1))
                    m.then_inc(l_done, 1)
            run_steps(pe, body, 1)

        @block.scalar
        def _(act):
            def body(t, turn, s0):
                if live(t, 0):
                    act.wait_ge(t_done, t + 1)
                    want(act, l_done, t - 2)
                    src = ps[s0][:, 0:2 * P].rearrange("p (c t) -> p c t", c=2)
                    nc.scalar.copy(zt[:, s0, :, :], src).then_inc(t_copied, 1)
                    nc.scalar.copy(zT[:, :, t, :], src).then_inc(t_copied, 1)
            run_steps(act, body, 1)


def route(nc, ctx, wT, ps_l, consts_sem, c):

    def sb(name, shape, dt=F32):
        return ctx.enter_context(nc.sbuf_tensor(name, shape, dt))

    def wide(x, n=E):
        return x.rearrange("p (a o) -> p a o", o=1).broadcast_to([P, x.shape[1], n])

    less = sb("r_less", [P, TILES, E])
    prob = sb("r_prob", [P, TILES, E])
    key = sb("r_key", [P, TILES, E])
    eq = sb("r_eq", [P, TILES, E])
    sel = sb("r_sel", [P, PICKS, TILES, E])
    best = sb("r_best", [P, PICKS, TILES])
    low = sb("r_low", [P, 4, TILES])
    eqt = sb("r_total_by_expert", [P, E, PICKS * TILES])
    run = sb("r_run", [P, E, PICKS * TILES])
    pos = sb("r_pos", [P, PICKS * TILES, E])
    w = sb("r_w", [P, TILES, E])
    step_done = ctx.enter_context(nc.semaphore("route_step"))
    less_done = ctx.enter_context(nc.semaphore("less_done"))
    exp_done = ctx.enter_context(nc.semaphore("route_exp"))
    sel_done = ctx.enter_context(nc.semaphore("sel_done"))
    counted = ctx.enter_context(nc.semaphore("counted"))
    w_done = ctx.enter_context(nc.semaphore("w_done"))
    w_turned = ctx.enter_context(nc.semaphore("w_turned"))
    wT_done = ctx.enter_context(nc.semaphore("wT_done"))

    with nc.psum_tensor("r_rank", [P, 512], F32) as ps_rank, nc.psum_tensor("r_total", [P, 512], F32) as ps_total, \
            nc.psum_tensor("r_wT", [P, GROUPS, GROUP], F32) as ps_w, nc.Block() as block:

        @block.vector
        def _(dve):
            steps = [0]

            def then(ins):
                steps[0] += 1
                ins.then_inc(step_done, 1)
                dve.wait_ge(step_done, steps[0])

            v = nc.vector
            dve.wait_ge(consts_sem, c["loaded"])
            lg = ps_l[:]
            then(v.tensor_reduce(low[:, 0, :], lg, AX.X, ALU.max))
            v.tensor_tensor(less[:], lg, wide(low[:, 0, :]), ALU.subtract).then_inc(less_done, 1)
            dve.wait_ge(exp_done, 1)
            then(v.tensor_reduce(low[:, 1, :], prob[:], AX.X, ALU.add))
            then(v.reciprocal(low[:, 2, :], low[:, 1, :]))
            then(v.tensor_tensor(prob[:], prob[:], wide(low[:, 2, :]), ALU.mult))
            for k in range(PICKS):
                then(v.tensor_reduce(best[:, k, :], prob[:], AX.X, ALU.max))
                then(v.tensor_tensor(eq[:], prob[:], wide(best[:, k, :]), ALU.is_equal))
                then(v.tensor_tensor(key[:], eq[:], c["order"][:].rearrange("p (o e) -> p o e", o=1).broadcast_to([P, TILES, E]), ALU.mult))
                then(v.tensor_reduce(low[:, 3, :], key[:], AX.X, ALU.max))
                then(v.tensor_tensor(sel[:, k, :, :], key[:], wide(low[:, 3, :]), ALU.is_equal))
                if k == 0:
                    then(v.scalar_tensor_tensor(out=prob[:], in0=sel[:, 0, :, :], scalar=-2.0, in1=prob[:], op0=ALU.mult, op1=ALU.add))
            then(v.tensor_tensor(low[:, 0, :], best[:, 0, :], best[:, 1, :], ALU.add))
            then(v.reciprocal(low[:, 1, :], low[:, 0, :]))
            last = v.scalar_tensor_tensor(out=best[:], in0=best[:], scalar=0.5,
                                          in1=low[:, 1:2, :].broadcast_to([P, PICKS, TILES]), op0=ALU.mult, op1=ALU.mult)
            then(last)
            v.memset(low[:, 2, :], 0.0).then_inc(sel_done, 1)
            dve.wait_ge(counted, 2)
            total = ps_total[:, 0:PICKS * TILES * E].rearrange("p (j e) -> p e j", e=E)
            then(v.tensor_tensor(eqt[:], total, c["zero"][:].rearrange("p (a b) -> p a b", a=E), ALU.add))
            then(v.tensor_tensor_scan(run[:].rearrange("p e j -> p (e j)"), c["carry"][:], eqt[:].rearrange("p e j -> p (e j)"), 0.0, ALU.mult, ALU.add))
            then(v.tensor_tensor(run[:], run[:], eqt[:], ALU.subtract))
            then(v.tensor_tensor(pos[:], ps_rank[:, 0:PICKS * TILES * E].rearrange("p (j e) -> p j e", e=E), run[:].rearrange("p e j -> p j e"), ALU.add))
            selj = sel[:].rearrange("p k t e -> p (k t) e")
            then(v.scalar_tensor_tensor(out=pos[:], in0=pos[:], scalar=float(CAP), in1=selj, op0=ALU.is_le, op1=ALU.mult))
            then(v.tensor_tensor(pos[:], pos[:], wide(best[:].rearrange("p k t -> p (k t)")), ALU.mult))
            v.tensor_tensor(w[:], pos[:, 0:TILES, :], pos[:, TILES:, :], ALU.add).then_inc(w_done, 1)
            dve.wait_ge(w_turned, 1)
            for g in range(GROUPS):
                m = v.tensor_copy(wT[:, g * GROUP:(g + 1) * GROUP], ps_w[0:E, g, :])
            m.then_inc(wT_done, 1)

        @block.scalar
        def _(act):
            act.wait_ge(less_done, 1)
            nc.scalar.activation(prob[:], less[:], ACT.Exp).then_inc(exp_done, 1)

        @block.tensor
        def _(pe):
            pe.wait_ge(sel_done, 1)
            s = sel[:].rearrange("p k t e -> p (k t e)")
            n = PICKS * TILES * E
            pe.matmul(ps_rank[:, 0:n], c["upto"][:], s, start=True, stop=True).then_inc(counted, 1)
            pe.matmul(ps_total[:, 0:n], c["ones"][:], s, start=True, stop=True).then_inc(counted, 1)
            pe.wait_ge(w_done, 1)
            for t in range(TILES):
                m = pe.transpose(ps_w[0:E, t // GT, (t % GT) * P:(t % GT + 1) * P], w[:, t, :], c["ident"][:])
            m.then_inc(w_turned, 1)


def experts(nc, ctx, io, xres, zT, wT, consts_sem, c):

    def sb(name, shape, dt=F32):
        return ctx.enter_context(nc.sbuf_tensor(name, shape, dt))

    def sem(name):
        return ctx.enter_context(nc.semaphore(name))

    up3 = sb("up3", [P, 2, GROUP])
    prod = sb("prod", [P, 2, GROUP])
    act_h = sb("act_h", [P, 2, GROUP])
    hid = sb("hid", [P, HID, GROUP])
    out = sb("x_out", [P, 2, 2, D])
    up_done, up3_copied, prod_done, silu_done, hid_done, down_done, out_done = (
        sem("e_" + n) for n in ("up_done", "up3_copied", "prod_done", "silu_done", "hid_done", "down_done", "out_done"))
    twice = sem("e_twice")
    stored = [sem(f"stored{i}") for i in range(2)]
    ps_1, ps_3, ps_w, ps_d = ([ctx.enter_context(nc.psum_tensor(f"e_ps{n}{i}", [P, 512], F32)) for i in range(2)] for n in "13wd")
    out_tiles = io["out"].rearrange("(n b) s d -> (b s) n d", b=2)

    with nc.Block() as block:
        @block.sync
        def _(sp):
            def body(g):
                for half in range(2):
                    sp.wait_ge(out_done, GT * g + 2 * half + 2)
                    sp.dma_start(out_tiles[:, bass.ds(GT * g + 2 * half, 2), :], out[:, half, :, :]).then_inc(stored[half], 16)
            body(0)
            with sp.Fori(1, GROUPS) as g:
                body(g)
            for half in range(2):
                sp.wait_ge(stored[half], 16 * GROUPS)

        @block.tensor
        def _(pe):
            pe.wait_ge(consts_sem, c["loaded"])
            def body(g):
                z = [zT[:, ch, bass.ds(GT * g, GT), :].rearrange("p t c -> p (t c)") for ch in range(2)]
                for h in range(HID):
                    cols = slice(h * P, (h + 1) * P)
                    want(pe, hid_done, HID * g + max(h - 1, 0))
                    for ch in range(2):
                        pe.matmul(ps_1[h % 2][:], c["w1"][:, ch, cols], z[ch], start=(ch == 0), stop=(ch == 1))
                    for ch in range(2):
                        pe.matmul(ps_3[h % 2][:], c["w3"][:, ch, cols], z[ch], start=(ch == 0), stop=(ch == 1))
                    pe.matmul(ps_w[h % 2][:], c["expand"][:, cols], wT[:, bass.ds(GROUP * g, GROUP)], start=True, stop=True).then_inc(up_done, 1)
                pe.wait_ge(hid_done, HID * g + HID)
                for t in range(GT):
                    want(pe, out_done, GT * g + max(t - 1, 0))
                    for h in range(HID):
                        m = pe.matmul(ps_d[t % 2][:, 0:D], hid[:, h, t * P:(t + 1) * P], c["w2"][:, h, :], start=(h == 0), stop=(h == HID - 1))
                    m.then_inc(down_done, 1)
            body(0)
            with pe.Fori(1, GROUPS) as g:
                body(g)

        @block.scalar
        def _(act):
            def body(g):
                for h in range(HID):
                    act.wait_ge(up_done, HID * g + h + 1)
                    if h == 2:
                        act.wait_ge(prod_done, HID * g + 1)
                    else:
                        want(act, prod_done, HID * g)
                    nc.scalar.copy(up3[:, h % 2, :], ps_3[h % 2][:]).then_inc(up3_copied, 1)
                    act.wait_ge(prod_done, HID * g + h + 1)
                    nc.scalar.activation(act_h[:, h % 2, :], prod[:, h % 2, :], ACT.Tanh, scale=0.5).then_inc(silu_done, 1)
            body(0)
            with act.Fori(1, GROUPS) as g:
                body(g)

        @block.vector
        def _(dve):
            def body(g):
                for h in range(HID):
                    dve.wait_ge(up3_copied, HID * g + h + 1)
                    nc.vector.tensor_tensor(prod[:, h % 2, :], ps_1[h % 2][:], up3[:, h % 2, :], ALU.mult).then_inc(prod_done, 1)
                    dve.wait_ge(silu_done, HID * g + h + 1)
                    nc.vector.scalar_tensor_tensor(out=act_h[:, h % 2, :], in0=act_h[:, h % 2, :], scalar=1.0, in1=prod[:, h % 2, :],
                                                   op0=ALU.add, op1=ALU.mult).then_inc(twice, 1)
                    dve.wait_ge(twice, HID * g + h + 1)
                    want(dve, down_done, GT * g)
                    nc.vector.tensor_tensor(hid[:, h, :], act_h[:, h % 2, :], ps_w[h % 2][:], ALU.mult).then_inc(hid_done, 1)
                for t in range(GT):
                    dve.wait_ge(down_done, GT * g + t + 1)
                    want(dve, stored[t // 2], 16 * g)
                    nc.vector.tensor_tensor(out[:, t // 2, t % 2, :], ps_d[t % 2][:, 0:D], xres[:, GT * g + t, :], ALU.add).then_inc(out_done, 1)
            body(0)
            with dve.Fori(1, GROUPS) as g:
                body(g)


def program(nc, io, DEBUG=False):
    ctx = ExitStack()
    with ctx:
        def sb(name, shape, dt=F32):
            return ctx.enter_context(nc.sbuf_tensor(name, shape, dt))

        xres = sb("xres", [P, TILES, D])

        def load(names, stage, narrow=()):
            loaded = stage.enter_context(nc.semaphore("consts_" + names[0]))
            c = {n: stage.enter_context(nc.sbuf_tensor(f"{names[0]}_{n}", list(io[n].shape), io[n].dtype)) for n in names}
            c16 = {n: stage.enter_context(nc.sbuf_tensor(f"{n}_16", list(io[n].shape), BF16)) for n in narrow}
            with nc.Block() as block:
                @block.sync
                def _(sp):
                    for n in names:
                        sp.dma_start(c[n][:], io[n]).then_inc(loaded, 16)
                    sp.wait_ge(loaded, 16 * len(names))

                @block.vector
                def _(dve):
                    if narrow:
                        dve.wait_ge(loaded, 16 * len(names))
                    for n in narrow:
                        i = nc.vector.tensor_copy(c16[n][:], c[n][:])
                    if narrow:
                        i.then_inc(loaded, 1)
            c.update(c16)
            c["loaded"] = 16 * len(names) + (1 if narrow else 0)
            return loaded, c

        with ExitStack() as stage:
            loaded, c = load(["ident", "wqk", "wv", "wo", "qkb", "vb", "ob", "cos", "sin", "hmask", "minus_half", "eps"], stage)
            self_attention(nc, stage, io, xres, loaded, c)
        with ExitStack() as stage:
            loaded, c = load(["identb", "w_qk", "w_v", "b_qk", "b_v", "w_out", "b_out", "w_ct", "b_ct", "band_in", "band_0", "band_3",
                              "pick", "den_rows", "ident2", "minus_half_rows", "minus_half", "eps"], stage, ["identb", "band_in", "band_0", "band_3", "pick"])
            ctx_attention(nc, stage, io, xres, loaded, c)
        if DEBUG:
            with nc.Block() as block, nc.semaphore("out_done") as od:
                @block.sync
                def _(sp):
                    sp.dma_start(io["out"].rearrange("(n b) s d -> (b s) n d", b=2), xres[:]).then_inc(od, 16)
                    sp.wait_ge(od, 16)
            return
        with ExitStack() as stage:
            loaded, c = load(["gate", "order", "carry", "zero", "upto", "ones", "expand", "w1", "w3", "w2", "ident", "minus_half", "eps"], stage)
            zT = stage.enter_context(nc.sbuf_tensor("zT_all", [P, 2, TILES, P], F32))
            wT = stage.enter_context(nc.sbuf_tensor("wT", [E, NB * SEQ], F32))
            with nc.psum_tensor("logits", [P, TILES, E], F32) as ps_l:
                gate_logits(nc, stage, xres, zT, ps_l, loaded, c)
                route(nc, stage, wT, ps_l, loaded, c)
            experts(nc, stage, io, xres, zT, wT, loaded, c)


def layout(x):
    f = np.float32

    def cut(w):
        return np.ascontiguousarray(w.reshape(2, P, -1).transpose(1, 0, 2))

    pos = np.arange(SEQ, dtype=f)
    inv = (1.0 / 10000.0 ** (np.arange(0, D1, 2, dtype=f) / f(D1))).astype(f)
    ang = np.tile(pos[:, None] * inv[None, :], (2, 2)).astype(f)
    sin = np.sin(ang)
    sin[:, :D1 // 2] *= -1
    def pair(w):
        out = np.zeros((P, P), f)
        out[:64, :64] = out[64:, 64:] = w
        return out

    w_in, b_in = x["L0_xattn_w_in"], x["L0_xattn_b_in"]
    pq, ph = np.arange(P) % 64, np.arange(P) // 64
    col = np.arange(64)
    prev = np.where(col[None] >= pq[:, None], 0, NEG).astype(f)
    nxt = np.where(col[None] <= pq[:, None], 0, NEG).astype(f)
    w_out = np.zeros((P, 64), f)
    den = np.zeros((P, P), f)
    for h in range(H2):
        w_out[16 * h:16 * h + D2] = x["L0_xattn_w_out"].T[D2 * h:D2 * h + D2]
        den[16 * h + D2, 16 * h:16 * h + 16] = 1
    pick = np.zeros((96, 2 * HP, P), f)
    for j in range(3):
        for r in range(16):
            pick[32 * j + r, r // 2] = ph == r % 2
    b_v = np.tile(b_in[128:].reshape(HP, 2, D2), (2, 1, 1)).transpose(1, 0, 2).reshape(2, 64)
    rows = lambda v: np.ascontiguousarray(np.broadcast_to(v, (P, v.shape[-1])))
    return {
        "x": x["x"],
        "minus_half": np.full((P, 1), -0.5, f),
        "eps": np.full((P, 1), EPS, f),
        "ident": np.eye(P, dtype=f),
        "wqk": cut(np.concatenate([x["L0_attn_q_w"].T, x["L0_attn_k_w"].T], 1)),
        "wv": cut(x["L0_attn_v_w"].T),
        "wo": cut(x["L0_attn_out_w"].T),
        "qkb": rows(np.concatenate([x["L0_attn_q_b"], x["L0_attn_k_b"]])),
        "vb": rows(np.concatenate([x["L0_attn_v_b"]] * 2)),
        "ob": rows(x["L0_attn_out_b"]),
        "cos": np.cos(ang).astype(f),
        "sin": sin.astype(f),
        "ctx": x["ctx_2048"],
        "identb": np.eye(P, dtype=f),
        "w_qk": np.stack([pair(w_in[0:64].T), pair(w_in[64:128].T)], 1),
        "w_v": pair(w_in[128:].T),
        "b_qk": np.stack([np.tile(b_in[0:64], 2), np.tile(b_in[64:128], 2)], 1),
        "b_v": np.ascontiguousarray(np.broadcast_to(b_v, (P, 2, 64))),
        "w_out": w_out,
        "b_out": np.tile(x["L0_xattn_b_out"], 2)[:, None],
        "w_ct": pair(x["L0_xattn_w_ct"]),
        "b_ct": np.tile(x["L0_xattn_b_ct"], 2)[:, None],
        "band_in": np.concatenate([prev, nxt, prev, nxt], 1),
        "band_0": np.tile(nxt, (1, 4)),
        "band_3": np.tile(prev, (1, 4)),
        "pick": pick,
        "den_rows": den,
        "ident2": (pq[:, None] == col[None]).astype(f),
        "minus_half_rows": -(ph[:, None] == np.arange(2)[None]).astype(f),
        "gate": cut(x["L0_ffn_gate_w"].T),
        "order": rows(np.arange(E, 0, -1).astype(f)),
        "carry": rows((np.arange(E * PICKS * TILES) % (PICKS * TILES) > 0).astype(f)),
        "zero": np.zeros((P, E * PICKS * TILES), f),
        "upto": np.triu(np.ones((P, P), f)),
        "ones": np.ones((P, P), f),
        "expand": (np.arange(E)[:, None] == np.arange(E * F)[None] // F).astype(f),
        "w1": cut(x["L0_ffn_w1"].reshape(E * F, D).T),
        "w3": cut(x["L0_ffn_w3"].reshape(E * F, D).T),
        "w2": np.ascontiguousarray(x["L0_ffn_w2"].transpose(0, 2, 1).reshape(HID, P, D).transpose(1, 0, 2)),
        "hmask": (np.arange(P)[:, None] // D1 == np.arange(HC)[None]).astype(f),
    }


def kernel(**inputs):
    import concourse.bacc as bacc
    from concourse.bass_utils import run_bass_kernel_spmd

    nc = bacc.Bacc("TRN2", target_bir_lowering=False, num_devices=1)
    arrays = layout({k: np.asarray(v) for k, v in inputs.items()})
    io = {k: nc.dram_tensor("in_" + k, a.shape, mybir.dt.from_np(a.dtype), kind="ExternalInput").ap() for k, a in arrays.items()}
    io["out"] = nc.dram_tensor("out", (NB, SEQ, D), F32, kind="ExternalOutput").ap()
    program(nc, io)
    got = run_bass_kernel_spmd(nc, [{"in_" + k: a for k, a in arrays.items()}], core_ids=[0])
    return got.results[0]["out"]
```

```python
from contextlib import ExitStack

import numpy as np

import concourse.bass as bass
from concourse import mybir

ALU = mybir.AluOpType
ACT = mybir.ActivationFunctionType
F32 = mybir.dt.float32
BF16 = mybir.dt.bfloat16
AX = mybir.AxisListType

P = 128
D = 256
SEQ = 64
NB = 32
TILES = NB * SEQ // P
EPS = 1e-5

H1 = 16
D1 = D // H1
HC = H1 // 2

SLOTS = 3


def want(eng, sem, n):
    if isinstance(n, int) and n <= 0:
        return
    eng.wait_ge(sem, n)


def want_alone(eng, sem, n, passed):
    if isinstance(n, int) and n <= 0:
        return
    eng.wait_ge(sem, n)
    eng.sem_inc(passed, 1)


def run_steps(eng, body, lags, head=2, first=0):
    last = TILES // SLOTS
    for t in range(first, SLOTS * head):
        body(t, t // SLOTS, t % SLOTS)
    with eng.Fori(head, last) as turn:
        for slot in range(SLOTS):
            body(turn * SLOTS + slot, turn, slot)
    for t in range(last * SLOTS, TILES + lags):
        body(t, t // SLOTS, t % SLOTS)


def live(t, lag):
    return not isinstance(t, int) or 0 <= t - lag < TILES


def self_attention(nc, ctx, io, xres, c, loaded, ps_qk, ps_zT, ps_s, ahead):

    def sb(name, shape, dt=F32):
        return ctx.enter_context(nc.sbuf_tensor(name, shape, dt))

    def sem(name):
        return ctx.enter_context(nc.semaphore(name))

    c.update({n: sb("c_" + n, list(io[n].shape), io[n].dtype) for group in OWN_CONSTS for n in CONSTS[group]})
    stats = sb("stats", [P, SLOTS, 6])
    stats_ready = sb("a_stats_ready", [1, 1])
    mv = sb("mv", [P, SLOTS, 2])
    vare = sb("vare", [P, SLOTS, 1])
    rstd = sb("rstd", [P, SLOTS, 1])
    z = sb("z", [P, SLOTS, D])
    zT = sb("zT", [P, 2, P])
    qk = sb("qk", [P, 2 * D])
    qk_cos = sb("qk_cos", [P, 2 * D])
    qk_rot = sb("qk_rot", [P, 2 * D])
    qk_rope = sb("qk_rope", [P, 2 * D])
    qkT = sb("qkT", [P, SLOTS, 4, P])
    kTm = sb("kTm", [P, SLOTS, 2, HC, P])
    v_bd = sb("v_bd", [P, SLOTS, 2, HC, 2, D1 + 1])
    top = sb("top", [P, SLOTS, H1])
    prob = sb("prob", [P, SLOTS, H1, SEQ])
    probT = sb("probT", [P, HC, P])
    rden = sb("rden", [P, H1])
    att = sb("att", [P, H1, D1])
    attT = sb("attT", [P, 2, P])

    ps_z = ps_zT[:, 0:2 * P].rearrange("p (c t) -> p c t", c=2)
    ps_v = ctx.enter_context(nc.psum_tensor("ps_v", [P, 512], F32))
    ps_pT = ctx.enter_context(nc.psum_tensor("ps_pT", [P, 2, 512], F32))
    ps_o = ctx.enter_context(nc.psum_tensor("ps_o", [P, 512], F32))

    x_loaded = [sem(f"a_x_loaded{i}") for i in range(SLOTS)]
    cleared = sem("a_cleared")
    stats_done = sem("a_stats")
    stats_seen = sem("a_stats_seen")
    mv_done = sem("a_mean_var")
    vare_done = sem("a_vare")
    rstd_done = sem("a_rstd")
    norm_done = sem("a_norm")
    xb_done = sem("a_xb")
    zT_done = sem("a_zT")
    zT_copied = sem("a_zT_copied")
    qk_done = sem("a_qk")
    v_done = sem("a_v")
    qk_biased = sem("a_qk_biased")
    v_copied = sem("a_v_copied")
    cos_done = sem("a_cos")
    rot_done = sem("a_rot")
    rope_done = sem("a_rope")
    qkT_done = sem("a_qkT")
    qkT_copied = sem("a_qkT_copied")
    masked = sem("a_masked")
    s_done = sem("a_s")
    top_done = sem("a_top")
    sub_done = sem("a_sub")
    exp_done = sem("a_exp")
    pT_done = sem("a_pT")
    pT_copied = sem("a_pT_copied")
    o_done = sem("a_o")
    rden_done = sem("a_rden")
    att_done = sem("a_att")
    attT_done = sem("a_attT")
    attT_copied = sem("a_attT_copied")
    y_done = sem("a_y")
    x1_done = sem("a_x1")

    x_tiles = io["x"].rearrange("(n b) s d -> n (b s) d", b=2)
    block = nc.Block()
    ctx.enter_context(block)

    LAGS = 5
    LEAD = TILES
    LEADS = (LEAD, LEAD + 1, LEAD + 3)

    @block.sync
    def _(sp):
        def body(t, turn, s0):
            if live(t, 0):
                want(sp, norm_done, t - 2)
                sp.dma_start(xres[:, t, :], x_tiles[t]).then_inc(x_loaded[s0], 16)
            if isinstance(t, int) and t < SLOTS:
                for g in ((0, 1), (2,), (3,))[t]:
                    for n in CONSTS[g]:
                        sp.dma_start(c[n][:], io[n]).then_inc(loaded[g], 16)
        run_steps(sp, body, LAGS)
        sp.wait_ge(loaded[3], 16 * len(CONSTS[3]))
        for t in range(AHEAD_STEPS):
            ahead("sync", sp, t)

    @block.gpsimd
    def _(pool):
        pool.memset(v_bd[:], 0.0).then_inc(cleared, 1)
        pool.wait_ge(cleared, 1)
        pool.memset(v_bd[0:64, :, :, :, 0, D1], 1.0).then_inc(cleared, 1)
        pool.memset(v_bd[64:128, :, :, :, 1, D1], 1.0).then_inc(cleared, 1)
        pool.wait_ge(cleared, 3)
        pool.wait_ge(loaded[0], 16 * len(CONSTS[0]))

        def body(t, turn, s0):
            if isinstance(t, int) and t == LEAD:
                ahead("gpsimd", pool, 0)
            if live(t, 0):
                pool.wait_ge(mv_done, t + 1)
                want(pool, norm_done, t - 2)
                pool.tensor_tensor(vare[:, s0, :], mv[:, s0, 1:2], c["eps"][:], ALU.add).then_inc(vare_done, 1)
                pool.wait_ge(vare_done, t + 1)
                pool.tensor_tensor(rstd[:, s0, :], vare[:, s0, :], c["minus_half"][:], ALU.pow).then_inc(rstd_done, 1)
            if live(t, 2):
                i, s = t - 2, (s0 - 2) % SLOTS
                pool.wait_ge(qkT_copied, i + 1)
                want(pool, s_done, i - 2)
                for ch in range(2):
                    m = pool.tensor_tensor(
                        kTm[:, s, ch, :, :],
                        qkT[:, s, 2 + ch:3 + ch, :].broadcast_to([P, HC, P]),
                        c["hmask"][:].rearrange("p (h o) -> p h o", o=1).broadcast_to([P, HC, P]), ALU.mult)
                m.then_inc(masked, 1)
            if live(t, 1):
                i, s = t - 1, (s0 - 1) % SLOTS
                if isinstance(t, int) and t == 1:
                    pool.wait_ge(loaded[1], 16 * len(CONSTS[1]))
                pool.wait_ge(qk_biased, i + 1)
                want(pool, rope_done, i)
                pool.tensor_tensor(
                    qk_cos[:, :].rearrange("p (h d) -> p h d", d=D1), qk[:, :].rearrange("p (h d) -> p h d", d=D1),
                    c["cos"][:].rearrange("p (o d) -> p o d", o=1).broadcast_to([P, 2 * H1, D1]), ALU.mult).then_inc(cos_done, 1)
            if live(t, 0):
                if isinstance(t, int) and t == 0:
                    pool.wait_ge(loaded[2], 16 * len(CONSTS[2]))
                pool.wait_ge(norm_done, t + 1)
                pool.tensor_tensor(xres[:, t, :], xres[:, t, :], c["ob"][:], ALU.add).then_inc(xb_done, 1)
            if isinstance(t, int) and t == SLOTS:
                ahead("gpsimd", pool, PREPARE)
            if isinstance(t, int) and t in LEADS[1:]:
                ahead("gpsimd", pool, LEADS.index(t))
        run_steps(pool, body, LAGS)

    @block.tensor
    def _(pe):
        pe.wait_ge(loaded[0], 16 * len(CONSTS[0]))

        def body(t, turn, s0):
            if live(t, 4):
                i, s = t - 4, (s0 - 4) % SLOTS
                pe.wait_ge(exp_done, i + 1)
                want(pe, pT_copied, 2 * i)
                for hh in range(HC):
                    m = pe.transpose(ps_pT[:, hh // 4, (hh % 4) * P:(hh % 4 + 1) * P],
                                     prob[:, s, 2 * hh:2 * hh + 2, :].rearrange("p h k -> p (h k)"), c["ident"][:])
                    if hh % 4 == 3:
                        m.then_inc(pT_done, 1)
            if live(t, 1):
                i, s = t - 1, (s0 - 1) % SLOTS
                pe.wait_ge(norm_done, i + 1)
                want(pe, zT_copied, i)
                for ch in range(2):
                    m = pe.transpose(ps_z[:, ch, :], z[:, s, ch * P:(ch + 1) * P], c["ident"][:])
                m.then_inc(zT_done, 1)
            if live(t, 5):
                i, s = t - 5, (s0 - 5) % SLOTS
                pe.wait_ge(att_done, i + 1)
                for ch in range(2):
                    m = pe.transpose(ps_o[:, ch * P:(ch + 1) * P], att[:, ch * 8:ch * 8 + 8, :].rearrange("p h d -> p (h d)"), c["ident"][:])
                m.then_inc(attT_done, 1)
            if live(t, 2):
                i, s = t - 2, (s0 - 2) % SLOTS
                pe.wait_ge(rope_done, i + 1)
                for j in range(4):
                    m = pe.transpose(ps_qk[:, j * P:(j + 1) * P], qk_rope[:, j * P:(j + 1) * P], c["ident"][:])
                m.then_inc(qkT_done, 1)
            if live(t, 3):
                i, s = t - 3, (s0 - 3) % SLOTS
                pe.wait_ge(masked, i + 1)
                want(pe, sub_done, i)
                for ch in range(2):
                    for b in range(2):
                        m = pe.matmul(ps_s[64 * b:64 * b + 64, ch, :].rearrange("p (h k) -> p h k", k=SEQ),
                                      qkT[:, s, ch, 64 * b:64 * b + 64], kTm[:, s, ch, :, 64 * b:64 * b + 64],
                                      start=True, stop=True)
                m.then_inc(s_done, 1)
            if live(t, 5):
                i, s = t - 5, (s0 - 5) % SLOTS
                pe.wait_ge(attT_copied, i + 1)
                if live(t, 2):
                    pe.wait_ge(v_copied, t - 1)
                else:
                    want(pe, x1_done, i)
                for ch in range(2):
                    m = pe.matmul(ps_v[:, 0:D], attT[:, ch, :], c["wo"][:, ch, :], start=(ch == 0), stop=(ch == 1))
                m.then_inc(y_done, 1)
            if live(t, 1):
                i, s = t - 1, (s0 - 1) % SLOTS
                if isinstance(t, int) and t == 1:
                    pe.wait_ge(loaded[1], 16 * len(CONSTS[1]))
                pe.wait_ge(zT_copied, i + 1)
                want(pe, qkT_copied, i)
                for ch in range(2):
                    m = pe.matmul(ps_qk[:], zT[:, ch, :], c["wqk"][:, ch, :], start=(ch == 0), stop=(ch == 1))
                m.then_inc(qk_done, 1)
            if live(t, 4):
                i, s = t - 4, (s0 - 4) % SLOTS
                pe.wait_ge(pT_copied, 2 * (i + 1))
                pe.wait_ge(v_copied, i + 1)
                want(pe, attT_copied, i)
                for hh in range(HC):
                    for b in range(2):
                        m = pe.matmul(ps_o[64 * b:64 * b + 64, hh * 34:hh * 34 + 34],
                                      probT[:, hh, 64 * b:64 * b + 64],
                                      v_bd[:, s, b, hh, :, :].rearrange("p g d -> p (g d)"),
                                      start=True, stop=True)
                m.then_inc(o_done, 1)
            if live(t, 1):
                i, s = t - 1, (s0 - 1) % SLOTS
                if isinstance(t, int) and t == 1:
                    pe.wait_ge(loaded[2], 16 * len(CONSTS[2]))
                want(pe, v_copied, i)
                want(pe, x1_done, t - 4)
                for ch in range(2):
                    m = pe.matmul(ps_v[:, 0:D], zT[:, ch, :], c["wv"][:, ch, :], start=(ch == 0), stop=(ch == 1))
                m.then_inc(v_done, 1)
            if isinstance(t, int) and t in LEADS:
                if t == LEAD + 1:
                    pe.wait_ge(qkT_copied, TILES)
                    pe.wait_ge(zT_copied, TILES)
                if t == LEADS[-1]:
                    pe.wait_ge(sub_done, TILES)
                ahead("tensor", pe, LEADS.index(t))
        run_steps(pe, body, LAGS)

    @block.scalar
    def _(act):
        def body(t, turn, s0):
            if live(t, 1):
                i, s = t - 1, (s0 - 1) % SLOTS
                act.wait_ge(zT_done, i + 1)
                want(act, v_done, i)
                nc.scalar.copy(zT[:, :, :].rearrange("p c t -> p (c t)"), ps_zT[:, 0:2 * P]).then_inc(zT_copied, 1)
            if live(t, 5):
                i, s = t - 5, (s0 - 5) % SLOTS
                act.wait_ge(attT_done, i + 1)
                want(act, y_done, i)
                nc.scalar.copy(attT[:, :, :].rearrange("p c t -> p (c t)"), ps_o[:, 0:2 * P]).then_inc(attT_copied, 1)
            if live(t, 2):
                i, s = t - 2, (s0 - 2) % SLOTS
                act.wait_ge(qkT_done, i + 1)
                want(act, s_done, i - 2)
                nc.scalar.copy(qkT[:, s, :, :].rearrange("p c t -> p (c t)"), ps_qk[:]).then_inc(qkT_copied, 1)
            if live(t, 4):
                i, s = t - 4, (s0 - 4) % SLOTS
                want(act, o_done, i)
                for half in range(2):
                    act.wait_ge(pT_done, 2 * i + half + 1)
                    nc.scalar.copy(probT[:, 4 * half:4 * half + 4, :].rearrange("p h t -> p (h t)"), ps_pT[:, half, :]).then_inc(pT_copied, 1)
            if live(t, 3):
                i, s = t - 3, (s0 - 3) % SLOTS
                act.wait_ge(sub_done, i + 1)
                pr = prob[:, s, :, :].rearrange("p h k -> p (h k)")
                nc.scalar.activation(pr, pr, ACT.Exp, scale=float(D1) ** -0.5).then_inc(exp_done, 1)
            if isinstance(t, int) and t in LEADS:
                ahead("scalar", act, LEADS.index(t))
        run_steps(act, body, LAGS)

    @block.vector
    def _(dve):
        dve.wait_ge(cleared, 3)

        def body(t, turn, s0):
            if live(t, 2):
                i, s = t - 2, (s0 - 2) % SLOTS
                if isinstance(t, int) and t == 2:
                    dve.wait_ge(loaded[2], 16 * len(CONSTS[2]))
                dve.wait_ge(v_done, i + 1)
                want(dve, o_done, i - 2)
                for g in range(2):
                    for b in range(2):
                        rows = slice(64 * g, 64 * g + 64)
                        m = nc.vector.tensor_tensor(
                            v_bd[rows, s, b, :, g, 0:D1],
                            ps_v[64 * b:64 * b + 64, 0:D].rearrange("p (h g d) -> p h g d", g=2, d=D1)[:, :, g, :],
                            c["vb"][rows, :].rearrange("p (h g d) -> p h g d", g=2, d=D1)[:, :, g, :], ALU.add)
                m.then_inc(v_copied, 1)
            if live(t, 0):
                dve.wait_ge(x_loaded[s0], 16 * (turn + 1))
                nc.vector.bn_stats(stats[:, s0, :], xres[:, t, :]).then_inc(stats_done, 1)
                dve.wait_ge(stats_done, t + 1)
                nc.vector.tensor_copy(stats_ready[:], stats[0:1, s0, 0:1]).then_inc(stats_seen, 1)
                nc.vector.bn_aggr(mv[:, s0, :], stats[:, s0, :]).then_inc(mv_done, 1)
            if isinstance(t, int) and t in (LEAD, LEAD + 2, LEAD + 4):
                dve.wait_ge(x1_done, AHEAD_STEPS)
                ahead("vector", dve, (t - LEAD) // 2)
            if live(t, 3):
                i, s = t - 3, (s0 - 3) % SLOTS
                dve.wait_ge(s_done, i + 1)
                sc = ps_s[:].rearrange("p c (h k) -> p (c h) k", k=SEQ)
                nc.vector.tensor_reduce(top[:, s, :], sc, AX.X, ALU.max).then_inc(top_done, 1)
                dve.wait_ge(top_done, i + 1)
                want(dve, pT_done, 2 * (i - 2))
                nc.vector.tensor_tensor(prob[:, s, :, :], sc, top[:, s, :].rearrange("p (h o) -> p h o", o=1).broadcast_to([P, H1, SEQ]),
                                        ALU.subtract).then_inc(sub_done, 1)
            if live(t, 5):
                i = t - 5
                dve.wait_ge(y_done, i + 1)
                dve.wait_ge(xb_done, i + 1)
                nc.vector.tensor_tensor(xres[:, i, :], ps_v[:, 0:D], xres[:, i, :], ALU.add).then_inc(x1_done, 1)
            if live(t, 0):
                dve.wait_ge(rstd_done, t + 1)
                want(dve, zT_done, t - 2)
                nc.vector.tensor_scalar(z[:, s0, :], xres[:, t, :], mv[:, s0, 0:1], rstd[:, s0, :], ALU.subtract, ALU.mult).then_inc(norm_done, 1)
            if live(t, 1):
                i, s = t - 1, (s0 - 1) % SLOTS
                if isinstance(t, int) and t == 1:
                    dve.wait_ge(loaded[1], 16 * len(CONSTS[1]))
                dve.wait_ge(qk_done, i + 1)
                want(dve, cos_done, i)
                want(dve, rope_done, i)
                want(dve, rot_done, 2 * i)
                nc.vector.tensor_tensor(qk[:, :], ps_qk[:], c["qkb"][:], ALU.add).then_inc(qk_biased, 1)
                dve.wait_ge(qk_biased, i + 1)
                q4 = qk[:, :].rearrange("p (h two d) -> p h two d", two=2, d=D1 // 2)
                r4 = qk_rot[:, :].rearrange("p (h two d) -> p h two d", two=2, d=D1 // 2)
                for half in range(2):
                    nc.vector.tensor_tensor(
                        r4[:, :, half, :], q4[:, :, 1 - half, :],
                        c["sin"][:, half * 8:half * 8 + 8].rearrange("p (o d) -> p o d", o=1).broadcast_to([P, 2 * H1, D1 // 2]),
                        ALU.mult).then_inc(rot_done, 1)
            if live(t, 4):
                i, s = t - 4, (s0 - 4) % SLOTS
                dve.wait_ge(o_done, i + 1)
                o = ps_o[:, 0:H1 * (D1 + 1)].rearrange("p (h d) -> p h d", d=D1 + 1)
                nc.vector.reciprocal(rden[:, :], o[:, :, D1]).then_inc(rden_done, 1)
                dve.wait_ge(rden_done, i + 1)
                want(dve, attT_done, i)
                nc.vector.tensor_tensor(att[:, :, :], o[:, :, 0:D1],
                                        rden[:, :].rearrange("p (h o) -> p h o", o=1).broadcast_to([P, H1, D1]), ALU.mult).then_inc(att_done, 1)
            if live(t, 1):
                i = t - 1
                dve.wait_ge(rot_done, 2 * (i + 1))
                dve.wait_ge(cos_done, i + 1)
                want(dve, qkT_done, i)
                nc.vector.tensor_tensor(qk_rope[:, :], qk_cos[:, :], qk_rot[:, :], ALU.add).then_inc(rope_done, 1)
        run_steps(dve, body, LAGS)


AHEAD_STEPS = 3
PREPARE = -1

H2 = 8
D2 = SEQ // H2
HP = H2 // 2
TERMS = 6
ROWS = TERMS * D2
NEG = -1e30
MAXIMA = 64
THIRD = 96
WAY = (0, 1, 2, 0)
ORDER = ((0, 0, 0, 1, 1, 2), (0, 1, 2, 0, 1, 0))
KB = D // 64
W_IN = 192


def ctx_attention(nc, ctx, io, xres, zT, logits, c, loaded, before, after):

    def sb(name, shape, dt=F32):
        return ctx.enter_context(nc.sbuf_tensor(name, shape, dt))

    def sem(name):
        return ctx.enter_context(nc.semaphore(name))

    def bank(name):
        return ctx.enter_context(nc.psum_tensor(name, [P, 512], F32))

    stats = sb("b_stats", [P, SLOTS, 6])
    mv = sb("b_mv", [P, SLOTS, 2])
    vare = sb("b_vare", [P, SLOTS, 1])
    rstd = sb("b_rstd", [P, SLOTS, 1])
    z = sb("b_z", [P, SLOTS, D])
    split = sb("split", [P, SLOTS, 2, 3, D], BF16)
    rest = sb("rest", [P, SLOTS, 2, D])
    stack = [sb(f"stack{i}", [P, SLOTS, 2, HP, D], BF16) for i in range(2)]
    v_bd = sb("b_v_bd", [P, SLOTS, 2, HP, KB, 32])
    stats_ready = sb("stats_ready", [1, 1])
    shift = sb("shift", [P, SLOTS, 3, D], BF16)
    scratch = nc.dram_tensor("qk_terms", [SLOTS, 2, 16, TERMS, D2, D], BF16, kind="Internal").ap()

    top = sb("b_top", [P, SLOTS, KB, 2, HP])
    top_bd = sb("top_bd", [P, SLOTS, KB, 32])

    ps_a = bank("b_ps_a")
    ps_b = bank("b_ps_b")
    by_query = ctx.enter_context(nc.psum_tensor("b_ps_s", [P, 2, 512], F32))
    ps_s = [by_query[:, i, :] for i in range(2)]

    cleared = sem("b_cleared")
    stats_done = sem("b_stats_done")
    stats_seen = sem("b_stats_seen")
    mv_done = sem("b_mv_done")
    vare_done = sem("b_vare_done")
    rstd_done = sem("b_rstd_done")
    norm_done = sem("b_norm_done")
    qk_done = sem("b_qk_done")
    v_done = sem("b_v_done")
    part0_done = sem("part0_done")
    rest_done = sem("rest_done")
    part1_done = sem("part1_done")
    part2_done = sem("part2_done")
    v_copied = sem("b_v_copied")
    written = [sem(f"written{i}") for i in range(SLOTS)]
    stacked = [sem(f"stacked{i}") for i in range(SLOTS)]
    enc_loaded = [sem(f"enc_loaded{i}") for i in range(SLOTS)]
    s_done = sem("b_s_done")
    max_done = sem("b_max_done")
    top_bd_done = sem("top_bd_done")
    shift_ps = sem("shift_ps")
    shift0 = sem("shift0")
    shift_r = sem("shift_r")
    shift1 = sem("shift1")
    shift2 = sem("shift2")
    band_set = sem("band_set")
    narrowed = sem("narrowed")
    t_done = sem("b_t_done")
    exp_done = sem("b_exp_done")
    o_done = sem("b_o_done")
    oT_copied = sem("oT_copied")
    den_done = sem("den_done")
    rden_done = sem("b_rden_done")
    on_done = sem("on_done")
    y_done = sem("b_y_done")
    yr_done = sem("yr_done")
    gated_done = sem("gated_done")
    passed = sem("sp_passed")
    f_done = sem("f_done")
    x2_done = sem("x2_done")
    x2_seen = sem("x2_seen")
    stats3_done = sem("g_stats_done")
    stats3_seen = sem("g_stats_seen")
    mv3_done = sem("g_mv_done")
    vare3_done = sem("g_vare_done")
    rstd3_done = sem("g_rstd_done")
    norm3_done = sem("g_norm_done")
    zT3_done = sem("g_zT_done")
    zT3_copied = sem("g_zT_copied")
    logits_done = sem("logits_done")
    logits_copied = sem("logits_copied")

    def units(b):
        if b < HP:
            return [(b, kb, (kb - 1) * W_IN, (kb - 1) * 64, W_IN) for kb in (1, 2)]
        kb = 0 if b == HP else 3
        return [(hp, kb, hp * 128, 0 if kb == 0 else 128, 128) for hp in range(HP)]

    BANKS = HP + 2
    cols = [2 * W_IN] * HP + [512, 512]
    start = [sum(cols[:b]) for b in range(BANKS)]

    def masked_out(ps, b):
        if b < HP:
            return ps[:, 0:2 * W_IN].rearrange("p (u s c) -> p u s c", u=2, s=3)[:, :, 0:3:2, :]
        half = 1 if b == HP else 0
        return ps[:, :].rearrange("p (u s c) -> p u s c", u=4, s=2)[:, :, half, :]

    def mask_of(b):
        if b < HP:
            return c["band_in_16"][:].rearrange("p (u s c) -> p u s c", u=2, s=2)
        return (c["band_0_16"] if b == HP else c["band_3_16"])[:].rearrange("p (u c) -> p u c", u=4)

    n_tiles = io["ctx"].rearrange("(n b) s d -> n (b s) d", b=2)

    def threefold(x):
        return x.rearrange("p (o t) -> p o t", o=1).broadcast_to([x.shape[0], 3, D])

    def tile_turn(turn, s0, lag):
        return turn + (s0 - lag) // SLOTS

    LAGS = 6
    LATE = 5
    BOTH = 2 * BANKS

    def by_key(t, u):
        lag, e = (3, u - LATE) if u >= LATE else (4, u - LATE + BOTH)
        return lag, e // BANKS, e % BANKS

    def early_up(t, u, made=True):
        for k, (up_at, then_at) in enumerate(EARLY_UPS):
            if isinstance(t, int) and (t, u) == (up_at if made else then_at):
                return k
        return None

    def early_banks(k):
        return ps_t if k >= EARLY_SINGLE and k % 2 else ps_s

    def sync_steps(sp):
        def body(t, turn, s0):
            if live(t, 3):
                i, s = t - 3, (s0 - 3) % SLOTS
                want_alone(sp, gated_done, i - 2, passed)
                sp.dma_start(enc[:, s, :], n_tiles[i]).then_inc(enc_loaded[s], 16)
            if live(t, 1):
                i, s = t - 1, (s0 - 1) % SLOTS
                own = tile_turn(turn, s0, 1)
                want_alone(sp, stacked[s], 64 * own, passed)
                for j, done, n in ((0, part0_done, 2 * (i + 1)), (1, part1_done, i + 1), (2, part2_done, i + 1)):
                    want_alone(sp, done, n, passed)
                    for qk, order in enumerate(ORDER):
                        for term in range(TERMS):
                            if order[term] == j:
                                sp.dma_start(scratch[s, qk, :, term, :, :], split[:, s, qk, j, :]).then_inc(written[s], 16)
                want_alone(sp, written[s], 2 * TERMS * 16 * (own + 1), passed)
                want_alone(sp, t_done, BOTH * (i - 2), passed)
                for qk in range(2):
                    for g in range(2):
                        sp.dma_start(stack[qk][64 * g:64 * g + ROWS, s, :, :, :].rearrange("r n h t -> r (n h) t"),
                                     scratch[s, qk].rearrange("(x g) m d t -> g (m d) x t", g=2)[g]).then_inc(stacked[s], 16)
        return body

    def gpsimd_steps(pool):
        def early_silus(t, banks):
            for u in banks:
                k = early_up(t, u, made=False)
                if k is not None:
                    ups.silu(pool, k)

        def body(t, turn, s0):
            if live(t, 1):
                i, s = t - 1, (s0 - 1) % SLOTS
                pool.wait_ge(part1_done, i + 1)
                want(pool, written[s], 2 * TERMS * 16 * tile_turn(turn, s0, 1))
                pool.tensor_tensor(split[:, s, :, 2, :], rest[:, s, :, :], split[:, s, :, 1, :], ALU.subtract).then_inc(part2_done, 1)
            if live(t, 5):
                i, s = t - 5, (s0 - 5) % SLOTS
                pool.wait_ge(yr_done, i + 1)
                pool.wait_ge(enc_loaded[s], 16 * (tile_turn(turn, s0, 5) + 1))
                want(pool, f_done, i)
                pool.tensor_tensor(gated[:], yr[:], enc[:, s, :], ALU.mult).then_inc(gated_done, 1)
            if live(t, 6):
                i, s = t - 6, (s0 - 6) % SLOTS
                pool.wait_ge(mv3_done, i + 1)
                want(pool, norm3_done, i - 2)
                pool.tensor_tensor(vare3[:, s, :], mv3[:, s, 1:2], c["eps"][:], ALU.add).then_inc(vare3_done, 1)
                pool.wait_ge(vare3_done, i + 1)
                pool.tensor_tensor(rstd3[:, s, :], vare3[:, s, :], c["minus_half"][:], ALU.pow).then_inc(rstd3_done, 1)
            if live(t, 0):
                pool.wait_ge(mv_done, t + 1)
                want(pool, norm_done, t - 2)
                pool.tensor_tensor(vare[:, s0, :], mv[:, s0, 1:2], c["eps"][:], ALU.add).then_inc(vare_done, 1)
                pool.wait_ge(vare_done, t + 1)
                pool.tensor_tensor(rstd[:, s0, :], vare[:, s0, :], c["minus_half"][:], ALU.pow).then_inc(rstd_done, 1)
            early_silus(t, range(8))
            if live(t, 4):
                i = t - 4
                for n in range(2):
                    pool.wait_ge(rden_done, 4 * i + 2 * n + 2)
                    want(pool, y_done, 2 * i + n - 1)
                    pool.tensor_tensor(on[:, n, :], oT[:, n, :], rden[:, n, :], ALU.mult).then_inc(on_done, 1)
            early_silus(t, range(8, BOTH))
        return body

    def tensor_steps(pe):
        def scores(n, b, s, ps, left, right):
            for hp, kb, col, tok, w in units(b):
                for g in range(2):
                    r = slice(64 * g, 64 * g + ROWS)
                    m = pe.matmul(ps[64 * g:64 * g + 64, col:col + w], left[r, s, n, hp, 64 * kb:64 * kb + 64],
                                  right[r, s, n, hp, tok:tok + w], start=False, stop=False, skip_group_check=True)
            return m

        def weighted(i, s, n):
            if n == 0:
                pe.wait_ge(v_copied, i + 1)
            pe.wait_ge(exp_done, BOTH * i + BANKS * (n + 1))
            want(pe, oT_copied, 2 * i + n)
            for kb in (1, 3, 0, 2):
                for hp in range(HP):
                    b = hp if kb in (1, 2) else HP + (kb == 3)
                    _, _, col, tok, w = [u for u in units(b) if u[0] == hp and u[1] == kb][0]
                    m = pe.matmul(ps_o[32 * hp:32 * hp + 32, tok:tok + w], v_bd[:, s, n, hp, kb, :],
                                  prob[:, n, start[b] + col:start[b] + col + w],
                                  start=(kb == 1), stop=(kb == 2), skip_group_check=True)
            m.then_inc(o_done, 1)

        def between(t, s0, u):
            if u == 0 and live(t, 3):
                i, s = t - 3, (s0 - 3) % SLOTS
                pe.wait_ge(top_bd_done, i + 1)
                want(pe, rden_done, 4 * (i - 1))
                for qb in range(KB):
                    for j in (2, 3):
                        m = pe.matmul(ps_c[32 * j:32 * j + 32, 64 * qb:64 * qb + 64], top_bd[:, s, qb, :], c["ident2"][:],
                                      start=True, stop=True)
                m.then_inc(shift_ps, 1)
            if u == 6 and live(t, 5):
                i = t - 5
                pe.wait_ge(gated_done, i + 1)
                pe.matmul(ps_b[:, 0:D], c["w_ct"][:], gated[:], start=True, stop=True).then_inc(f_done, 1)
            if u == 6 and live(t, 4):
                weighted(t - 4, (s0 - 4) % SLOTS, 1)
            if u == 8 and live(t, 1):
                i, s = t - 1, (s0 - 1) % SLOTS
                want(pe, x2_done, t - 4)
                for pair in range(2):
                    m = pe.matmul(ps_b[:, pair * P:(pair + 1) * P], z[:, s, pair * P:(pair + 1) * P], c["w_v"][:], start=True, stop=True)
                m.then_inc(v_done, 1)
            if u == 7 and live(t, 4):
                i = t - 4
                pe.wait_ge(oT_copied, 2 * i + 2)
                if live(t, 3):
                    pe.wait_ge(shift_r, i + 2)
                pe.matmul(ps_c[:], c["den_rows"][:], oT[:].rearrange("p n t -> p (n t)"), start=True, stop=True).then_inc(den_done, 1)
            if u == 2 and live(t, 5):
                i = t - 5
                if live(t, 2):
                    pe.wait_ge(v_copied, t - 1)
                else:
                    want(pe, x2_done, i)
                for n in range(2):
                    pe.wait_ge(on_done, 2 * i + n + 1)
                    pe.matmul(ps_b[64 * n:64 * n + 64, 0:D], c["w_out"][:], on[:, n, :], start=True, stop=True).then_inc(y_done, 1)
            if u == 11 and live(t, 6):
                i, s = t - 6, (s0 - 6) % SLOTS
                pe.wait_ge(zT3_copied, 2 * (i + 1))
                for ch in range(2):
                    m = pe.matmul(ps_a[:, 2 * P:2 * P + E], zt3[:, s, ch, :], c["gate"][:, ch, :], start=(ch == 0), stop=(ch == 1))
                m.then_inc(logits_done, 1)
            if u == 11 and live(t, 3):
                weighted(t - 3, (s0 - 3) % SLOTS, 0)
            if u == 8 and live(t, 6):
                i, s = t - 6, (s0 - 6) % SLOTS
                pe.wait_ge(norm3_done, i + 1)
                if live(t, 1):
                    pe.wait_ge(rest_done, 2 * t)
                else:
                    want(pe, logits_copied, i)
                for ch in range(2):
                    m = pe.transpose(ps_a[:, ch * P:(ch + 1) * P], z3[:, s, ch * P:(ch + 1) * P], c["ident"][:])
                m.then_inc(zT3_done, 1)

        def body(t, turn, s0):
            if live(t, 1):
                i, s = t - 1, (s0 - 1) % SLOTS
                pe.wait_ge(norm_done, i + 1)
                want(pe, rest_done, 2 * i)
                want(pe, logits_copied, t - 6)
                for qk in range(2):
                    m = pe.matmul(ps_a[:, qk * D:(qk + 1) * D], c["w_qk"][:, qk, :], z[:, s, :], start=True, stop=True)
                m.then_inc(qk_done, 1)
            for u in range(BOTH):
                if live(t, 2):
                    i, s = t - 2, (s0 - 2) % SLOTS
                    if u == 0:
                        pe.wait_ge(stacked[s], 64 * (tile_turn(turn, s0, 2) + 1))
                    e = BOTH * i + u
                    want(pe, max_done, e - 1)
                    ps, b = ps_s[u % 2], u % BANKS
                    pe.matmul(masked_out(ps, b), c["identb_16"][:], mask_of(b), start=True, stop=False, skip_group_check=True)
                    scores(u // BANKS, b, s, ps, stack[0], stack[1]).then_inc(s_done, 1)
                lag, n, b = by_key(t, u)
                if live(t, lag):
                    i, s = t - lag, (s0 - lag) % SLOTS
                    e = BOTH * i + BANKS * n + b
                    if isinstance(t, int) and t == 3 and n == 0 and b == 0:
                        pe.wait_ge(band_set, SLOTS)
                    if n == 0 and b == 0:
                        pe.wait_ge(shift1, 2 * (i + 1))
                        pe.wait_ge(shift2, i + 1)
                    want(pe, exp_done, e - 1)
                    ps = ps_t[b % 2]
                    for j, (hp, kb, col, tok, w) in enumerate(units(b)):
                        pe.matmul(ps[:, col:col + w], c["pick_16"][:, n * HP + hp, :], shift[:, s, WAY[kb], tok:tok + w],
                                  start=(j == 0), stop=False, skip_group_check=True)
                    scores(n, b, s, ps, stack[1], stack[0]).then_inc(t_done, 1)
                between(t, s0, u)
                k = early_up(t, u)
                if k is not None:
                    if k == 0:
                        pe.wait_ge(max_done, BOTH * TILES)
                    pe.wait_ge(zT3_copied, 2 * GT * (k // HID + 1))
                    ups.up(pe, k, *early_banks(k), 1 if k < EARLY_SINGLE else 2)
        return body

    def scalar_steps(act):
        def copy_o(i, n):
            act.wait_ge(o_done, 2 * i + n + 1)
            want(act, on_done, 2 * i + n - 1)
            nc.scalar.copy(oT[:, n, :], ps_o[:, 0:D]).then_inc(oT_copied, 1)

        def body(t, turn, s0):
            if live(t, 4):
                copy_o(t - 4, 0)
            if live(t, 1):
                i, s = t - 1, (s0 - 1) % SLOTS
                act.wait_ge(qk_done, i + 1)
                want(act, written[s], 2 * TERMS * 16 * tile_turn(turn, s0, 1))
                for qk in range(2):
                    nc.scalar.activation(split[:, s, qk, 0, :], ps_a[:, qk * D:(qk + 1) * D], ACT.Identity,
                                         bias=c["b_qk"][:, qk:qk + 1]).then_inc(part0_done, 1)
            for u in range(BOTH):
                k = early_up(t, u, made=False)
                if k is not None:
                    ups.copy(act, k, early_banks(k)[1])
                if u == 1 and live(t, 3):
                    act.wait_ge(shift_ps, t - 3 + 1)
                    nc.scalar.copy(shift_head[MAXIMA:], ps_c[MAXIMA:, 0:D]).then_inc(shift0, 1)
                lag, n, b = by_key(t, u)
                if live(t, lag):
                    i = t - lag
                    if b == 0:
                        want(act, o_done, 2 * i + n - 1)
                    act.wait_ge(t_done, BOTH * i + BANKS * n + b + 1)
                    nc.scalar.activation(prob[:, n, start[b]:start[b] + cols[b]], ps_t[b % 2][:, 0:cols[b]],
                                         ACT.Exp, scale=float(D2) ** -0.5).then_inc(exp_done, 1)
                if u == 2 and live(t, 3):
                    i, s = t - 3, (s0 - 3) % SLOTS
                    act.wait_ge(shift_r, i + 1)
                    want(act, shift2, i)
                    nc.scalar.copy(shift_tail[THIRD:], shift_rest[THIRD:]).then_inc(shift1, 1)
                    want(act, t_done, BOTH * (i - 2))
                    nc.scalar.copy(shift[MAXIMA:THIRD, s], threefold(shift_rest[MAXIMA:THIRD])).then_inc(shift1, 1)
                if u == 1 and live(t, 1):
                    i, s = t - 1, (s0 - 1) % SLOTS
                    act.wait_ge(rest_done, 2 * (i + 1))
                    nc.scalar.copy(split[:, s, :, 1, :], rest[:, s, :, :]).then_inc(part1_done, 1)
                if u == 3 and live(t, 5):
                    i = t - 5
                    act.wait_ge(y_done, 2 * (i + 1))
                    want(act, gated_done, i)
                    nc.scalar.activation(yr[:], ps_b[:, 0:D], ACT.Relu, bias=c["b_out"][:]).then_inc(yr_done, 1)
                if u == 6 and live(t, 4):
                    copy_o(t - 4, 1)
                if u == 9 and live(t, 6):
                    i, s = t - 6, (s0 - 6) % SLOTS
                    act.wait_ge(zT3_done, i + 1)
                    want(act, logits_done, i - 2)
                    src = ps_a[:, 0:2 * P].rearrange("p (c t) -> p c t", c=2)
                    nc.scalar.copy(zt3[:, s, :, :], src).then_inc(zT3_copied, 1)
                    nc.scalar.copy(zT[:, :, i, :], src).then_inc(zT3_copied, 1)
                if u == 11 and live(t, 6):
                    act.wait_ge(logits_done, t - 6 + 1)
                    nc.scalar.copy(logits[:, t - 6, :], ps_a[:, 2 * P:2 * P + E]).then_inc(logits_copied, 1)
                if k is not None:
                    ups.half_tanh(act, k)
        return body

    def vector_steps(dve):
        def between(t, s0, u):
            if u == 2 and live(t, 6):
                i, s = t - 6, (s0 - 6) % SLOTS
                dve.wait_ge(x2_done, i + 1)
                nc.vector.tensor_copy(stats_ready[:], c["eps"][0:1, :]).then_inc(x2_seen, 1)
                nc.vector.bn_stats(stats3[:, s, :], xres[:, i, :]).then_inc(stats3_done, 1)
            if u == 4 and live(t, 6):
                i, s = t - 6, (s0 - 6) % SLOTS
                dve.wait_ge(stats3_done, i + 1)
                nc.vector.tensor_copy(stats_ready[:], stats3[0:1, s, 0:1]).then_inc(stats3_seen, 1)
                nc.vector.bn_aggr(mv3[:, s, :], stats3[:, s, :]).then_inc(mv3_done, 1)
            if u == 6 and live(t, 6):
                i, s = t - 6, (s0 - 6) % SLOTS
                dve.wait_ge(rstd3_done, i + 1)
                want(dve, zT3_done, i - 2)
                nc.vector.tensor_scalar(z3[:, s, :], xres[:, i, :], mv3[:, s, 0:1], rstd3[:, s, :], ALU.subtract, ALU.mult).then_inc(norm3_done, 1)
            if u == 0 and live(t, 1):
                i, s = t - 1, (s0 - 1) % SLOTS
                dve.wait_ge(part0_done, 2 * (i + 1))
                want(dve, part2_done, i - 2)
                for qk in range(2):
                    nc.vector.scalar_tensor_tensor(out=rest[:, s, qk, :], in0=ps_a[:, qk * D:(qk + 1) * D], scalar=c["b_qk"][:, qk:qk + 1],
                                                   in1=split[:, s, qk, 0, :], op0=ALU.add, op1=ALU.subtract).then_inc(rest_done, 1)
            if u == 1 and live(t, 3):
                i, s = t - 3, (s0 - 3) % SLOTS
                dve.wait_ge(shift0, i + 1)
                want(dve, shift1, 2 * i)
                nc.vector.scalar_tensor_tensor(out=shift_rest[MAXIMA:], in0=shift_head[MAXIMA:], scalar=c["less_first"][MAXIMA:],
                                               in1=ps_c[MAXIMA:, 0:D], op0=ALU.mult, op1=ALU.add).then_inc(shift_r, 1)
            if u == 7 and live(t, 5):
                i = t - 5
                dve.wait_ge(f_done, i + 1)
                nc.vector.scalar_tensor_tensor(out=xres[:, i, :], in0=ps_b[:, 0:D], scalar=c["b_ct"][:], in1=xres[:, i, :],
                                               op0=ALU.add, op1=ALU.add).then_inc(x2_done, 1)
            if u == 3 and live(t, 3):
                i, s = t - 3, (s0 - 3) % SLOTS
                dve.wait_ge(shift1, 2 * i + 1)
                want(dve, t_done, BOTH * (i - 2))
                nc.vector.tensor_tensor(shift[THIRD:, s], threefold(shift_rest[THIRD:]), threefold(shift_tail[THIRD:]), ALU.subtract).then_inc(shift2, 1)
            if u == 5 and live(t, 0):
                nc.vector.bn_stats(stats[:, s0, :], xres[:, t, :]).then_inc(stats_done, 1)
            if u == 6 and live(t, 0):
                dve.wait_ge(stats_done, t + 1)
                nc.vector.tensor_copy(stats_ready[:], stats[0:1, s0, 0:1]).then_inc(stats_seen, 1)
                nc.vector.bn_aggr(mv[:, s0, :], stats[:, s0, :]).then_inc(mv_done, 1)
            if u == 7 and live(t, 0):
                dve.wait_ge(rstd_done, t + 1)
                want(dve, v_done, t - 2)
                nc.vector.tensor_scalar(z[:, s0, :], xres[:, t, :], mv[:, s0, 0:1], rstd[:, s0, :], ALU.subtract, ALU.mult).then_inc(norm_done, 1)
            if u == 9 and live(t, 1):
                i, s = t - 1, (s0 - 1) % SLOTS
                dve.wait_ge(v_done, i + 1)
                want(dve, o_done, 2 * (i - 2))
                for g in range(2):
                    for odd in range(2):
                        r = slice(64 * g, 64 * g + 64)
                        m = nc.vector.tensor_tensor(
                            v_bd[r, s, :, :, odd:KB:2, 16 * g:16 * g + D2].rearrange("p n h k d -> p (n h) k d"),
                            ps_b[64 * odd:64 * odd + 64, 0:2 * P].rearrange("p (k x g d) -> p g x k d", k=2, g=2, d=D2)[:, g],
                            c["b_v"][r, g, :].rearrange("p (x o d) -> p x o d", o=1, d=D2).broadcast_to([64, 8, 2, D2]), ALU.add)
                m.then_inc(v_copied, 1)
            if u >= 8 and live(t, 4):
                i, n, half = t - 4, (u - 8) // 2, (u - 8) % 2
                dve.wait_ge(den_done, i + 1)
                want(dve, on_done, 2 * i + n - 1)
                q = slice(half * P, (half + 1) * P)
                nc.vector.reciprocal(rden[:, n, q], ps_c[:, n * D + half * P:n * D + (half + 1) * P]).then_inc(rden_done, 1)

        def body(t, turn, s0):
            for u in range(BOTH):
                if live(t, 2):
                    i, s, n, b = t - 2, (s0 - 2) % SLOTS, u // BANKS, u % BANKS
                    dve.wait_ge(s_done, BOTH * i + u + 1)
                    if b < HP:
                        dst, src = top[:, s, 1:3, n, b], ps_s[b % 2][:, 0:2 * W_IN].rearrange("p (u w) -> p u w", u=2)
                    else:
                        dst, src = top[:, s, 0 if b == HP else 3, n, :], ps_s[b % 2][:].rearrange("p (u w) -> p u w", u=4)
                    nc.vector.tensor_reduce(dst, src, AX.X, ALU.max).then_inc(max_done, 1)
                between(t, s0, u)
                k = early_up(t, u, made=False)
                if k is not None:
                    ups.product(dve, k, early_banks(k)[0])
            if live(t, 2):
                i, s = t - 2, (s0 - 2) % SLOTS
                dve.wait_ge(max_done, BOTH * (i + 1))
                for r in (0, 16):
                    m = nc.vector.tensor_tensor(
                        top_bd[:, s, :, r:r + 16].rearrange("p k (x g) -> p k x g", g=2),
                        top[:, s, :, :, :].rearrange("p k n (h o) -> p k (n h) o", o=1).broadcast_to([P, KB, 8, 2]),
                        c["minus_half_rows"][:].rearrange("p (a b g) -> p a b g", a=1, b=1).broadcast_to([P, KB, 8, 2]), ALU.mult)
                m.then_inc(top_bd_done, 1)
        return body

    steps = {"sync": sync_steps, "gpsimd": gpsimd_steps, "tensor": tensor_steps, "scalar": scalar_steps, "vector": vector_steps}

    def ahead(engine, eng, t):
        if engine == "gpsimd" and t == PREPARE:
            eng.memset(v_bd[:], 0.0).then_inc(cleared, 1)
            eng.wait_ge(cleared, 1)
            eng.memset(v_bd[0:64, :, :, :, :, D2], 1.0).then_inc(cleared, 1)
            eng.memset(v_bd[64:128, :, :, :, :, 16 + D2], 1.0).then_inc(cleared, 1)
            eng.wait_ge(cleared, 3)
        if engine == "vector" and t == 0:
            eng.wait_ge(cleared, 3)
        if engine == "tensor" and t == 2:
            eng.wait_ge(narrowed, len(NARROW))
        if engine != "sync" and t == 0:
            eng.wait_ge(loaded[3], 16 * len(CONSTS[3]))
        if engine == "scalar" and t == 0:
            for n in NARROW:
                nc.scalar.copy(c[n + "_16"][:], c[n][:]).then_inc(narrowed, 1)
            for s in range(SLOTS):
                nc.scalar.copy(shift[0:64, s, :, :], c["band_rows"][:]).then_inc(band_set, 1)
        if 0 <= t < AHEAD_STEPS:
            steps[engine](eng)(t, t // SLOTS, t % SLOTS)

    before(ps_a, ps_b, by_query, ahead)

    ups = Ups(nc, ctx, zT, c)

    with ExitStack() as late:
        def late_sb(name, shape, dt=F32):
            return late.enter_context(nc.sbuf_tensor(name, shape, dt))

        def late_bank(name):
            return late.enter_context(nc.psum_tensor(name, [P, 512], F32))

        shift_head = late_sb("shift_head", [P, D], BF16)
        shift_rest = late_sb("shift_rest", [P, D])
        shift_tail = late_sb("shift_tail", [P, D], BF16)
        prob = late_sb("b_prob", [P, 2, 5 * 512])
        oT = late_sb("oT", [P, 2, D])
        rden = late_sb("b_rden", [P, 2, D])
        on = late_sb("on", [P, 2, D])
        enc = late_sb("enc", [P, SLOTS, D])
        yr = late_sb("yr", [P, D])
        gated = late_sb("gated", [P, D])
        stats3 = late_sb("g_stats", [P, SLOTS, 6])
        mv3 = late_sb("g_mv", [P, SLOTS, 2])
        vare3 = late_sb("g_vare", [P, SLOTS, 1])
        rstd3 = late_sb("g_rstd", [P, SLOTS, 1])
        z3 = late_sb("g_z", [P, SLOTS, D])
        zt3 = late_sb("g_zt", [P, SLOTS, 2, P])
        ps_t = [late_bank(f"b_ps_t{i}") for i in range(2)]
        ps_c = late_bank("b_ps_c")
        ps_o = late_bank("b_ps_o")

        with nc.Block() as block:
            @block.sync
            def _(sp):
                run_steps(sp, sync_steps(sp), LAGS, head=3, first=AHEAD_STEPS)

            @block.gpsimd
            def _(pool):
                run_steps(pool, gpsimd_steps(pool), LAGS, head=3, first=AHEAD_STEPS)

            @block.tensor
            def _(pe):
                pe.wait_ge(narrowed, len(NARROW))
                run_steps(pe, tensor_steps(pe), LAGS, head=3, first=AHEAD_STEPS)

            @block.scalar
            def _(act):
                run_steps(act, scalar_steps(act), LAGS, head=3, first=AHEAD_STEPS)

            @block.vector
            def _(dve):
                run_steps(dve, vector_steps(dve), LAGS, head=3, first=AHEAD_STEPS)

    after(ups, ps_s, [ps_a, ps_b])


E = 12
F = 32
CAP = -(-NB * SEQ * 5 // (E * 4))
HID = E * F // P
GROUP = 512
GROUPS = NB * SEQ // GROUP
GT = GROUP // P
PICKS = 2
EARLY_UPS = (((TILES + 2, 4), (TILES + 2, 5)), ((TILES + 2, 10), (TILES + 2, 11)), ((TILES + 3, 7), (TILES + 3, 11)),
             ((TILES + 4, 2), (TILES + 4, 4)), ((TILES + 4, 7), (TILES + 5, 7)), ((TILES + 5, 8), (TILES + 5, 10)))
EARLY_SINGLE = 3
EARLY = len(EARLY_UPS)


class Ups:

    def __init__(self, nc, ctx, zT, c):
        self.nc, self.zT, self.c = nc, zT, c
        self.up3 = ctx.enter_context(nc.sbuf_tensor("up3", [P, 2, GROUP], F32))
        self.prod = ctx.enter_context(nc.sbuf_tensor("prod", [P, 2, GROUP], F32))
        self.tanh = ctx.enter_context(nc.sbuf_tensor("tanh", [P, 2, GROUP], F32))
        self.hid = ctx.enter_context(nc.sbuf_tensor("hid", [P, HID, NB * SEQ], F32))
        self.up_done = ctx.enter_context(nc.semaphore("up_done"))
        self.up3_copied = ctx.enter_context(nc.semaphore("up3_copied"))
        self.prod_done = ctx.enter_context(nc.semaphore("prod_done"))
        self.tanh_done = ctx.enter_context(nc.semaphore("tanh_done"))
        self.by_tanh = ctx.enter_context(nc.semaphore("by_tanh"))
        self.silu_done = ctx.enter_context(nc.semaphore("silu_done"))

    def up(self, pe, k, ps_1, ps_3, banks):
        z = [self.zT[:, ch, GT * (k // HID):GT * (k // HID + 1), :].rearrange("p t c -> p (t c)") for ch in range(2)]
        cols = slice((k % HID) * P, (k % HID + 1) * P)
        want(pe, self.prod_done, k + 1 - banks)
        for ps, weights in ((ps_1, self.c["w1"]), (ps_3, self.c["w3"])):
            for ch in range(2):
                m = pe.matmul(ps[:], weights[:, ch, cols], z[ch], start=(ch == 0), stop=(ch == 1))
        m.then_inc(self.up_done, 1)

    def copy(self, act, k, ps_3):
        act.wait_ge(self.up_done, k + 1)
        want(act, self.prod_done, k - 1)
        self.nc.scalar.copy(self.up3[:, k % 2, :], ps_3[:]).then_inc(self.up3_copied, 1)

    def product(self, dve, k, ps_1):
        dve.wait_ge(self.up3_copied, k + 1)
        want(dve, self.silu_done, k - 1)
        self.nc.vector.tensor_tensor(self.prod[:, k % 2, :], ps_1[:], self.up3[:, k % 2, :], ALU.mult).then_inc(self.prod_done, 1)

    def half_tanh(self, act, k):
        act.wait_ge(self.prod_done, k + 1)
        want(act, self.silu_done, k - 1)
        self.nc.scalar.activation(self.tanh[:, k % 2, :], self.prod[:, k % 2, :], ACT.Tanh, scale=0.5).then_inc(self.tanh_done, 1)

    def silu(self, pool, k):
        pool.wait_ge(self.tanh_done, k + 1)
        pool.tensor_tensor(self.tanh[:, k % 2, :], self.tanh[:, k % 2, :], self.prod[:, k % 2, :], ALU.mult).then_inc(self.by_tanh, 1)
        pool.wait_ge(self.by_tanh, k + 1)
        pool.tensor_tensor(self.hid[:, k % HID, GROUP * (k // HID):GROUP * (k // HID + 1)], self.tanh[:, k % 2, :], self.prod[:, k % 2, :],
                           ALU.add).then_inc(self.silu_done, 1)


def feed_forward(nc, ctx, io, xres, logits, c, ups, ps_up, ps_w):

    def sb(name, shape, dt=F32):
        return ctx.enter_context(nc.sbuf_tensor(name, shape, dt))

    def sem(name):
        return ctx.enter_context(nc.semaphore(name))

    def wide(x, n=E):
        return x.rearrange("p (a o) -> p a o", o=1).broadcast_to([P, x.shape[1], n])

    less = sb("r_less", [P, TILES, E])
    prob = sb("r_prob", [P, TILES, E])
    key = sb("r_key", [P, TILES, E])
    eq = sb("r_eq", [P, TILES, E])
    sel = sb("r_sel", [P, PICKS, TILES, E], BF16)
    best = sb("r_best", [P, PICKS, TILES])
    low = sb("r_low", [P, 4, TILES])
    total = sb("r_total_by_expert", [P, E, PICKS * TILES])
    run = sb("r_run", [P, E, PICKS * TILES])
    pos = sb("r_pos", [P, PICKS * TILES, E])
    w = sb("r_w", [P, TILES, E])
    w_parts = sb("w_parts", [P, TILES, 3, E], BF16)
    wT = sb("wT", [3 * E, NB * SEQ], BF16)
    hid = ups.hid
    out = sb("x_out", [P, 4, 2, D])

    step_done = sem("route_step")
    less_done = sem("less_done")
    exp_done = sem("route_exp")
    sel_done = sem("sel_done")
    counted = sem("counted")
    w_done = sem("w_done")
    w_turned = sem("w_turned")
    wT_done = sem("wT_done")
    spread = sem("weights_spread")
    hid_done = sem("hid_done")
    down_done = sem("down_done")
    out_done = sem("out_done")
    stored = [sem(f"stored{i}") for i in range(4)]
    ps_up2, ps_d = ([ctx.enter_context(nc.psum_tensor(f"e_ps{n}{i}", [P, 512], F32)) for i in range(2)] for n in "ud")
    ps_1, ps_3 = ([ps_up[i], ps_up2[i]] for i in range(2))
    ps_x, ps_y = ps_w + ps_1, ps_d + ps_3
    out_tiles = io["out"].rearrange("(n b) s d -> (b s) n d", b=2)

    with nc.Block() as block:
        @block.sync
        def _(sp):
            for pair in range(TILES // 2):
                slot = pair % len(stored)
                sp.wait_ge(out_done, 2 * pair + 2)
                sp.dma_start(out_tiles[:, 2 * pair:2 * pair + 2, :], out[:, slot, :, :]).then_inc(stored[slot], 16)
            for done in stored:
                sp.wait_ge(done, 16 * (TILES // 2 // len(stored)))

        @block.tensor
        def _(pe):
            def up(k):
                ups.up(pe, k, ps_1[k % 2], ps_3[k % 2], 2)

            for k in range(EARLY, EARLY + 3):
                up(k)
            pe.wait_ge(sel_done, 1)
            s = sel[:].rearrange("p k t e -> p (k t e)")
            n = PICKS * TILES * E
            pe.matmul(ps_d[0][:, 0:n], c["upto_16"][:], s, start=True, stop=True).then_inc(counted, 1)
            pe.matmul(ps_d[1][:, 0:n], c["ones_16"][:], s, start=True, stop=True).then_inc(counted, 1)
            up(EARLY + 3)
            up(EARLY + 4)
            pe.wait_ge(w_done, 1)
            for t in range(TILES):
                m = pe.matmul((ps_w + ps_d)[t // GT][0:3 * E, (t % GT) * P:(t % GT + 1) * P],
                              w_parts[:, t, :, :].rearrange("p a e -> p (a e)"), c["identb_16"][:], start=True, stop=True)
            m.then_inc(w_turned, 1)
            up(EARLY + 5)
            def spread_weights(k):
                want(pe, hid_done, k + 1 - len(ps_x))
                pe.matmul(ps_x[k % len(ps_x)][:], c["expand_16"][:, (k % HID) * P:(k % HID + 1) * P],
                          wT[:, GROUP * (k // HID):GROUP * (k // HID + 1)], start=True, stop=True).then_inc(spread, 1)

            def body(j):
                if j + 1 < GROUPS:
                    for h in range(HID):
                        spread_weights(HID * (j + 1) + h)
                pe.wait_ge(hid_done, HID * (j + 1))
                for t in range(GT):
                    want(pe, out_done, GT * j + t + 1 - len(ps_y))
                    for h in range(HID):
                        m = pe.matmul(ps_y[t % len(ps_y)][:, 0:D], hid[:, h, GROUP * j + t * P:GROUP * j + (t + 1) * P], c["w2"][:, h, :],
                                      start=(h == 0), stop=(h == HID - 1))
                    m.then_inc(down_done, 1)
            pe.wait_ge(wT_done, GROUPS)
            pe.wait_ge(ups.prod_done, HID * GROUPS)
            for h in range(HID):
                spread_weights(h)
            for j in range(GROUPS):
                body(j)

        @block.scalar
        def _(act):
            act.wait_ge(less_done, 1)
            nc.scalar.activation(prob[:], less[:], ACT.Exp).then_inc(exp_done, 1)
            def silu(k):
                ups.copy(act, k, ps_3[k % 2])
                ups.half_tanh(act, k)

            for k in range(EARLY, EARLY + 5):
                silu(k)
            act.wait_ge(w_turned, 1)
            for g in range(GROUPS):
                nc.scalar.copy(wT[:, g * GROUP:(g + 1) * GROUP], (ps_w + ps_d)[g][0:3 * E, :]).then_inc(wT_done, 1)
            silu(EARLY + 5)

        @block.gpsimd
        def _(pool):
            for k in range(EARLY, HID * GROUPS):
                ups.silu(pool, k)

        @block.vector
        def _(dve):
            v = nc.vector
            steps = [0]

            def then(ins):
                steps[0] += 1
                ins.then_inc(step_done, 1)
                dve.wait_ge(step_done, steps[0])

            def product(k):
                ups.product(dve, k, ps_1[k % 2])

            then(v.tensor_reduce(low[:, 0, :], logits[:], AX.X, ALU.max))
            v.tensor_tensor(less[:], logits[:], wide(low[:, 0, :]), ALU.subtract).then_inc(less_done, 1)
            dve.wait_ge(exp_done, 1)
            then(v.tensor_reduce(low[:, 1, :], prob[:], AX.X, ALU.add))
            then(v.reciprocal(low[:, 2, :], low[:, 1, :]))
            then(v.tensor_tensor(prob[:], prob[:], wide(low[:, 2, :]), ALU.mult))
            for k in range(PICKS):
                then(v.tensor_reduce(best[:, k, :], prob[:], AX.X, ALU.max))
                then(v.tensor_tensor(eq[:], prob[:], wide(best[:, k, :]), ALU.is_equal))
                then(v.tensor_tensor(key[:], eq[:], c["order"][:].rearrange("p (o e) -> p o e", o=1).broadcast_to([P, TILES, E]), ALU.mult))
                then(v.tensor_reduce(low[:, 3, :], key[:], AX.X, ALU.max))
                then(v.tensor_tensor(sel[:, k, :, :], key[:], wide(low[:, 3, :]), ALU.is_equal))
                if k == 0:
                    then(v.scalar_tensor_tensor(out=prob[:], in0=sel[:, 0, :, :], scalar=-2.0, in1=prob[:], op0=ALU.mult, op1=ALU.add))
                    product(EARLY)
            v.memset(low[:, 2, :], 0.0).then_inc(sel_done, 1)
            product(EARLY + 1)
            then(v.tensor_tensor(low[:, 0, :], best[:, 0, :], best[:, 1, :], ALU.add))
            then(v.reciprocal(low[:, 1, :], low[:, 0, :]))
            then(v.scalar_tensor_tensor(out=best[:], in0=best[:], scalar=0.5,
                                        in1=low[:, 1:2, :].broadcast_to([P, PICKS, TILES]), op0=ALU.mult, op1=ALU.mult))
            product(EARLY + 2)
            dve.wait_ge(counted, 2)
            by_tile = ps_d[1][:, 0:PICKS * TILES * E].rearrange("p (j e) -> p e j", e=E)
            then(v.tensor_tensor(total[:], by_tile, c["zero"][:].rearrange("p (a b) -> p a b", a=E), ALU.add))
            then(v.tensor_tensor_scan(run[:].rearrange("p e j -> p (e j)"), c["carry"][:], total[:].rearrange("p e j -> p (e j)"), 0.0, ALU.mult, ALU.add))
            then(v.tensor_tensor(run[:], run[:], total[:], ALU.subtract))
            then(v.tensor_tensor(pos[:], ps_d[0][:, 0:PICKS * TILES * E].rearrange("p (j e) -> p j e", e=E), run[:].rearrange("p e j -> p j e"), ALU.add))
            selj = sel[:].rearrange("p k t e -> p (k t) e")
            then(v.scalar_tensor_tensor(out=pos[:], in0=pos[:], scalar=float(CAP), in1=selj, op0=ALU.is_le, op1=ALU.mult))
            then(v.tensor_tensor(pos[:], pos[:], wide(best[:].rearrange("p k t -> p (k t)")), ALU.mult))
            then(v.tensor_tensor(w[:], pos[:, 0:TILES, :], pos[:, TILES:, :], ALU.add))
            product(EARLY + 3)
            then(v.tensor_copy(w_parts[:, :, 0, :], w[:]))
            then(v.tensor_tensor(w[:], w[:], w_parts[:, :, 0, :], ALU.subtract))
            then(v.tensor_copy(w_parts[:, :, 1, :], w[:]))
            v.tensor_tensor(w_parts[:, :, 2, :], w[:], w_parts[:, :, 1, :], ALU.subtract).then_inc(w_done, 1)
            product(EARLY + 4)
            product(EARLY + 5)

            def weigh(j):
                dve.wait_ge(ups.silu_done, HID * (j + 1))
                for h in range(HID):
                    dve.wait_ge(spread, HID * j + h + 1)
                    x = hid[:, h, GROUP * j:GROUP * (j + 1)]
                    v.tensor_tensor(x, x, ps_x[(HID * j + h) % len(ps_x)][:], ALU.mult).then_inc(hid_done, 1)

            weigh(0)
            for j in range(GROUPS):
                if j + 1 < GROUPS:
                    weigh(j + 1)
                for t in range(GT):
                    pair, own = GT // 2 * j + t // 2, (GT // 2 * j + t // 2) // len(stored)
                    dve.wait_ge(down_done, GT * j + t + 1)
                    want(dve, stored[pair % len(stored)], 16 * own)
                    v.tensor_tensor(out[:, pair % len(stored), t % 2, :], ps_y[t % len(ps_y)][:, 0:D], xres[:, GT * j + t, :],
                                    ALU.add).then_inc(out_done, 1)


CONSTS = (("minus_half", "eps", "ident"),
          ("wqk", "qkb", "sin", "cos"),
          ("wv", "vb", "ob", "hmask", "wo"),
          ("identb", "w_qk", "w_v", "b_qk", "b_v", "w_out", "b_out", "w_ct", "b_ct", "band_in", "band_0", "band_3", "band_rows", "pick", "less_first",
           "den_rows", "ident2", "minus_half_rows", "gate", "order", "carry", "zero", "upto", "ones", "expand", "w1", "w3", "w2"))
OWN_CONSTS = (1, 2)
NARROW = ("identb", "band_in", "band_0", "band_3", "pick", "upto", "ones", "expand")


def program(nc, io):
    with ExitStack() as ctx:
        def sb(name, shape, dt=F32):
            return ctx.enter_context(nc.sbuf_tensor(name, shape, dt))

        c = {n: sb("c_" + n, list(io[n].shape), io[n].dtype) for i, group in enumerate(CONSTS) for n in group if i not in OWN_CONSTS}
        c.update({n + "_16": sb(n + "_16", list(io[n].shape), BF16) for n in NARROW})
        loaded = [ctx.enter_context(nc.semaphore(f"consts{i}")) for i in range(len(CONSTS))]
        xres = sb("xres", [P, TILES, D])
        zT = sb("zT_all", [P, 2, TILES, P])
        logits = sb("logits", [P, TILES, E])

        def first(*lent):
            with ExitStack() as stage:
                self_attention(nc, stage, io, xres, c, loaded, *lent)

        def last(*lent):
            with ExitStack() as stage:
                feed_forward(nc, stage, io, xres, logits, c, *lent)

        with ExitStack() as stage:
            ctx_attention(nc, stage, io, xres, zT, logits, c, loaded, first, last)


def layout(x):
    f = np.float32

    def cut(w):
        return np.ascontiguousarray(w.reshape(2, P, -1).transpose(1, 0, 2))

    pos = np.arange(SEQ, dtype=f)
    inv = (1.0 / 10000.0 ** (np.arange(0, D1, 2, dtype=f) / f(D1))).astype(f)
    ang = np.tile(pos[:, None] * inv[None, :], (2, 2)).astype(f)
    sin = np.sin(ang)
    sin[:, :D1 // 2] *= -1
    def pair(w):
        out = np.zeros((P, P), f)
        out[:64, :64] = out[64:, 64:] = w
        return out

    w_in, b_in = x["L0_xattn_w_in"], x["L0_xattn_b_in"]
    pq, ph = np.arange(P) % 64, np.arange(P) // 64
    col = np.arange(64)
    prev = np.where(col[None] >= pq[:, None], 0, NEG).astype(f)
    nxt = np.where(col[None] <= pq[:, None], 0, NEG).astype(f)
    w_out = np.zeros((P, 64), f)
    den = np.zeros((P, P), f)
    for h in range(H2):
        w_out[16 * h:16 * h + D2] = x["L0_xattn_w_out"].T[D2 * h:D2 * h + D2]
        den[16 * h + D2, 16 * h:16 * h + 16] = 1
    pick = np.zeros((P, 2 * HP, P), f)
    pick[:64] = np.eye(64, dtype=f)[:, pq][:, None]
    for j in range(3):
        for r in range(16):
            pick[MAXIMA + 16 * j + r, r // 2] = ph == r % 2
    band_rows = np.zeros((64, 3, KB, 64), f)
    for kb in range(KB):
        if kb > 0:
            band_rows[:, WAY[kb], kb - 1] = prev[:64]
        if kb < KB - 1:
            band_rows[:, WAY[kb], kb + 1] = nxt[:64]
    b_v = np.tile(b_in[128:].reshape(HP, 2, D2), (2, 1, 1)).transpose(1, 0, 2).reshape(2, 64)
    rows = lambda v: np.ascontiguousarray(np.broadcast_to(v, (P, v.shape[-1])))
    return {
        "x": x["x"],
        "minus_half": np.full((P, 1), -0.5, f),
        "eps": np.full((P, 1), EPS, f),
        "ident": np.eye(P, dtype=f),
        "wqk": cut(np.concatenate([x["L0_attn_q_w"].T, x["L0_attn_k_w"].T], 1)),
        "wv": cut(x["L0_attn_v_w"].T),
        "wo": cut(x["L0_attn_out_w"].T),
        "qkb": rows(np.concatenate([x["L0_attn_q_b"], x["L0_attn_k_b"]])),
        "vb": rows(x["L0_attn_v_b"]),
        "ob": rows(x["L0_attn_out_b"]),
        "cos": np.cos(ang).astype(f),
        "sin": sin.astype(f),
        "ctx": x["ctx_2048"],
        "identb": np.eye(P, dtype=f),
        "w_qk": np.stack([pair(w_in[0:64].T), pair(w_in[64:128].T)], 1),
        "w_v": pair(w_in[128:].T),
        "b_qk": np.stack([np.tile(b_in[0:64], 2), np.tile(b_in[64:128], 2)], 1),
        "b_v": np.ascontiguousarray(np.broadcast_to(b_v, (P, 2, 64))),
        "w_out": w_out,
        "b_out": np.tile(x["L0_xattn_b_out"], 2)[:, None],
        "w_ct": pair(x["L0_xattn_w_ct"]),
        "b_ct": np.tile(x["L0_xattn_b_ct"], 2)[:, None],
        "band_in": np.concatenate([prev, nxt, prev, nxt], 1),
        "band_0": np.tile(nxt, (1, 4)),
        "band_3": np.tile(prev, (1, 4)),
        "pick": pick,
        "band_rows": band_rows.reshape(64, 3, D),
        "less_first": -(np.arange(P)[:, None] >= MAXIMA + 16).astype(f),
        "den_rows": den,
        "ident2": (pq[:, None] == col[None]).astype(f),
        "minus_half_rows": -(ph[:, None] == np.arange(2)[None]).astype(f),
        "gate": cut(x["L0_ffn_gate_w"].T),
        "order": rows(np.arange(E, 0, -1).astype(f)),
        "carry": rows((np.arange(E * PICKS * TILES) % (PICKS * TILES) > 0).astype(f)),
        "zero": np.zeros((P, E * PICKS * TILES), f),
        "upto": np.triu(np.ones((P, P), f)),
        "ones": np.ones((P, P), f),
        "expand": (np.tile(np.arange(E), 3)[:, None] == np.arange(E * F)[None] // F).astype(f),
        "w1": cut(x["L0_ffn_w1"].reshape(E * F, D).T),
        "w3": cut(x["L0_ffn_w3"].reshape(E * F, D).T),
        "w2": np.ascontiguousarray(x["L0_ffn_w2"].transpose(0, 2, 1).reshape(HID, P, D).transpose(1, 0, 2)),
        "hmask": (np.arange(P)[:, None] // D1 == np.arange(HC)[None]).astype(f),
    }


def kernel(**inputs):
    import concourse.bacc as bacc
    from concourse.bass_utils import run_bass_kernel_spmd

    nc = bacc.Bacc("TRN2", target_bir_lowering=False, num_devices=1)
    arrays = layout({k: np.asarray(v) for k, v in inputs.items()})
    io = {k: nc.dram_tensor("in_" + k, a.shape, mybir.dt.from_np(a.dtype), kind="ExternalInput").ap() for k, a in arrays.items()}
    io["out"] = nc.dram_tensor("out", (NB, SEQ, D), F32, kind="ExternalOutput").ap()
    program(nc, io)
    got = run_bass_kernel_spmd(nc, [{"in_" + k: a for k, a in arrays.items()}], core_ids=[0])
    return got.results[0]["out"]
```
